# Optimizing a Trainium2 kernel written in Bass

```python
import numpy as np
import jax
import jax.numpy as jnp

def _softmax(x, axis=-1):
    return jax.nn.softmax(x, axis=axis)

def _gelu(x):
    return jax.nn.gelu(x, approximate=True)

def _silu(x):
    return jax.nn.silu(x)

def _sigmoid(x):
    return jax.nn.sigmoid(x)

def _layernorm(x, axis=-1, eps=1e-05):
    m = jnp.mean(x, axis=axis, keepdims=True)
    v = jnp.var(x, axis=axis, keepdims=True)
    return (x - m) / jnp.sqrt(v + eps)

def _scatter_add(tgt, idx, src, axis=0):
    return tgt.at[idx].add(src)

def _segment_sum(src, seg, n):
    return jax.ops.segment_sum(src, seg, n)
kernel_name = 'mk_adaln_d1_jaxref_r4_0935bf'

def setup_inputs(seed: int=0):
    np.random.seed(seed)
    _w = jnp.asarray

    def _L0_attn_setup():
        import jax, jax.numpy as jnp
        import numpy as np
        D_MODEL = 256
        N_HEADS = 16
        HEAD_DIM = D_MODEL // N_HEADS
        WINDOW = 128
        LOCAL_BLOCK = 64
        LATENT_TOKENS = 64
        LATENT_D = 64
        LATENT_HEADS = 4
        LATENT_HD = LATENT_D // LATENT_HEADS
        NEG = -1000000000.0

        def _local_attention(q, k, v):
            B, H, S, hd = q.shape
            bs = min(S, max(WINDOW, LOCAL_BLOCK))
            nb = S // bs
            w = WINDOW
            L = bs + w - 1
            k_pad = jnp.pad(k, ((0, 0), (0, 0), (w - 1, 0), (0, 0)))
            v_pad = jnp.pad(v, ((0, 0), (0, 0), (w - 1, 0), (0, 0)))
            starts = jnp.arange(nb) * bs
            idx = starts[:, None] + jnp.arange(L)[None, :]
            kb = k_pad[:, :, idx]
            vb = v_pad[:, :, idx]
            qb = q.reshape(B, H, nb, bs, hd)
            q_pos = starts[:, None] + jnp.arange(bs)[None, :]
            k_gpos = starts[:, None] + jnp.arange(L)[None, :] - (w - 1)
            dist = q_pos[:, :, None] - k_gpos[:, None, :]
            allowed = (dist > 0) & (dist <= w) & (k_gpos[:, None, :] >= 0)
            scale = 1.0 / np.sqrt(hd)
            scores = jnp.einsum('bhnqd,bhnkd->bhnqk', qb, kb) * scale
            scores = jnp.where(allowed, scores, NEG)
            attn = jax.nn.softmax(scores, axis=-1)
            attn = jnp.where(allowed.any(-1)[None, None, :, :, None], attn, 0.0)
            out = jnp.einsum('bhnqk,bhnkd->bhnqd', attn, vb)
            return out.reshape(B, H, S, hd)
        key = jax.random.key(seed)
        ks = jax.random.split(key, 14)
        B, S = (2, 1024)
        s = 0.02
        f32 = jnp.float32
        return {'x': jax.random.normal(ks[0], (B, S, D_MODEL), f32), 'qkv_w': jax.random.normal(ks[1], (D_MODEL, 3 * D_MODEL), f32) * s, 'qkv_b': jnp.zeros((3 * D_MODEL,), f32), 'rq_w': jax.random.normal(ks[2], (D_MODEL, LATENT_D), f32) * s, 'rq_b': jnp.zeros((LATENT_D,), f32), 'rkv_w': jax.random.normal(ks[3], (D_MODEL, 2 * LATENT_D), f32) * s, 'rkv_b': jnp.zeros((2 * LATENT_D,), f32), 'rout_w': jax.random.normal(ks[4], (LATENT_D, D_MODEL), f32) * s, 'rout_b': jnp.zeros((D_MODEL,), f32), 'out_w': jax.random.normal(ks[5], (D_MODEL, D_MODEL), f32) * s, 'out_b': jnp.zeros((D_MODEL,), f32), 'gl_w': jax.random.normal(ks[6], (HEAD_DIM, 1), f32) * s, 'gr_w': jax.random.normal(ks[7], (HEAD_DIM, 1), f32) * s}
    _L0_attn_in = _L0_attn_setup()

    def _L0_ffn_setup():
        import jax, jax.numpy as jnp
        import numpy as np
        S, B, D, H, DH = (1024, 8, 256, 16, 64)

        def _forward(x, Wg, Wq, bq, Wkv, bkv, Wo, bo, ln_g, ln_b):
            s_len, bsz, d_model = x.shape
            n_head, _, d_head = Wq.shape
            cap = s_len // n_head
            scale = 1.0 / d_head ** 0.5
            h = jnp.transpose(x, (1, 0, 2))
            t = h
            probs = jax.nn.softmax(h @ Wg, axis=-1)
            scores = jnp.transpose(probs, (0, 2, 1))
            _, idx = jax.lax.top_k(scores, cap)
            idx = jnp.sort(idx, axis=-1)
            hg = jnp.take_along_axis(h[:, None, :, :], idx[..., None], axis=2)
            hg = jnp.transpose(hg, (1, 0, 2, 3))
            q = jnp.einsum('hbcd,hde->hbce', hg, Wq) + bq[:, None, None, :]
            kv = jnp.einsum('hbcd,hde->hbce', hg, Wkv) + bkv[:, None, None, :]
            k, v = jnp.split(kv, 2, axis=-1)
            att = jnp.einsum('hbid,hbjd->hbij', q, k) * scale
            p = jax.nn.softmax(att, axis=1)
            av = jnp.einsum('hbij,hbjd->hbid', p, v)
            ao = jnp.einsum('hbid,hde->hbie', av, Wo) + bo
            tok = jnp.transpose(idx, (1, 0, 2))
            b_ids = jnp.arange(bsz)[None, :, None]
            outs = jnp.zeros_like(t).at[b_ids, tok].add(ao)
            y = t + outs
            mu = jnp.mean(y, axis=-1, keepdims=True)
            var = jnp.var(y, axis=-1, keepdims=True)
            yn = (y - mu) * jax.lax.rsqrt(var + 1e-05) * ln_g + ln_b
            return jnp.transpose(yn, (1, 0, 2))
        key = jax.random.key(seed)
        ks = jax.random.split(key, 6)
        s = 0.02
        return {'x': jax.random.normal(ks[0], (S, B, D), jnp.float32), 'attn_mask': jnp.zeros((S, S), jnp.bool_), 'Wg': jax.random.normal(ks[1], (D, H), jnp.float32) * s, 'Wq': jax.random.normal(ks[2], (H, D, DH), jnp.float32) * s, 'bq': jnp.zeros((H, DH), jnp.float32), 'Wkv': jax.random.normal(ks[3], (H, D, 2 * DH), jnp.float32) * s, 'bkv': jnp.zeros((H, 2 * DH), jnp.float32), 'Wo': jax.random.normal(ks[4], (H, DH, D), jnp.float32) * s, 'bo': jnp.zeros((D,), jnp.float32), 'ln_g': jnp.ones((D,), jnp.float32), 'ln_b': jnp.zeros((D,), jnp.float32)}
    _L0_ffn_in = _L0_ffn_setup()
    _L0_c = _w((lambda *s: np.random.randn(*s).astype(np.float32) * 0.05)(4, 256))
    _L0_wmod = _w((lambda *s: np.random.randn(*s).astype(np.float32) * 0.05)(256, 6 * 256) * 256 ** (-0.5))
    _d = {'L0_attn_x': _L0_attn_in['x'], 'L0_attn_qkv_w': _L0_attn_in['qkv_w'], 'L0_attn_qkv_b': _L0_attn_in['qkv_b'], 'L0_attn_rq_w': _L0_attn_in['rq_w'], 'L0_attn_rq_b': _L0_attn_in['rq_b'], 'L0_attn_rkv_w': _L0_attn_in['rkv_w'], 'L0_attn_rkv_b': _L0_attn_in['rkv_b'], 'L0_attn_rout_w': _L0_attn_in['rout_w'], 'L0_attn_rout_b': _L0_attn_in['rout_b'], 'L0_attn_out_w': _L0_attn_in['out_w'], 'L0_attn_out_b': _L0_attn_in['out_b'], 'L0_attn_gl_w': _L0_attn_in['gl_w'], 'L0_attn_gr_w': _L0_attn_in['gr_w'], 'L0_ffn_attn_mask': _L0_ffn_in['attn_mask'], 'L0_ffn_Wg': _L0_ffn_in['Wg'], 'L0_ffn_Wq': _L0_ffn_in['Wq'], 'L0_ffn_bq': _L0_ffn_in['bq'], 'L0_ffn_Wkv': _L0_ffn_in['Wkv'], 'L0_ffn_bkv': _L0_ffn_in['bkv'], 'L0_ffn_Wo': _L0_ffn_in['Wo'], 'L0_ffn_bo': _L0_ffn_in['bo'], 'L0_ffn_ln_g': _L0_ffn_in['ln_g'], 'L0_ffn_ln_b': _L0_ffn_in['ln_b'], 'L0_c': _L0_c, 'L0_wmod': _L0_wmod}
    _x0 = _d['L0_attn_x']
    _d['L0_attn_x'] = jax.random.normal(jax.random.fold_in(jax.random.key(seed), 1), (4, 1024, 256), dtype=_x0.dtype)
    del _x0
    return _d

def reference(L0_attn_x, L0_attn_qkv_w, L0_attn_qkv_b, L0_attn_rq_w, L0_attn_rq_b, L0_attn_rkv_w, L0_attn_rkv_b, L0_attn_rout_w, L0_attn_rout_b, L0_attn_out_w, L0_attn_out_b, L0_attn_gl_w, L0_attn_gr_w, L0_ffn_attn_mask, L0_ffn_Wg, L0_ffn_Wq, L0_ffn_bq, L0_ffn_Wkv, L0_ffn_bkv, L0_ffn_Wo, L0_ffn_bo, L0_ffn_ln_g, L0_ffn_ln_b, L0_c, L0_wmod):

    def _L0_attn_ref(x, qkv_w, qkv_b, rq_w, rq_b, rkv_w, rkv_b, rout_w, rout_b, out_w, out_b, gl_w, gr_w):
        import jax, jax.numpy as jnp
        import numpy as np
        D_MODEL = 256
        N_HEADS = 16
        HEAD_DIM = D_MODEL // N_HEADS
        WINDOW = 128
        LOCAL_BLOCK = 64
        LATENT_TOKENS = 64
        LATENT_D = 64
        LATENT_HEADS = 4
        LATENT_HD = LATENT_D // LATENT_HEADS
        NEG = -1000000000.0

        def _local_attention(q, k, v):
            B, H, S, hd = q.shape
            bs = min(S, max(WINDOW, LOCAL_BLOCK))
            nb = S // bs
            w = WINDOW
            L = bs + w - 1
            k_pad = jnp.pad(k, ((0, 0), (0, 0), (w - 1, 0), (0, 0)))
            v_pad = jnp.pad(v, ((0, 0), (0, 0), (w - 1, 0), (0, 0)))
            starts = jnp.arange(nb) * bs
            idx = starts[:, None] + jnp.arange(L)[None, :]
            kb = k_pad[:, :, idx]
            vb = v_pad[:, :, idx]
            qb = q.reshape(B, H, nb, bs, hd)
            q_pos = starts[:, None] + jnp.arange(bs)[None, :]
            k_gpos = starts[:, None] + jnp.arange(L)[None, :] - (w - 1)
            dist = q_pos[:, :, None] - k_gpos[:, None, :]
            allowed = (dist > 0) & (dist <= w) & (k_gpos[:, None, :] >= 0)
            scale = 1.0 / np.sqrt(hd)
            scores = jnp.einsum('bhnqd,bhnkd->bhnqk', qb, kb) * scale
            scores = jnp.where(allowed, scores, NEG)
            attn = jax.nn.softmax(scores, axis=-1)
            attn = jnp.where(allowed.any(-1)[None, None, :, :, None], attn, 0.0)
            out = jnp.einsum('bhnqk,bhnkd->bhnqd', attn, vb)
            return out.reshape(B, H, S, hd)
        B, S, D = x.shape
        qkv = x @ qkv_w + qkv_b
        q, k, v = jnp.split(qkv, 3, axis=-1)

        def heads(t):
            return t.reshape(B, S, N_HEADS, HEAD_DIM).transpose(0, 2, 1, 3)
        local = _local_attention(heads(q), heads(k), heads(v))
        chunk = -(-S // min(LATENT_TOKENS, S))
        nlat = S // chunk
        pooled = x.reshape(B, nlat, chunk, D).mean(axis=2)
        chunk_ids = jnp.arange(S) // chunk
        rq = (x @ rq_w + rq_b).reshape(B, S, LATENT_HEADS, LATENT_HD).transpose(0, 2, 1, 3)
        rkv = pooled @ rkv_w + rkv_b
        rk, rv = jnp.split(rkv, 2, axis=-1)
        rk = rk.reshape(B, nlat, LATENT_HEADS, LATENT_HD).transpose(0, 2, 1, 3)
        rv = rv.reshape(B, nlat, LATENT_HEADS, LATENT_HD).transpose(0, 2, 1, 3)
        lscale = 1.0 / np.sqrt(LATENT_HD)
        lscores = jnp.einsum('bhsd,bhld->bhsl', rq, rk) * lscale
        lat_allowed = jnp.arange(nlat)[None, :] < chunk_ids[:, None]
        lscores = jnp.where(lat_allowed[None, None], lscores, NEG)
        lattn = jax.nn.softmax(lscores, axis=-1)
        lattn = jnp.where(lat_allowed.any(-1)[None, None, :, None], lattn, 0.0)
        lat_out = jnp.einsum('bhsl,bhld->bhsd', lattn, rv)
        lat_out = lat_out.transpose(0, 2, 1, 3).reshape(B, S, LATENT_D)
        remote = lat_out @ rout_w + rout_b
        remote_h = remote.reshape(B, S, N_HEADS, HEAD_DIM).transpose(0, 2, 1, 3)
        gate = jax.nn.sigmoid(local @ gl_w + remote_h @ gr_w)
        mixed = gate * local + (1.0 - gate) * remote_h
        mixed = mixed.transpose(0, 2, 1, 3).reshape(B, S, D)
        return mixed @ out_w + out_b

    def _L0_ffn_ref(x, attn_mask, Wg, Wq, bq, Wkv, bkv, Wo, bo, ln_g, ln_b):
        import jax, jax.numpy as jnp
        import numpy as np
        S, B, D, H, DH = (1024, 8, 256, 16, 64)

        def _forward(x, Wg, Wq, bq, Wkv, bkv, Wo, bo, ln_g, ln_b):
            s_len, bsz, d_model = x.shape
            n_head, _, d_head = Wq.shape
            cap = s_len // n_head
            scale = 1.0 / d_head ** 0.5
            h = jnp.transpose(x, (1, 0, 2))
            t = h
            probs = jax.nn.softmax(h @ Wg, axis=-1)
            scores = jnp.transpose(probs, (0, 2, 1))
            _, idx = jax.lax.top_k(scores, cap)
            idx = jnp.sort(idx, axis=-1)
            hg = jnp.take_along_axis(h[:, None, :, :], idx[..., None], axis=2)
            hg = jnp.transpose(hg, (1, 0, 2, 3))
            q = jnp.einsum('hbcd,hde->hbce', hg, Wq) + bq[:, None, None, :]
            kv = jnp.einsum('hbcd,hde->hbce', hg, Wkv) + bkv[:, None, None, :]
            k, v = jnp.split(kv, 2, axis=-1)
            att = jnp.einsum('hbid,hbjd->hbij', q, k) * scale
            p = jax.nn.softmax(att, axis=1)
            av = jnp.einsum('hbij,hbjd->hbid', p, v)
            ao = jnp.einsum('hbid,hde->hbie', av, Wo) + bo
            tok = jnp.transpose(idx, (1, 0, 2))
            b_ids = jnp.arange(bsz)[None, :, None]
            outs = jnp.zeros_like(t).at[b_ids, tok].add(ao)
            y = t + outs
            mu = jnp.mean(y, axis=-1, keepdims=True)
            var = jnp.var(y, axis=-1, keepdims=True)
            yn = (y - mu) * jax.lax.rsqrt(var + 1e-05) * ln_g + ln_b
            return jnp.transpose(yn, (1, 0, 2))
        return _forward(x, Wg, Wq, bq, Wkv, bkv, Wo, bo, ln_g, ln_b)
    x = L0_attn_x
    mod = (_silu(L0_c) @ L0_wmod).reshape(L0_c.shape[0], 6, 1, -1)
    sa, ca, ga, sb, cb, gb = (mod[:, 0], mod[:, 1], mod[:, 2], mod[:, 3], mod[:, 4], mod[:, 5])
    ga = (2 * (ga >= 0) - 1) * jnp.maximum(jnp.abs(ga), 0.25)
    gb = (2 * (gb >= 0) - 1) * jnp.maximum(jnp.abs(gb), 0.25)
    h = _layernorm(x, axis=-1) * (1 + ca) + sa
    x = x + ga * _L0_attn_ref(h, L0_attn_qkv_w, L0_attn_qkv_b, L0_attn_rq_w, L0_attn_rq_b, L0_attn_rkv_w, L0_attn_rkv_b, L0_attn_rout_w, L0_attn_rout_b, L0_attn_out_w, L0_attn_out_b, L0_attn_gl_w, L0_attn_gr_w)
    h = _layernorm(x, axis=-1) * (1 + cb) + sb
    x = x + gb * _L0_ffn_ref(h, L0_ffn_attn_mask, L0_ffn_Wg, L0_ffn_Wq, L0_ffn_bq, L0_ffn_Wkv, L0_ffn_bkv, L0_ffn_Wo, L0_ffn_bo, L0_ffn_ln_g, L0_ffn_ln_b)
    return x

_drawn_inputs = setup_inputs


def setup_inputs(seed=0):
    import zlib

    import numpy as np

    out = dict(_drawn_inputs(seed))
    spreads = {'L0_attn_qkv_b': (0.0, 0.8),
     'L0_attn_rq_b': (0.0, 0.8),
     'L0_attn_rkv_b': (0.0, 0.8),
     'L0_attn_rout_b': (0.0, 0.8),
     'L0_attn_out_b': (0.0, 0.347),
     'L0_ffn_bq': (0.0, 0.1),
     'L0_ffn_bkv': (0.0, 0.1),
     'L0_ffn_bo': (0.0, 0.1),
     'L0_ffn_ln_g': (1.0, 0.2),
     'L0_ffn_ln_b': (0.0, 0.344)}
    factors = {'L0_attn_qkv_w': 8.0,
     'L0_attn_rq_w': 8.0,
     'L0_attn_rkv_w': 8.0,
     'L0_attn_rout_w': 8.0,
     'L0_attn_out_w': 8.0,
     'L0_attn_gl_w': 8.0,
     'L0_attn_gr_w': 8.0}
    for name, (base, spread) in spreads.items():
        noise = np.random.default_rng([zlib.crc32(name.encode()), seed]).standard_normal(out[name].shape)
        drawn = base * np.exp(spread * noise) if base else spread * noise
        out[name] = jnp.asarray(drawn.astype(out[name].dtype))
    for name, factor in factors.items():
        out[name] = (out[name] * factor).astype(out[name].dtype)
    return out
```

```python
from contextlib import ExitStack

import concourse.bass as bass
from concourse import mybir

F32 = mybir.dt.float32
BF16 = mybir.dt.bfloat16
ALU = mybir.AluOpType
ACT = mybir.ActivationFunctionType
AX_X = mybir.AxisListType.X

B, S, D = 4, 1024, 256
P = 128
KC = D // P
H, HD = 16, 16
NB = S // P
NT = B * NB
LH, LT, LD = 4, 64, 64
CH = S // LT
CPB = P // CH
VC = HD + 2
NTERM = 6
KS = NTERM * HD
NP = H // 2
NG = H // 4
RING = 4
EPS = 1e-5
BIG = -1.0e9
Q_SLOTS = {1: (2, 5, 1), 2: (1, 6, 4), 3: (0, 1, 1)}
K_SLOTS = {1: (0, 3, 1), 2: (3, 6, 2), 3: (4, 5, 1)}

BASE = 6
Y_BASE = 3

SU_SILU, SU_MODT, SU_PRE, SU_GA, SU_BATCH = 4, 6, 30, 9, 17
SU_ALL = SU_PRE + B * SU_BATCH + 3 + RING
SU_POOL = 22

C_ID, C_SM, C_SM0, C_BD, C_RV = 0, P, P + 2 * P, P + 3 * P, P + 3 * P + NB * LH * LT
C_IND = C_RV + 2 * LD
C_SEL = C_IND + P
C_VAL = C_SEL + H
C_BRK = C_VAL + 1
C_END = C_BRK + 1

R_QK, R_V, R_RV = 0, 2 * D, 3 * D
R_G, R_B, R_O = R_RV + LD, R_RV + LD + D, R_RV + LD + 2 * D
R_GL, R_GR = R_O + D, R_O + D + HD
R_END = R_GR + HD


def build(nc, x, qkv_w, rq_w, rq_b, rkv_w, rk_b, rout_w, rout_b, out_w, c_t, wmod, rows, consts, out):
    ctx = ExitStack()
    with ctx:
        def sb(name, shape, dt=F32):
            return ctx.enter_context(nc.sbuf_tensor(name, shape, dt))

        def bank(name):
            return ctx.enter_context(nc.psum_tensor(name, [P, 512], F32))

        started = {"PE": [], "DVE": [], "ACT": [], "POOL": []}

        def sem(name):
            return ctx.enter_context(nc.semaphore(name))

        def counted(name, engine, dummies=0):
            s = sem(name)
            started[engine].append((s, BASE - dummies))
            return s

        XPAD = 3
        x_all = sb("x_all", [P, (XPAD + NT + 1) * D])
        cst = sb("cst", [P, C_END])
        row = sb("row", [P, R_END])
        ident = cst[:, C_ID:C_ID + P]
        ident_bf = sb("ident_bf", [P, P], BF16)
        smask = cst[:, C_SM:C_SM + 2 * P]
        smask0 = cst[:, C_SM0:C_SM0 + P]
        wqk = sb("wqk", [P, KC, 2 * D])
        wv = sb("wv", [P, KC, H, HD + 1])
        bv = sb("bv", [P, H, HD + 1])
        wrq = sb("wrq", [P, KC, P])
        wrk = sb("wrk", [P, KC, P])
        wrv = sb("wrv", [P, KC, LD])
        brq = sb("brq", [LD, 1])
        brk = sb("brk", [P, 1])
        wro = sb("wro", [P, D + H])
        wo = sb("wo", [P, (B + 1) * KC * D])
        obg = sb("obg", [P, (B + 1) * D])
        c1 = sb("c1", [P, (B + 1) * D])
        s1 = sb("s1", [P, (B + 1) * D])
        g3 = sb("g3", [P, (B + 1) * D])
        b3 = sb("b3", [P, (B + 1) * D])
        mod_t = sb("mod_t", [P, (B + 1) * 8])
        ct = sb("ct", [P, KC, B])
        cs = sb("cs", [P, KC, B])
        cbc = sb("cbc", [P, KC, B, P])
        st = sb("st", [P, 6])
        mv = sb("mv", [P, 2])
        rstd = sb("rstd", [P, 1])
        ve1, ve2, ve3 = sb("ve1", [P, 1]), sb("ve2", [P, 1]), sb("ve3", [P, 1])
        half = sb("half", [P, 1])
        xn = sb("xn", [P, 2, D])
        hT = sb("hT", [P, 2, KC, P])
        pooled = sb("pooled", [P, KC, 2, LT])
        qkf = sb("qkf", [P, 2 * D])
        res = sb("res", [P, 2 * D])
        qtok = sb("qtok", [P, H, KS], BF16)
        ktok = sb("ktok", [P, H, KS], BF16)
        qst = sb("qst", [P, RING, H, P], BF16)
        kst = sb("kst", [P, RING, H, P], BF16)
        vp = sb("vp", [P, RING, H, VC])
        rqT = sb("rqT", [P, 2, P])
        bd = sb("bd", [P, 2, LH, LT])
        rvb = sb("rvb", [P, LD])
        bvd = sb("bvd", [P, 2, 2, P])
        mx = sb("mx", [P, H])
        mtok = sb("mtok", [P, P], BF16)
        junk = sb("junk", [P, 4, 2 * P], BF16)
        pr = sb("pr", [P, H, 2, P])
        oT = sb("oT", [P, 4 * P])
        lmx = sb("lmx", [P, LH])
        ls = sb("ls", [P, LH, LT])
        le = sb("le", [P, LH, LT])
        lsum = sb("lsum", [P, LH])
        lrec = sb("lrec", [P, LH])
        lrec2 = sb("lrec2", [P, LH])
        lp = sb("lp", [P, LH * LT])
        lpT = sb("lpT", [P, 2 * P])
        loT = sb("loT", [P, P])
        rem = sb("rem", [P, RING, D + H])
        ssum = sb("ssum", [P, H])
        srec = sb("srec", [P, H])
        local = sb("local", [P, H, HD])
        zl = sb("zl", [P, H])
        z = sb("z", [P, H])
        ez = sb("ez", [P, H])
        g1 = sb("g1", [P, H])
        gate = sb("gate", [P, H])
        dif = sb("dif", [P, D])
        dg = sb("dg", [P, D])
        mix = sb("mix", [P, D])
        mixT = sb("mixT", [P, D])
        xb = sb("xb", [P, D])
        x1 = sb("x1", [P, 2, D])
        st2 = sb("st2", [P, 6])
        mv2 = sb("mv2", [P, 2])
        rstd2 = sb("rstd2", [P, 1])
        h2n = sb("h2n", [P, D])
        h2a = sb("h2a", [P, D])
        h2 = sb("h2", [P, D])
        st3 = sb("st3", [P, 6])
        mv3 = sb("mv3", [P, 2])
        rstd3 = sb("rstd3", [P, 1])
        h3 = sb("h3", [P, D])
        ux = sb("ux", [P, D])
        ya = sb("ya", [P, D])
        y = sb("y", [P, 2, D])
        wm = pr[:, 0:12, :, :].rearrange("p h a n -> p (h a n)").rearrange("p (k n) -> p k n", k=KC)
        gt = pr[:, 12:16, :, :].rearrange("p h a n -> p (h a n)")
        tmp = kst[:, :, :, :].rearrange("p r h n -> p (r h n)").bitcast(F32)[:, 0:2 * KC * D]

        p_a, p_qkv, p_misc = bank("p_a"), bank("p_qkv"), bank("p_misc")
        p_x = [bank("p_x0"), bank("p_x1")]
        p_y = [bank("p_y0"), bank("p_y1")]
        p_pv = bank("p_pv")

        loaded_c, loaded_w, loaded_x0, loaded_x = sem("loaded_c"), sem("loaded_w"), sem("loaded_x0"), sem("loaded_x")
        y_stored = [sem("y_stored0"), sem("y_stored1")]
        su_dve, su_act, su_pe, su_pool = sem("setup_dve"), sem("setup_act"), sem("setup_pe"), sem("setup_pool")

        st1_ready, mv1_ready, ve1_ready = (counted(n, "DVE") for n in ("st1_ready", "mv1_ready", "ve1_ready"))
        rstd1_ready = counted("rstd1_ready", "POOL")
        xn_ready = counted("xn_ready", "DVE")
        hT_psum, hT_ready = counted("hT_psum", "PE"), counted("hT_ready", "ACT")
        pooled_once, pooled_ready = counted("pooled_once", "DVE"), counted("pooled_ready", "DVE")
        qk_psum, qk_copied = counted("qk_psum", "PE"), counted("qk_copied", "DVE")
        v_psum, v_copied = counted("v_psum", "PE"), counted("v_copied", "DVE")
        lat_psum, lat_copied, rvb_ready, bvd_ready = (counted("lat_psum", "PE"), counted("lat_copied", "DVE"),
                                                      counted("rvb_ready", "DVE"), counted("bvd_ready", "DVE"))
        part1_ready, res_ready = counted("part1_ready", "ACT"), counted("res_ready", "POOL")
        part2_ready, part3_ready = counted("part2_ready", "ACT"), counted("part3_ready", "POOL")
        stack_psum = [counted(f"stack_psum{u}", "PE") for u in range(4)]
        stack_copied = [counted(f"stack_copied{u}", "ACT" if u < 2 else "DVE") for u in range(4)]
        s_psum = [counted(f"s_psum{i}", "PE") for i in range(NP)]
        s_max = [counted(f"s_max{i}", "DVE") for i in range(NP)]
        m_ready = counted("m_ready", "DVE")
        mT_psum, shift_ready = counted("mT_psum", "PE", 1), counted("shift_ready", "DVE", 1)
        st_psum = [counted(f"st_psum{i}", "PE", 1) for i in range(NP)]
        exp_done = [counted(f"exp_done{i}", "ACT", 1) for i in range(NP)]
        masked = [counted(f"masked{g}", "POOL", 1) for g in range(NG)]
        pv_psum = [counted(f"pv_psum{g}", "PE", 1) for g in range(NG)]
        ls_psum, lmx_ready, ls_ready, lexp_ready = (counted("ls_psum", "PE"), counted("lmx_ready", "DVE"),
                                                    counted("ls_ready", "DVE"), counted("lexp_ready", "ACT"))
        lsum_ready, lrec_ready, lval_ready, lp_ready = (counted(n, "DVE") for n in
                                                        ("lsum_ready", "lrec_ready", "lval_ready", "lp_ready"))
        lpT_psum, lpT_ready = counted("lpT_psum", "PE"), counted("lpT_ready", "ACT")
        loT_psum, loT_ready = counted("loT_psum", "PE"), counted("loT_ready", "ACT")
        rem_psum, rem_ready = counted("rem_psum", "PE"), counted("rem_ready", "ACT")
        oT_ready = counted("oT_ready", "ACT", 2)
        o_psum = counted("o_psum", "PE", 2)
        ssum_ready, srec_ready, zl_ready, local_ready, z_ready = (
            counted(n, "DVE", 2) for n in ("ssum_ready", "srec_ready", "zl_ready", "local_ready", "z_ready"))
        ez_ready = counted("ez_ready", "ACT", 2)
        g1_ready, gate_ready, dif_ready, dg_ready, mix_ready = (
            counted(n, "DVE", 2) for n in ("g1_ready", "gate_ready", "dif_ready", "dg_ready", "mix_ready"))
        mixT_psum, mixT_ready = counted("mixT_psum", "PE", 2), counted("mixT_ready", "ACT", 2)
        xb_ready = counted("xb_ready", "POOL", 2)
        out_psum, x1_ready = counted("out_psum", "PE", 2), counted("x1_ready", "DVE", 2)
        st2_ready, mv2_ready, ve2_ready, h2n_ready = (
            counted(n, "DVE", 3) for n in ("st2_ready", "mv2_ready", "ve2_ready", "h2n_ready"))
        rstd2_ready, rstd3_ready = counted("rstd2_ready", "POOL", 3), counted("rstd3_ready", "POOL", 3)
        ux_ready, h2a_ready, h2_ready = (counted(n, "POOL", 3) for n in ("ux_ready", "h2a_ready", "h2_ready"))
        st3_ready, mv3_ready, ve3_ready, h3_ready = (
            counted(n, "DVE", 3) for n in ("st3_ready", "mv3_ready", "ve3_ready", "h3_ready"))
        ya_ready, y_ready = counted("ya_ready", "POOL", 3), counted("y_ready", "POOL", 3)

        def done(t):
            return t[0] + (t[1] + 1 + BASE)

        def back(t, k):
            return (t[0], t[1] - k)

        def batch(t):
            return t[0] + 8 * (t[1] // NB) + 8

        def x_of(t):
            return x_all[:, bass.ds((t[0] + (t[1] + XPAD)) * D, D)]

        def per_batch(tile, t, width=D):
            return tile[:, bass.ds(batch(t) * (width // NB), width)]

        def heads(ap, k=HD):
            return ap.rearrange("p (h k) -> p h k", k=k)

        def bc(ap, n):
            return ap.unsqueeze(2).to_broadcast([ap.shape[0], ap.shape[1], n])

        def slots(tok, rule):
            a, e, s = rule
            return tok[:, :, :].rearrange("p h (s k) -> p h s k", k=HD)[:, :, a:e:s, :]

        def rep(ap, rule):
            a, e, s = rule
            n = len(range(a, e, s))
            return heads(ap).unsqueeze(2).to_broadcast([P, H, n, HD])

        block = ctx.enter_context(nc.Block())

        def wait_apart(eng, *waits):
            values = [v if isinstance(v, int) else eng.snap(eng.to_reg(v)) for _, v in waits]
            eng.wait_ge(su_act, 1)
            for (s, _), v in zip(waits, values):
                eng.wait_ge(s, v)

        def run(eng, slot):
            with eng.Fori(0, NT - NB + 1, NB) as i:
                for n in range(NB):
                    slot((i, n), "ASTCD")
            slot((NT, 0), "TCD")
            slot((NT, 1), "CD")
            slot((NT, 2), "D")

        def stored(t):
            return t[0] * 8 + 16 * (t[1] // 2 + 1 + Y_BASE)

        @block.sync
        def _(sp):
            for p in range(2):
                sp.sem_inc(y_stored[p], 16 * Y_BASE)
            sp.dma_start(ct[:, :, :], c_t).then_inc(loaded_c, 16)
            sp.dma_start(wm, wmod.rearrange("(k p) n -> p k n", p=P)).then_inc(loaded_c, 16)
            sp.dma_start(cst[:, :], consts).then_inc(loaded_w, 16)
            sp.dma_start(row[:, :], rows.partition_broadcast(P)).then_inc(loaded_w, 16)
            sp.dma_start(x_all[:, XPAD * D:(XPAD + NB) * D].rearrange("p (t d) -> p t d", d=D),
                         x[0:NB].rearrange("t p d -> p t d")).then_inc(loaded_x0, 16)
            sp.dma_start(x_all[:, (XPAD + NB) * D:(XPAD + NT) * D].rearrange("p (t d) -> p t d", d=D),
                         x[NB:NT].rearrange("t p d -> p t d")).then_inc(loaded_x, 16)

            def store(t):
                sp.wait_ge(y_ready, done(t))
                sp.dma_start(out[bass.ds(t[0] + t[1], 1)].rearrange("t p d -> (t p) d"),
                             y[:, t[1] % 2, :]).then_inc(y_stored[t[1] % 2], 16)

            for n in range(3, NB):
                store((0, n - 3))
            with sp.Fori(NB, NT - NB + 1, NB) as i:
                for n in range(NB):
                    store((i, n - 3))
            for n in range(3):
                store((NT, n - 3))
            for p in range(2):
                sp.wait_ge(y_stored[p], stored((NT, p - 2)))

        @block.gpsimd
        def _(pool):
            for s, v in started["POOL"]:
                pool.sem_inc(s, v)
            for t in (rqT, vp, loT, bvd, rem, pooled, wrq, wrk, wro, mtok, mod_t):
                pool.memset(t[:], 0.0).then_inc(su_pool, 1)
            pool.memset(oT[:, :], 0.0).then_inc(su_pool, 1)
            pool.memset(x_all[:, 0:XPAD * D], 0.0).then_inc(su_pool, 1)
            pool.memset(x_all[:, (XPAD + NT) * D:], 0.0).then_inc(su_pool, 1)
            for t in (obg, c1, s1, g3, b3):
                pool.memset(t[:, 0:D], 0.0).then_inc(su_pool, 1)
            pool.memset(wo[:, 0:KC * D], 0.0).then_inc(su_pool, 1)
            pool.memset(x1[:], 0.0).then_inc(su_pool, 1)
            pool.memset(half[:, :], -0.5).then_inc(su_pool, 1)
            pool.wait_ge(su_pool, SU_POOL)
            pool.wait_ge(su_dve, SU_ALL)
            pool.wait_ge(loaded_x0, 16)
            pool.wait_ge(loaded_x, 16)

            def res1(t):
                pool.wait_ge(part1_ready, done(t))
                pool.tensor_tensor(heads(res[:, 0:D]), heads(qkf[:, 0:D]), slots(qtok, Q_SLOTS[1])[:, :, 0, :], ALU.subtract)
                pool.tensor_tensor(heads(res[:, D:2 * D]), heads(qkf[:, D:2 * D]), slots(ktok, K_SLOTS[1])[:, :, 0, :],
                                   ALU.subtract).then_inc(res_ready, 1)

            def part3(t):
                pool.wait_ge(part2_ready, done(t))
                pool.tensor_tensor(slots(qtok, Q_SLOTS[3])[:, :, 0, :], heads(res[:, 0:D]),
                                   slots(qtok, Q_SLOTS[2])[:, :, 0, :], ALU.subtract)
                pool.tensor_tensor(slots(ktok, K_SLOTS[3])[:, :, 0, :], heads(res[:, D:2 * D]),
                                   slots(ktok, K_SLOTS[2])[:, :, 0, :], ALU.subtract).then_inc(part3_ready, 1)

            def mask(t, g):
                wait_apart(pool, (exp_done[2 * g + 1], done(t)))
                own = pr[:, 4 * g:4 * g + 4, 1, :]
                ins = pool.affine_select(out=own, in_=own, compare_op=ALU.is_ge, fill=0.0, base=-1,
                                         pattern=[[0, 4], [1, P]], channel_multiplier=-1)
                if t[1] % NB:
                    prev = pr[:, 4 * g:4 * g + 4, 0, :]
                    ins = pool.affine_select(out=prev, in_=prev, compare_op=ALU.is_ge, fill=0.0, base=-1,
                                             pattern=[[0, 4], [-P, P]], channel_multiplier=P + 1)
                ins.then_inc(masked[g], 1)

            def power(ve_, rstd_, s_ve, s_rstd, t):
                pool.wait_ge(s_ve, done(t))
                pool.tensor_tensor(rstd_[:, :], ve_[:, :], half[:, :], ALU.pow).then_inc(s_rstd, 1)

            def rstd1(t):
                pool.wait_ge(xn_ready, done(back(t, 1)))
                power(ve1, rstd, ve1_ready, rstd1_ready, t)

            def rstd2_of(t):
                power(ve2, rstd2, ve2_ready, rstd2_ready, t)

            def rstd3_of(t):
                power(ve3, rstd3, ve3_ready, rstd3_ready, t)

            def add_bias(t):
                wait_apart(pool, (x1_ready, done(back(t, 1))))
                pool.tensor_tensor(xb[:, :], x_of(t), per_batch(obg, t), ALU.add).then_inc(xb_ready, 1)

            def add_u(t):
                wait_apart(pool, (x1_ready, done(t)), (y_ready, done(back(t, 1))))
                pool.tensor_tensor(ux[:, :], x1[:, t[1] % 2, :], per_batch(b3, t), ALU.add).then_inc(ux_ready, 1)

            def modulate(t):
                wait_apart(pool, (h2n_ready, done(t)), (h3_ready, done(back(t, 1))))
                pool.tensor_tensor(h2a[:, :], h2n[:, :], per_batch(c1, t), ALU.mult).then_inc(h2a_ready, 1)
                wait_apart(pool, (h2a_ready, done(t)))
                pool.tensor_tensor(h2[:, :], h2a[:, :], per_batch(s1, t), ALU.add).then_inc(h2_ready, 1)

            def finish(t):
                wait_apart(pool, (h3_ready, done(t)))
                pool.tensor_tensor(ya[:, :], h3[:, :], per_batch(g3, t), ALU.mult).then_inc(ya_ready, 1)
                pool.wait_ge(ya_ready, done(t))
                pool.wait_ge(ux_ready, done(t))
                pool.wait_ge(y_stored[t[1] % 2], stored(back(t, 2)))
                pool.tensor_tensor(y[:, t[1] % 2, :], ya[:, :], ux[:, :], ALU.add).then_inc(y_ready, 1)

            def slot(t, stages):
                if "A" in stages:
                    rstd1(back(t, -1))
                rstd2_of(back(t, 3))
                if "D" in stages:
                    add_u(back(t, 3))
                if "C" in stages:
                    add_bias(back(t, 2))
                if "D" in stages:
                    modulate(back(t, 3))
                if "T" in stages:
                    mask(back(t, 1), 0)
                if "A" in stages:
                    res1(back(t, -1))
                if "T" in stages:
                    mask(back(t, 1), 1)
                rstd3_of(back(t, 3))
                if "A" in stages:
                    part3(back(t, -1))
                if "T" in stages:
                    mask(back(t, 1), 2)
                if "D" in stages:
                    finish(back(t, 3))
                if "T" in stages:
                    mask(back(t, 1), 3)

            rstd1((0, 0))
            res1((0, 0))
            part3((0, 0))
            run(pool, slot)

        @block.scalar
        def _(act):
            act.dma_start(wqk[:, :, :], qkv_w[:, 0:2 * D].rearrange("(k p) n -> p k n", p=P)).then_inc(loaded_w, 16)
            act.dma_start(tmp[:, 0:KC * D].rearrange("p (k n) -> p k n", k=KC),
                          qkv_w[:, 2 * D:3 * D].rearrange("(k p) n -> p k n", p=P)).then_inc(loaded_w, 16)
            act.dma_start(tmp[:, KC * D:2 * KC * D].rearrange("p (k n) -> p k n", k=KC),
                          out_w.rearrange("(k p) n -> p k n", p=P)).then_inc(loaded_w, 16)
            act.wait_ge(su_pool, SU_POOL)
            act.dma_start(wrq[:, :, 0:LD], rq_w.rearrange("(k p) n -> p k n", p=P)).then_inc(loaded_w, 16)
            act.dma_start(wrk[:, :, 0:LD], rkv_w[:, 0:LD].rearrange("(k p) n -> p k n", p=P)).then_inc(loaded_w, 16)
            act.dma_start(wrv[:, :, :], rkv_w[:, LD:2 * LD].rearrange("(k p) n -> p k n", p=P)).then_inc(loaded_w, 16)
            act.dma_start(wro[0:LD, 0:D], rout_w).then_inc(loaded_w, 16)
            act.dma_start(wro[LD:LD + 1, 0:D], rout_b).then_inc(loaded_w, 16)
            act.dma_start(brq[:, :], rq_b).then_inc(loaded_w, 16)
            act.dma_start(brk[0:LD, :], rk_b).then_inc(loaded_w, 16)
            for s, v in started["ACT"]:
                act.sem_inc(s, v)
            act.wait_ge(loaded_c, 32)
            act.activation(cs[:, :, :], ct[:, :, :], ACT.Exp, scale=-1.0).then_inc(su_act, 1)

            def modulated(t):
                wait_apart(act, (hT_psum, done(t)), (v_psum, done(back(t, 2))), (lat_psum, done(back(t, 2))))
                for k in range(KC):
                    ins = act.activation(hT[:, t[1] % 2, k, :], p_a[:, k * P:(k + 1) * P], ACT.Identity,
                                         scale=mod_t[:, bass.ds(batch(t) + (k - 8), 1)],
                                         bias=mod_t[:, bass.ds(batch(t) + (k + KC - 8), 1)])
                ins.then_inc(hT_ready, 1)

            def part1(t):
                act.wait_ge(qk_copied, done(t))
                act.wait_ge(stack_psum[3], done(back(t, 1)))
                act.activation(slots(qtok, Q_SLOTS[1]), rep(qkf[:, 0:D], Q_SLOTS[1]), ACT.Copy)
                act.activation(slots(ktok, K_SLOTS[1]), rep(qkf[:, D:2 * D], K_SLOTS[1]), ACT.Copy).then_inc(part1_ready, 1)

            def part2(t):
                act.wait_ge(res_ready, done(t))
                act.activation(slots(qtok, Q_SLOTS[2]), rep(res[:, 0:D], Q_SLOTS[2]), ACT.Copy)
                act.activation(slots(ktok, K_SLOTS[2]), rep(res[:, D:2 * D], K_SLOTS[2]), ACT.Copy).then_inc(part2_ready, 1)

            def q_stack(t, u):
                act.wait_ge(stack_psum[u], done(t))
                act.wait_ge(st_psum[NP - 1], done(back(t, 3)))
                act.activation(qst[0:KS, t[1] % RING, 8 * u:8 * u + 8, :].rearrange("p h n -> p (h n)"),
                               p_x[u][0:KS, :].bitcast(BF16), ACT.Copy).then_inc(stack_copied[u], 1)

            def exps(t, i):
                act.wait_ge(st_psum[i], done(t))
                act.wait_ge(pv_psum[i // 2], done(back(t, 1)))
                src = p_y[i % 2][:, :].rearrange("p (h a n) -> p h a n", h=2, a=2)
                if t[1] % NB:
                    act.activation(pr[:, 2 * i:2 * i + 2, :, :], src, ACT.Exp).then_inc(exp_done[i], 1)
                else:
                    act.activation(pr[:, 2 * i:2 * i + 2, 1, :], src[:, :, 1, :], ACT.Exp).then_inc(exp_done[i], 1)

            def out_t(t):
                act.wait_ge(pv_psum[NG - 1], done(t))
                act.wait_ge(o_psum, done(back(t, 1)))
                act.activation(oT[:, :], p_pv[:, :], ACT.Copy).then_inc(oT_ready, 1)

            def lat_exp(t):
                act.wait_ge(ls_ready, done(t))
                act.wait_ge(lp_ready, done(back(t, 1)))
                act.activation(le[:, :, :], ls[:, :, :], ACT.Exp).then_inc(lexp_ready, 1)

            def lat_pT(t):
                act.wait_ge(lpT_psum, done(t))
                act.wait_ge(loT_psum, done(back(t, 1)))
                act.activation(lpT[:, :], p_misc[:, 0:2 * P], ACT.Copy).then_inc(lpT_ready, 1)

            def lat_oT(t):
                act.wait_ge(loT_psum, done(t))
                act.wait_ge(rem_psum, done(back(t, 1)))
                act.activation(loT[0:LD, :], p_misc[0:LD, 0:P], ACT.Copy).then_inc(loT_ready, 1)

            def remote(t):
                act.wait_ge(rem_psum, done(t))
                act.wait_ge(mix_ready, done(back(t, RING)))
                act.activation(rem[:, t[1] % RING, :], p_misc[:, 0:D + H], ACT.Copy).then_inc(rem_ready, 1)

            def gate_exp(t):
                act.wait_ge(z_ready, done(t))
                act.wait_ge(g1_ready, done(back(t, 1)))
                act.activation(ez[:, :], z[:, :], ACT.Exp, scale=-1.0).then_inc(ez_ready, 1)

            def mixed_t(t):
                act.wait_ge(mixT_psum, done(t))
                act.wait_ge(out_psum, done(back(t, 1)))
                act.activation(mixT[:, :], p_misc[:, 0:D], ACT.Copy).then_inc(mixT_ready, 1)

            def slot(t, stages):
                a, m, c = back(t, -1), back(t, 1), back(t, 2)
                if "C" in stages:
                    out_t(c)
                if "A" in stages:
                    modulated(a)
                    lat_exp(t)
                if "T" in stages:
                    exps(m, 0)
                    exps(m, 1)
                if "C" in stages:
                    gate_exp(c)
                if "A" in stages:
                    part1(a)
                if "T" in stages:
                    exps(m, 2)
                    exps(m, 3)
                if "A" in stages:
                    lat_pT(t)
                    part2(a)
                if "C" in stages:
                    mixed_t(c)
                if "T" in stages:
                    exps(m, 4)
                    exps(m, 5)
                if "A" in stages:
                    lat_oT(t)
                if "T" in stages:
                    exps(m, 6)
                if "A" in stages:
                    remote(t)
                if "T" in stages:
                    exps(m, 7)
                if "A" in stages:
                    q_stack(a, 0)
                    q_stack(a, 1)

            act.wait_ge(su_dve, SU_MODT)
            modulated((0, 0))
            part1((0, 0))
            part2((0, 0))
            q_stack((0, 0), 0)
            q_stack((0, 0), 1)
            act.wait_ge(su_dve, SU_ALL)
            run(act, slot)

        @block.tensor
        def _(pe):
            for s, v in started["PE"]:
                pe.sem_inc(s, v)
            pe.wait_ge(su_dve, SU_SILU)
            pe.wait_ge(loaded_c, 32)
            for j in range(2 * KC):
                for k in range(KC):
                    ins = pe.matmul(p_a[:, j * B:(j + 1) * B], wm[:, k, j * P:(j + 1) * P], cs[:, k, :],
                                    start=(k == 0), stop=(k == KC - 1))
            ins.then_inc(su_pe, 1)
            for b in range(B):
                for j in range(2):
                    if b:
                        pe.wait_ge(su_dve, SU_PRE + SU_BATCH * (b - 1) + (SU_GA, SU_BATCH)[j])
                    for k in range(KC):
                        ins = pe.matmul(p_y[j][:, :], cbc[:, k, b, :], wm[:, k, 2 * D + j * 512:2 * D + (j + 1) * 512],
                                        start=(k == 0), stop=(k == KC - 1))
                    ins.then_inc(su_pe, 1)
            pe.wait_ge(su_dve, SU_ALL)

            def ln_t(t):
                pe.wait_ge(xn_ready, done(t))
                pe.wait_ge(rvb_ready, done(back(t, 1)))
                for k in range(KC):
                    ins = pe.transpose(p_a[:, k * P:(k + 1) * P], xn[:, t[1] % 2, k * P:(k + 1) * P], ident)
                ins.then_inc(hT_psum, 1)

            def project_qk(t):
                pe.wait_ge(hT_ready, done(t))
                pe.wait_ge(v_copied, done(back(t, 1)))
                for k in range(KC):
                    ins = pe.matmul(p_qkv[:, :], hT[:, t[1] % 2, k, :], wqk[:, k, :], start=(k == 0), stop=(k == KC - 1))
                ins.then_inc(qk_psum, 1)

            def project_v(t):
                pe.wait_ge(qk_copied, done(t))
                for k in range(KC):
                    ins = pe.matmul(p_qkv[:, 0:H * (HD + 1)], hT[:, t[1] % 2, k, :],
                                    wv[:, k, :, :].rearrange("p h k -> p (h k)"), start=(k == 0), stop=(k == KC - 1))
                ins.then_inc(v_psum, 1)

            def project_lat(t):
                pe.wait_ge(pooled_ready, done(t))
                for k in range(KC):
                    pe.matmul(p_a[:, 0:P], wrq[:, k, :], hT[:, t[1] % 2, k, :], start=(k == 0), stop=(k == KC - 1))
                for k in range(KC):
                    pe.matmul(p_a[:, 2 * P:2 * P + LT], wrk[:, k, :], pooled[:, k, 0, :], start=(k == 0), stop=(k == KC - 1))
                for k in range(KC):
                    ins = pe.matmul(p_a[:, 3 * P:3 * P + LD], pooled[:, k, :, :].rearrange("p a l -> p (a l)"), wrv[:, k, :], start=(k == 0), stop=(k == KC - 1))
                ins.then_inc(lat_psum, 1)

            def stack(t, u):
                pe.wait_ge(part3_ready, done(t))
                if u < 2:
                    pe.wait_ge(s_max[NP - 2 + u], done(back(t, 1)))
                else:
                    pe.wait_ge(stack_copied[u - 2], done(t))
                src = (qtok, ktok)[u // 2]
                dst = p_x[u % 2][0:KS, :].bitcast(BF16)
                for j in range(8):
                    ins = pe.transpose(dst[:, j * P:(j + 1) * P], src[:, 8 * (u % 2) + j, :], ident_bf[:, :])
                ins.then_inc(stack_psum[u], 1)

            def scores(t, i):
                if i == 0:
                    for u in range(4):
                        pe.wait_ge(stack_copied[u], done(t))
                if i >= 2:
                    pe.wait_ge(s_max[i - 2], done(t))
                n = t[1]
                for h in (2 * i, 2 * i + 1):
                    at = (h % 2) * 2 * P
                    q = qst[0:KS, n % RING, h, :]
                    if n % NB:
                        pe.matmul(p_x[i % 2][:, at:at + P], q, kst[0:KS, (n - 1) % RING, h, :], start=True, stop=True)
                    ins = pe.matmul(p_x[i % 2][:, at + P:at + 2 * P], q, kst[0:KS, n % RING, h, :], start=True, stop=True)
                ins.then_inc(s_psum[i], 1)

            def max_t(t):
                pe.wait_ge(m_ready, done(t))
                pe.wait_ge(oT_ready, done(back(t, 1)))
                pe.transpose(p_pv[:, 0:P // 2].bitcast(BF16), mtok[:, :], ident_bf[:, :]).then_inc(mT_psum, 1)

            def scores_t(t, i):
                pe.wait_ge(shift_ready, done(t))
                pe.wait_ge(exp_done[(i - 2) % NP], done(t if i >= 2 else back(t, 1)))
                n = t[1]
                for h in (2 * i, 2 * i + 1):
                    at = (h % 2) * 2 * P
                    q = qst[0:KS + H, n % RING, h, :]
                    if n % NB:
                        pe.matmul(p_y[i % 2][:, at:at + P], kst[0:KS + H, (n - 1) % RING, h, :], q, start=True, stop=True)
                    ins = pe.matmul(p_y[i % 2][:, at + P:at + 2 * P], kst[0:KS + H, n % RING, h, :], q, start=True, stop=True)
                ins.then_inc(st_psum[i], 1)

            def sum_v(t, g):
                pe.wait_ge(masked[g], done(t))
                n = t[1]
                for a in range(0 if n % NB else 1, 2):
                    for j in range(4):
                        h = 4 * g + j
                        ins = pe.matmul(p_pv[32 * j:32 * j + VC, g * P:(g + 1) * P], vp[:, (n - 1 + a) % RING, h, :],
                                        pr[:, h, a, :], start=(a == 0 or n % NB == 0), stop=(a == 1),
                                        tile_position=(0, 32 * j))
                ins.then_inc(pv_psum[g], 1)

            def lat_scores(t):
                pe.wait_ge(lat_copied, done(t))
                pe.wait_ge(rem_ready, done(back(t, 1)))
                pe.matmul(p_misc[:, 0:LH * LT], rqT[:, t[1] % 2, :], bd[:, t[1] % 2, :, :].rearrange("p h l -> p (h l)"),
                          start=True, stop=True).then_inc(ls_psum, 1)

            def lat_p_t(t):
                pe.wait_ge(lp_ready, done(t))
                pe.wait_ge(z_ready, done(back(t, 2)))
                for k in range(2):
                    ins = pe.transpose(p_misc[:, k * P:(k + 1) * P], lp[:, k * P:(k + 1) * P], ident)
                ins.then_inc(lpT_psum, 1)

            def lat_out_t(t):
                pe.wait_ge(lpT_ready, done(t))
                pe.wait_ge(bvd_ready, done(t))
                pe.wait_ge(mixT_ready, done(back(t, 2)))
                for k in range(2):
                    ins = pe.matmul(p_misc[:, 0:P], bvd[:, t[1] % 2, k, :], lpT[:, k * P:(k + 1) * P],
                                    start=(k == 0), stop=(k == 1))
                ins.then_inc(loT_psum, 1)

            def lat_remote(t):
                pe.wait_ge(loT_ready, done(t))
                pe.wait_ge(x1_ready, done(back(t, 2)))
                pe.matmul(p_misc[:, 0:D + H], loT[:, :], wro[:, :], start=True, stop=True).then_inc(rem_psum, 1)

            def out_tokens(t):
                pe.wait_ge(oT_ready, done(t))
                pe.wait_ge(ls_ready, done_or_last(t))
                pe.wait_ge(x1_ready, done(back(t, 1)))
                for g in range(4):
                    ins = pe.transpose(p_misc[:, g * P:(g + 1) * P], oT[:, g * P:(g + 1) * P], ident)
                ins.then_inc(o_psum, 1)

            def mixed_t(t):
                pe.wait_ge(mix_ready, done(t))
                pe.wait_ge(lpT_ready, done_or_last(t))
                for k in range(KC):
                    ins = pe.transpose(p_misc[:, k * P:(k + 1) * P], mix[:, k * P:(k + 1) * P], ident)
                ins.then_inc(mixT_psum, 1)

            def project_out(t):
                pe.wait_ge(mixT_ready, done(t))
                pe.wait_ge(loT_ready, done_or_last(t))
                for k in range(KC):
                    ins = pe.matmul(p_misc[:, 0:D], mixT[:, k * P:(k + 1) * P],
                                    wo[:, bass.ds(batch(t) * (KC * D // NB) + k * D, D)],
                                    start=(k == 0), stop=(k == KC - 1))
                ins.then_inc(out_psum, 1)

            def done_or_last(t):
                return done(back(t, -2)) if not isinstance(t[0], int) else min(done(back(t, -2)), done((NT, -1)))

            def slot(t, stages):
                a, m, c = back(t, -1), back(t, 1), back(t, 2)
                A, T, C = "A" in stages, "T" in stages, "C" in stages
                if A:
                    scores(t, 0)
                if T:
                    max_t(m)
                if A:
                    scores(t, 1)
                    lat_scores(t)
                    ln_t(a)
                    scores(t, 2)
                if T:
                    scores_t(m, 0)
                    scores_t(m, 1)
                if C:
                    out_tokens(c)
                if A:
                    project_qk(a)
                    scores(t, 3)
                if T:
                    scores_t(m, 2)
                if A:
                    project_lat(a)
                    scores(t, 4)
                if T:
                    scores_t(m, 3)
                if A:
                    lat_p_t(t)
                if T:
                    sum_v(m, 0)
                if A:
                    project_v(a)
                    scores(t, 5)
                if C:
                    mixed_t(c)
                if T:
                    scores_t(m, 4)
                    sum_v(m, 1)
                if A:
                    scores(t, 6)
                if T:
                    scores_t(m, 5)
                if A:
                    lat_out_t(t)
                if C:
                    project_out(c)
                if A:
                    scores(t, 7)
                if T:
                    scores_t(m, 6)
                    sum_v(m, 2)
                if A:
                    lat_remote(t)
                if T:
                    scores_t(m, 7)
                if A:
                    for u in range(4):
                        stack(a, u)
                if T:
                    sum_v(m, 3)

            first = (0, 0)
            ln_t(first)
            project_qk(first)
            project_lat(first)
            project_v(first)
            for u in range(4):
                stack(first, u)
            run(pe, slot)

        @block.vector
        def _(dve):
            for s, v in started["DVE"]:
                dve.sem_inc(s, v)
            count = [0]

            def setup(ins):
                count[0] += 1
                ins.then_inc(su_dve, 1)
                dve.wait_ge(su_dve, count[0])

            dve.wait_ge(su_act, 1)
            setup(dve.tensor_scalar(cs[:, :, :], cs[:, :, :], 1.0, None, ALU.add))
            setup(dve.reciprocal(cs[:, :, :], cs[:, :, :]))
            setup(dve.tensor_tensor(cs[:, :, :], cs[:, :, :], ct[:, :, :], ALU.mult))
            setup(dve.tensor_copy(cbc[:, :, :, :], cs[:, :, :].unsqueeze(3).to_broadcast([P, KC, B, P])))
            assert count[0] == SU_SILU
            dve.wait_ge(su_pe, 1)
            mt = mod_t[:, :].rearrange("p (b j) -> p j b", j=8)
            dve.wait_ge(su_pool, SU_POOL)
            setup(dve.tensor_scalar(mt[:, 0:KC, 0:B], p_a[:, KC * B:2 * KC * B].rearrange("p (j b) -> p j b", b=B),
                                    1.0, None, ALU.add))
            setup(dve.tensor_copy(mt[:, KC:2 * KC, 0:B], p_a[:, 0:KC * B].rearrange("p (j b) -> p j b", b=B)))
            assert count[0] == SU_MODT
            dve.wait_ge(loaded_w, 16 * 12)
            setup(dve.tensor_copy(ident_bf[:, :], ident))
            setup(dve.tensor_scalar(wqk[:, :, 0:D], wqk[:, :, 0:D], HD ** -0.5, None, ALU.mult))
            setup(dve.tensor_scalar(row[:, 0:D], row[:, 0:D], HD ** -0.5, None, ALU.mult))
            setup(dve.tensor_scalar(wrq[:, :, :], wrq[:, :, :], (LD // LH) ** -0.5, None, ALU.mult))
            setup(dve.tensor_scalar(brq[:, :], brq[:, :], (LD // LH) ** -0.5, None, ALU.mult))
            setup(dve.tensor_scalar(wrk[:, :, :], wrk[:, :, :], 1.0 / CH, None, ALU.mult))
            setup(dve.tensor_scalar(wrv[:, :, :], wrv[:, :, :], 1.0 / CH, None, ALU.mult))
            glb = row[:, R_GL:R_GL + HD].unsqueeze(1).to_broadcast([P, H, HD])
            grb = row[:, R_GR:R_GR + HD].unsqueeze(1).to_broadcast([P, H, HD])
            jk = heads(junk[:, 0:2, :].rearrange("p j n -> p (j n)").bitcast(F32))
            for k in range(KC):
                w = heads(tmp[:, k * D:(k + 1) * D])
                setup(dve.tensor_copy(wv[:, k, :, 0:HD], w))
                setup(dve.tensor_tensor(jk, w, glb, ALU.mult))
                setup(dve.tensor_reduce(wv[:, k, :, HD], jk, AX_X, ALU.add))
            bvr = heads(row[:, R_V:R_V + D])
            setup(dve.tensor_copy(bv[:, :, 0:HD], bvr))
            setup(dve.tensor_tensor(jk, bvr, glb, ALU.mult))
            setup(dve.tensor_reduce(bv[:, :, HD], jk, AX_X, ALU.add))
            setup(dve.tensor_tensor(jk, heads(wro[:, 0:D]), grb, ALU.mult))
            setup(dve.tensor_reduce(wro[:, D:D + H], jk, AX_X, ALU.add))
            setup(dve.memset(vp[:, :, :, HD + 1:VC], 1.0))
            setup(dve.memset(loT[LD:LD + 1, :], 1.0))
            setup(dve.memset(p_pv[:, :], 0.0))
            for p in range(2):
                setup(dve.tensor_copy(rqT[LD:P, p, :], cst[LD:P, C_IND:C_IND + P]))
            setup(dve.tensor_copy(brk[LD:P, :], cst[LD:P, C_BRK:C_BRK + 1]))
            assert count[0] == SU_PRE, count[0]
            wo_in = tmp[:, KC * D:2 * KC * D]
            for b in range(B):
                lo, hi = (b + 1) * D, (b + 2) * D
                for j, (src, at) in enumerate(((p_y[0], 0), (p_y[1], D))):
                    dve.wait_ge(su_pe, 2 + 2 * b + j)
                    g_in, g_abs, g_sign, g_out = (gt[:, q * D:(q + 1) * D] for q in range(4))
                    setup(dve.tensor_copy(g_in, src[:, at:at + D]))
                    setup(dve.scalar_tensor_tensor(out=g_abs, in0=g_in, scalar=-1.0, in1=g_in, op0=ALU.mult, op1=ALU.max))
                    setup(dve.tensor_scalar(g_abs, g_abs, 0.25, None, ALU.max))
                    setup(dve.tensor_scalar(g_sign, g_in, 0.0, 2.0, ALU.is_ge, ALU.mult))
                    setup(dve.scalar_tensor_tensor(out=g_out, in0=g_sign, scalar=-1.0, in1=g_abs, op0=ALU.add, op1=ALU.mult))
                    if j == 0:
                        for k in range(KC):
                            setup(dve.tensor_tensor(wo[:, ((b + 1) * KC + k) * D:((b + 1) * KC + k + 1) * D],
                                                    wo_in[:, k * D:(k + 1) * D], g_out, ALU.mult))
                        setup(dve.tensor_tensor(obg[:, lo:hi], row[:, R_O:R_O + D], g_out, ALU.mult))
                        setup(dve.tensor_copy(s1[:, lo:hi], p_y[0][:, D:2 * D]))
                    else:
                        setup(dve.tensor_tensor(g3[:, lo:hi], row[:, R_G:R_G + D], g_out, ALU.mult))
                        setup(dve.tensor_tensor(b3[:, lo:hi], row[:, R_B:R_B + D], g_out, ALU.mult))
                        setup(dve.tensor_scalar(c1[:, lo:hi], p_y[1][:, 0:D], 1.0, None, ALU.add))
            setup(dve.memset(pr[:, :, :, :].rearrange("p h a n -> p (h a n)"), 0.0))
            setup(dve.memset(qst[:, :, :, :].rearrange("p r h n -> p (r h n)"), 0.0))
            setup(dve.memset(kst[:, :, :, :].rearrange("p r h n -> p (r h n)"), 0.0))
            for p in range(RING):
                setup(dve.tensor_copy(kst[KS:KS + 32, p, :, :],
                                      bc(cst[KS:KS + 32, C_SEL:C_SEL + H], P)))
            assert count[0] == SU_ALL, count[0]

            def stats(src, st_, mv_, ve_, s_stats, s_mv, s_ve, t):
                dve.bn_stats(st_[:, :], src).then_inc(s_stats, 1)
                wait_apart(dve, (s_stats, done(t)))
                dve.bn_aggr(mv_[:, :], st_[:, :]).then_inc(s_mv, 1)
                dve.wait_ge(s_mv, done(t))
                dve.tensor_scalar(ve_[:, :], mv_[:, 1:2], EPS, None, ALU.add).then_inc(s_ve, 1)

            def stats1(t):
                stats(x_of(t), st, mv, ve1, st1_ready, mv1_ready, ve1_ready, t)

            def norm1(t):
                dve.wait_ge(rstd1_ready, done(t))
                dve.wait_ge(hT_psum, done(back(t, 2)))
                dve.tensor_scalar(xn[:, t[1] % 2, :], x_of(t), mv[:, 0:1], rstd[:, :], ALU.subtract, ALU.mult)\
                   .then_inc(xn_ready, 1)

            def pool_tokens(t):
                dve.wait_ge(hT_ready, done(t))
                dve.wait_ge(lat_psum, done(back(t, 1)))
                n = t[1] % NB
                new = slice(n * CPB, (n + 1) * CPB)
                dve.tensor_reduce(pooled[:, :, 0, new], hT[:, t[1] % 2, :, :].rearrange("p k (c s) -> p k c s", s=CH),
                                  AX_X, ALU.add).then_inc(pooled_once, 1)
                dve.wait_ge(pooled_once, done(t))
                dve.tensor_copy(pooled[:, :, 1, new], pooled[:, :, 0, new]).then_inc(pooled_ready, 1)

            def copy_qk(t):
                dve.wait_ge(qk_psum, done(t))
                dve.wait_ge(part3_ready, done(back(t, 1)))
                dve.tensor_tensor(qkf[:, :], p_qkv[:, :], row[:, R_QK:R_QK + 2 * D], ALU.add).then_inc(qk_copied, 1)

            def copy_v(t):
                dve.wait_ge(v_psum, done(t))
                dve.wait_ge(pv_psum[NG - 1], done(back(t, 3)))
                dve.tensor_tensor(vp[:, t[1] % RING, :, 0:HD + 1], heads(p_qkv[:, 0:H * (HD + 1)], HD + 1), bv[:, :, :],
                                  ALU.add).then_inc(v_copied, 1)

            def copy_lat(t):
                dve.wait_ge(lat_psum, done(t))
                dve.wait_ge(ls_psum, done(back(t, 2)))
                dve.wait_ge(loT_psum, done(back(t, 2)))
                p, n = t[1] % 2, t[1] % NB
                dve.tensor_scalar(rqT[0:LD, p, :], p_a[0:LD, 0:P], brq[:, :], None, ALU.add)
                rk = p_a[:, 2 * P:2 * P + LT].unsqueeze(1).to_broadcast([P, LH, LT])
                at = C_BD + n * LH * LT
                dve.scalar_tensor_tensor(out=bd[:, p, :, :], in0=rk, scalar=brk[:, :],
                                         in1=cst[:, at:at + LH * LT].rearrange("p (h l) -> p h l", h=LH),
                                         op0=ALU.add, op1=ALU.mult).then_inc(lat_copied, 1)
                dve.tensor_tensor(rvb[:, :], p_a[:, 3 * P:3 * P + LD], row[:, R_RV:R_RV + LD], ALU.add).then_inc(rvb_ready, 1)
                dve.wait_ge(rvb_ready, done(t))
                dve.tensor_tensor(bvd[:, p, :, 0:LD], rvb[:, :].unsqueeze(1).to_broadcast([P, 2, LD]),
                                  cst[:, C_RV:C_RV + 2 * LD].rearrange("p (k l) -> p k l", k=2), ALU.mult).then_inc(bvd_ready, 1)

            def k_stack(t, u):
                dve.wait_ge(stack_psum[2 + u], done(t))
                dve.wait_ge(st_psum[NP - 1], done(back(t, 3)))
                dve.tensor_copy(kst[0:KS, t[1] % RING, 8 * u:8 * u + 8, :].rearrange("p h n -> p (h n)"),
                                p_x[u][0:KS, :].bitcast(BF16)).then_inc(stack_copied[2 + u], 1)

            def maxima(t, i):
                wait_apart(dve, (s_psum[i], done(t)), (s_max[i - 2], done(t if i >= 2 else back(t, 1))),
                           (m_ready, done(back(t, 1))))
                for h in (2 * i, 2 * i + 1):
                    at = (h % 2) * 2 * P
                    scr = junk[:, h % 4, :]
                    if t[1] % NB:
                        ins = dve.tensor_tensor_reduce(scr, p_x[i % 2][:, at:at + 2 * P], smask, 1.0, -3.0e38,
                                                       ALU.add, ALU.max, mx[:, h:h + 1])
                    else:
                        ins = dve.tensor_tensor_reduce(scr[:, 0:P], p_x[i % 2][:, at + P:at + 2 * P], smask0, 1.0,
                                                       -3.0e38, ALU.add, ALU.max, mx[:, h:h + 1])
                ins.then_inc(s_max[i], 1)
                if i == NP - 1:
                    dve.wait_ge(s_max[i], done(t))
                    dve.wait_ge(mT_psum, done(back(t, 1)))
                    dve.tensor_scalar(mtok[:, KS:KS + H], mx[:, :], -1.0, None, ALU.mult).then_inc(m_ready, 1)

            def shift(t):
                dve.wait_ge(mT_psum, done(t))
                dve.tensor_copy(qst[KS:KS + H, t[1] % RING, :, :],
                                p_pv[KS:KS + H, 0:P // 2].bitcast(BF16).unsqueeze(1).to_broadcast([H, H, P]))\
                   .then_inc(shift_ready, 1)

            def lat_shift(t):
                dve.wait_ge(ls_psum, done(t))
                dve.wait_ge(lexp_ready, done(back(t, 1)))
                sc = p_misc[:, 0:LH * LT].rearrange("p (h l) -> p h l", h=LH)
                dve.tensor_reduce(lmx[:, :], sc, AX_X, ALU.max).then_inc(lmx_ready, 1)
                dve.wait_ge(lmx_ready, done(t))
                dve.tensor_tensor(ls[:, :, :], sc, bc(lmx[:, :], LT), ALU.subtract).then_inc(ls_ready, 1)

            def lat_norm(t):
                dve.wait_ge(lexp_ready, done(t))
                dve.wait_ge(lpT_psum, done(back(t, 1)))
                dve.tensor_reduce(lsum[:, :], le[:, :, :], AX_X, ALU.add).then_inc(lsum_ready, 1)
                dve.wait_ge(lsum_ready, done(t))
                dve.reciprocal(lrec[:, :], lsum[:, :]).then_inc(lrec_ready, 1)
                dve.wait_ge(lrec_ready, done(t))
                valid = cst[:, C_VAL:C_VAL + 1] if t[1] % NB == 0 else 1.0
                dve.tensor_scalar(lrec2[:, :], lrec[:, :], valid, None, ALU.mult).then_inc(lval_ready, 1)
                dve.wait_ge(lval_ready, done(t))
                dve.tensor_tensor(lp[:, :].rearrange("p (h l) -> p h l", h=LH), le[:, :, :], bc(lrec2[:, :], LT),
                                  ALU.mult).then_inc(lp_ready, 1)

            def gate_in(t):
                dve.wait_ge(o_psum, done(t))
                o = heads(p_misc[:, :], 32)
                dve.tensor_scalar(ssum[:, :], o[:, :, HD + 1], 1e-30, None, ALU.max).then_inc(ssum_ready, 1)
                dve.wait_ge(ssum_ready, done(t))
                dve.reciprocal(srec[:, :], ssum[:, :]).then_inc(srec_ready, 1)
                dve.wait_ge(srec_ready, done(t))
                dve.tensor_tensor(zl[:, :], o[:, :, HD], srec[:, :], ALU.mult).then_inc(zl_ready, 1)
                dve.tensor_tensor(local[:, :, :], o[:, :, 0:HD], bc(srec[:, :], HD), ALU.mult).then_inc(local_ready, 1)
                dve.wait_ge(local_ready, done(t))
                dve.wait_ge(rem_ready, done(t))
                dve.wait_ge(ez_ready, done(back(t, 1)))
                dve.tensor_tensor(z[:, :], zl[:, :], rem[:, t[1] % RING, D:D + H], ALU.add).then_inc(z_ready, 1)
                dve.tensor_tensor(heads(dif[:, :]), local[:, :, :], heads(rem[:, t[1] % RING, 0:D]), ALU.subtract)\
                   .then_inc(dif_ready, 1)

            def gate_mix(t):
                dve.wait_ge(ez_ready, done(t))
                dve.tensor_scalar(g1[:, :], ez[:, :], 1.0, None, ALU.add).then_inc(g1_ready, 1)
                dve.wait_ge(g1_ready, done(t))
                dve.reciprocal(gate[:, :], g1[:, :]).then_inc(gate_ready, 1)
                dve.wait_ge(gate_ready, done(t))
                dve.wait_ge(dif_ready, done(t))
                dve.tensor_tensor(heads(dg[:, :]), heads(dif[:, :]), bc(gate[:, :], HD), ALU.mult).then_inc(dg_ready, 1)
                dve.wait_ge(dg_ready, done(t))
                dve.wait_ge(mixT_psum, done(back(t, 1)))
                dve.tensor_tensor(mix[:, :], dg[:, :], rem[:, t[1] % RING, 0:D], ALU.add).then_inc(mix_ready, 1)

            def first_residual(t):
                dve.wait_ge(out_psum, done(t))
                dve.wait_ge(xb_ready, done(t))
                dve.wait_ge(ux_ready, done(back(t, 2)))
                dve.tensor_tensor(x1[:, t[1] % 2, :], p_misc[:, 0:D], xb[:, :], ALU.add).then_inc(x1_ready, 1)

            def stats2(t):
                dve.wait_ge(x1_ready, done(t))
                stats(x1[:, t[1] % 2, :], st2, mv2, ve2, st2_ready, mv2_ready, ve2_ready, t)

            def norm2(t):
                dve.wait_ge(rstd2_ready, done(t))
                dve.wait_ge(h2a_ready, done(back(t, 1)))
                dve.tensor_scalar(h2n[:, :], x1[:, t[1] % 2, :], mv2[:, 0:1], rstd2[:, :], ALU.subtract, ALU.mult)\
                   .then_inc(h2n_ready, 1)

            def stats3(t):
                dve.wait_ge(h2_ready, done(t))
                stats(h2[:, :], st3, mv3, ve3, st3_ready, mv3_ready, ve3_ready, t)

            def norm3(t):
                dve.wait_ge(rstd3_ready, done(t))
                dve.wait_ge(ya_ready, done(back(t, 1)))
                dve.tensor_scalar(h3[:, :], h2[:, :], mv3[:, 0:1], rstd3[:, :], ALU.subtract, ALU.mult)\
                   .then_inc(h3_ready, 1)

            def slot(t, stages):
                a, m, c, d = back(t, -1), back(t, 1), back(t, 2), back(t, 3)
                A, T, C = "A" in stages, "T" in stages, "C" in stages
                if A:
                    stats1(a)
                stats2(d)
                if A:
                    maxima(t, 0)
                    norm1(a)
                if T:
                    shift(m)
                if A:
                    maxima(t, 1)
                norm2(d)
                if A:
                    lat_shift(t)
                    maxima(t, 2)
                if C:
                    gate_in(c)
                if A:
                    maxima(t, 3)
                    pool_tokens(a)
                    copy_qk(a)
                    maxima(t, 4)
                    lat_norm(t)
                if C:
                    gate_mix(c)
                stats3(d)
                if A:
                    maxima(t, 5)
                    copy_lat(a)
                    copy_v(a)
                norm3(d)
                if A:
                    maxima(t, 6)
                if C:
                    first_residual(c)
                if A:
                    maxima(t, 7)
                    k_stack(a, 0)
                    k_stack(a, 1)

            first = (0, 0)
            dve.wait_ge(loaded_x0, 16)
            stats1(first)
            norm1(first)
            pool_tokens(first)
            copy_qk(first)
            copy_lat(first)
            copy_v(first)
            k_stack(first, 0)
            k_stack(first, 1)
            dve.wait_ge(loaded_x, 16)
            run(dve, slot)


def constants():
    import numpy as np

    c = np.zeros((P, C_END), np.float32)
    i, j = np.arange(P)[:, None], np.arange(P)[None, :]
    c[:, C_ID:C_ID + P] = i == j
    seen_before = (j >= i) & ((i > 0) | (j > 0))
    c[:, C_SM:C_SM + P] = np.where(seen_before, 0, BIG)
    c[:, C_SM + P:C_SM + 2 * P] = np.where(j < i, 0, BIG)
    c[:, C_SM0:C_SM0 + P] = np.where((j < i) | ((i == 0) & (j == 0)), 0, BIG)
    hd = LD // LH
    for n in range(NB):
        t = c[:, C_BD + n * LH * LT:C_BD + (n + 1) * LH * LT].reshape(P, LH, LT)
        for h in range(LH):
            t[h * hd:(h + 1) * hd, h, :] = 1
        for q in range(CPB):
            t[LD + q, :, n * CPB + q:] = BIG
    c[:, C_BD:C_BD + NB * LH * LT] = np.concatenate(
        [c[:, C_BD + n * LH * LT:C_BD + (n + 1) * LH * LT] for n in range(NB)], 1)
    for g in range(2):
        for u in range(2):
            h = 2 * g + u
            c[u * LT:(u + 1) * LT, C_RV + g * LD + h * hd:C_RV + g * LD + (h + 1) * hd] = 1
    for q in range(CPB):
        c[LD + q, C_IND + q * CH:C_IND + (q + 1) * CH] = 1
    for h in range(H):
        c[KS + h, C_SEL + h] = 1
    c[CH:, C_VAL] = 1
    c[LD:LD + CPB, C_BRK] = 1
    return c


def kernel(**inputs):
    import numpy as np
    import concourse.bacc as bacc
    from concourse.bass_utils import run_bass_kernel_spmd

    a = {k: np.ascontiguousarray(v) for k, v in inputs.items()}
    rows = np.concatenate([a["L0_attn_qkv_b"], a["L0_attn_rkv_b"][LD:], a["L0_ffn_ln_g"], a["L0_ffn_ln_b"],
                           a["L0_attn_out_b"], a["L0_attn_gl_w"][:, 0], a["L0_attn_gr_w"][:, 0]])
    arrays = {
        "x": a["L0_attn_x"].reshape(NT, P, D),
        "qkv_w": a["L0_attn_qkv_w"],
        "rq_w": a["L0_attn_rq_w"],
        "rq_b": a["L0_attn_rq_b"].reshape(LD, 1),
        "rkv_w": a["L0_attn_rkv_w"],
        "rk_b": np.ascontiguousarray(a["L0_attn_rkv_b"][:LD].reshape(LD, 1)),
        "rout_w": a["L0_attn_rout_w"],
        "rout_b": a["L0_attn_rout_b"].reshape(1, D),
        "out_w": a["L0_attn_out_w"],
        "c_t": np.ascontiguousarray(a["L0_c"].T.reshape(KC, P, B).transpose(1, 0, 2)),
        "wmod": a["L0_wmod"],
        "rows": rows,
        "consts": constants(),
    }
    nc = bacc.Bacc("TRN2", target_bir_lowering=False, num_devices=1)
    args = [nc.dram_tensor(f"in_{k}", v.shape, mybir.dt.from_np(v.dtype), kind="ExternalInput").ap()
            for k, v in arrays.items()]
    out = nc.dram_tensor("out_y", (NT, P, D), F32, kind="ExternalOutput").ap()
    build(nc, *args, out)
    r = run_bass_kernel_spmd(nc, [{f"in_{k}": v for k, v in arrays.items()}], core_ids=[0])
    return r.results[0]["out_y"].reshape(B, S, D)
```

```python
from contextlib import ExitStack

import concourse.bass as bass
from concourse import mybir

F32 = mybir.dt.float32
BF16 = mybir.dt.bfloat16
ALU = mybir.AluOpType
ACT = mybir.ActivationFunctionType
AX_X = mybir.AxisListType.X

B, S, D = 4, 1024, 256
P = 128
KC = D // P
H, HD = 16, 16
NB = S // P
NT = B * NB
LH, LT, LD = 4, 64, 64
CH = S // LT
CPB = P // CH
VC = HD + 2
NTERM = 6
KS = NTERM * HD
NP = H // 2
NG = H // 4
RING = 4
EPS = 1e-5
BIG = -1.0e9
Q_SLOTS = {1: (2, 5, 1), 2: (1, 6, 4), 3: (0, 1, 1)}
K_SLOTS = {1: (0, 3, 1), 2: (3, 6, 2), 3: (4, 5, 1)}

BASE = 6
Y_BASE = 3

SU_SILU, SU_MODT, SU_PRE, SU_GA, SU_BATCH = 4, 6, 30, 9, 17
SU_ALL = SU_PRE + B * SU_BATCH + 3 + RING
SU_POOL = 22

C_ID, C_SM, C_SM0, C_BD, C_RV = 0, P, P + 2 * P, P + 3 * P, P + 3 * P + NB * LH * LT
C_IND = C_RV + 2 * LD
C_SEL = C_IND + P
C_VAL = C_SEL + H
C_BRK = C_VAL + 1
C_END = C_BRK + 1

R_QK, R_V, R_RV = 0, 2 * D, 3 * D
R_G, R_B, R_O = R_RV + LD, R_RV + LD + D, R_RV + LD + 2 * D
R_GL, R_GR = R_O + D, R_O + D + HD
R_END = R_GR + HD


def build(nc, x, qkv_w, rq_w, rq_b, rkv_w, rk_b, rout_w, rout_b, out_w, c_t, wmod, rows, consts, out):
    ctx = ExitStack()
    with ctx:
        def sb(name, shape, dt=F32):
            return ctx.enter_context(nc.sbuf_tensor(name, shape, dt))

        def bank(name):
            return ctx.enter_context(nc.psum_tensor(name, [P, 512], F32))

        started = {"PE": [], "DVE": [], "ACT": [], "POOL": []}

        def sem(name):
            return ctx.enter_context(nc.semaphore(name))

        def counted(name, engine, dummies=0):
            s = sem(name)
            started[engine].append((s, BASE - dummies))
            return s

        XPAD = 3
        x_all = sb("x_all", [P, (XPAD + NT + 2) * D])
        cst = sb("cst", [P, C_END])
        row = sb("row", [P, R_END])
        ident = cst[:, C_ID:C_ID + P]
        ident_bf = sb("ident_bf", [P, P], BF16)
        smask = cst[:, C_SM:C_SM + 2 * P]
        smask0 = cst[:, C_SM0:C_SM0 + P]
        wqk = sb("wqk", [P, KC, 2 * D])
        wv = sb("wv", [P, KC, H, HD + 1])
        bv = sb("bv", [P, H, HD + 1])
        wrq = sb("wrq", [P, KC, P])
        wrk = sb("wrk", [P, KC, P])
        wrv = sb("wrv", [P, KC, LD])
        brq = sb("brq", [LD, 1])
        brk = sb("brk", [P, 1])
        wro = sb("wro", [P, D + H])
        wo = sb("wo", [P, (B + 1) * KC * D])
        obg = sb("obg", [P, (B + 1) * D])
        c1 = sb("c1", [P, (B + 1) * D])
        s1 = sb("s1", [P, (B + 1) * D])
        g3 = sb("g3", [P, (B + 1) * D])
        b3 = sb("b3", [P, (B + 1) * D])
        mod_t = sb("mod_t", [P, (B + 1) * 8])
        ct = sb("ct", [P, KC, B])
        cs = sb("cs", [P, KC, B])
        cbc = sb("cbc", [P, KC, B, P])
        st = sb("st", [P, 6])
        mv = sb("mv", [P, 2])
        rstd = sb("rstd", [P, 1])
        ve1, ve2, ve3 = sb("ve1", [P, 1]), sb("ve2", [P, 1]), sb("ve3", [P, 1])
        half = sb("half", [P, 1])
        xn = sb("xn", [P, 2, D])
        hT = sb("hT", [P, 2, KC, P])
        pooled = sb("pooled", [P, KC, 2, LT])
        qkf = sb("qkf", [P, 2 * D])
        res = sb("res", [P, 2 * D])
        qtok = sb("qtok", [P, H, KS], BF16)
        ktok = sb("ktok", [P, H, KS], BF16)
        qst = sb("qst", [P, RING, H, P], BF16)
        kst = sb("kst", [P, RING, H, P], BF16)
        vp = sb("vp", [P, RING, H, VC])
        rqT = sb("rqT", [P, 2, P])
        bd = sb("bd", [P, 2, LH, LT])
        rvb = sb("rvb", [P, LD])
        bvd = sb("bvd", [P, 2, 2, P])
        mx = sb("mx", [P, H])
        mtok = sb("mtok", [P, P], BF16)
        junk = sb("junk", [P, 4, 2 * P], BF16)
        pr = sb("pr", [P, H, 2, P])
        oT = sb("oT", [P, 4 * P])
        lmx = sb("lmx", [P, LH])
        ls = sb("ls", [P, LH, LT])
        le = sb("le", [P, LH, LT])
        lsum = sb("lsum", [P, LH])
        lrec = sb("lrec", [P, LH])
        lrec2 = sb("lrec2", [P, LH])
        lp = sb("lp", [P, LH * LT])
        lpT = sb("lpT", [P, 2 * P])
        loT = sb("loT", [P, P])
        rem = sb("rem", [P, RING, D + H])
        ssum = sb("ssum", [P, H])
        srec = sb("srec", [P, H])
        local = sb("local", [P, H, HD])
        zl = sb("zl", [P, H])
        z = sb("z", [P, H])
        ez = sb("ez", [P, H])
        g1 = sb("g1", [P, H])
        gate = sb("gate", [P, H])
        dif = sb("dif", [P, D])
        dg = sb("dg", [P, D])
        mix = sb("mix", [P, D])
        mixT = sb("mixT", [P, D])
        xb = sb("xb", [P, D])
        x1 = sb("x1", [P, 2, D])
        st2 = sb("st2", [P, 6])
        mv2 = sb("mv2", [P, 2])
        rstd2 = sb("rstd2", [P, 1])
        h2n = sb("h2n", [P, D])
        h2a = sb("h2a", [P, D])
        h2 = sb("h2", [P, D])
        st3 = sb("st3", [P, 6])
        mv3 = sb("mv3", [P, 2])
        rstd3 = sb("rstd3", [P, 1])
        h3 = sb("h3", [P, D])
        ux = sb("ux", [P, D])
        ya = sb("ya", [P, D])
        y = sb("y", [P, 2, D])
        wm = pr[:, 0:12, :, :].rearrange("p h a n -> p (h a n)").rearrange("p (k n) -> p k n", k=KC)
        gt = pr[:, 12:16, :, :].rearrange("p h a n -> p (h a n)")
        tmp = kst[:, :, :, :].rearrange("p r h n -> p (r h n)").bitcast(F32)[:, 0:2 * KC * D]

        p_a, p_qkv, p_misc = bank("p_a"), bank("p_qkv"), bank("p_misc")
        p_x = [bank("p_x0"), bank("p_x1")]
        p_y = [bank("p_y0"), bank("p_y1")]
        p_pv = bank("p_pv")

        loaded_c, loaded_w, loaded_x0, loaded_x = sem("loaded_c"), sem("loaded_w"), sem("loaded_x0"), sem("loaded_x")
        y_stored = [sem("y_stored0"), sem("y_stored1")]
        su_dve, su_act, su_pe, su_pool = sem("setup_dve"), sem("setup_act"), sem("setup_pe"), sem("setup_pool")

        st1_ready, mv1_ready, ve1_ready = (counted(n, "DVE") for n in ("st1_ready", "mv1_ready", "ve1_ready"))
        rstd1_ready = counted("rstd1_ready", "POOL")
        xn_ready = counted("xn_ready", "DVE")
        hT_psum, hT_ready = counted("hT_psum", "PE"), counted("hT_ready", "ACT")
        pooled_once, pooled_ready = counted("pooled_once", "DVE"), counted("pooled_ready", "DVE")
        qk_psum, qk_copied = counted("qk_psum", "PE"), counted("qk_copied", "DVE")
        v_psum, v_copied = counted("v_psum", "PE"), counted("v_copied", "DVE")
        rqT_ready = counted("rqT_ready", "DVE")
        lat_psum, lat_copied, rvb_ready, bvd_ready = (counted("lat_psum", "PE"), counted("lat_copied", "DVE"),
                                                      counted("rvb_ready", "DVE"), counted("bvd_ready", "DVE"))
        part1_ready, res_ready = counted("part1_ready", "ACT"), counted("res_ready", "POOL")
        part2_ready, part3_ready = counted("part2_ready", "ACT"), counted("part3_ready", "POOL")
        stack_psum = [counted(f"stack_psum{u}", "PE") for u in range(4)]
        stack_copied = [counted(f"stack_copied{u}", "DVE" if u % 2 else "ACT") for u in range(4)]
        s_psum = [counted(f"s_psum{i}", "PE") for i in range(NP)]
        s_max = [counted(f"s_max{i}", "DVE") for i in range(NP)]
        m_ready = counted("m_ready", "DVE")
        mT_psum, shift_ready = counted("mT_psum", "PE", 1), counted("shift_ready", "DVE", 1)
        st_psum = [counted(f"st_psum{i}", "PE", 1) for i in range(NP)]
        exp_done = [counted(f"exp_done{i}", "ACT", 1) for i in range(NP)]
        masked = [counted(f"masked{g}", "POOL", 1) for g in range(NG)]
        pv_psum = [counted(f"pv_psum{g}", "PE", 1) for g in range(NG)]
        ls_psum, lmx_ready, ls_ready, lexp_ready = (counted("ls_psum", "PE"), counted("lmx_ready", "DVE"),
                                                    counted("ls_ready", "DVE"), counted("lexp_ready", "ACT"))
        lsum_ready, lrec_ready, lval_ready, lp_ready = (counted(n, "DVE") for n in
                                                        ("lsum_ready", "lrec_ready", "lval_ready", "lp_ready"))
        lpT_psum, lpT_ready = counted("lpT_psum", "PE"), counted("lpT_ready", "ACT")
        loT_psum, loT_ready = counted("loT_psum", "PE"), counted("loT_ready", "ACT")
        rem_psum, rem_ready = counted("rem_psum", "PE"), counted("rem_ready", "ACT")
        oT_ready = counted("oT_ready", "ACT", 2)
        o_psum = counted("o_psum", "PE", 2)
        ssum_ready, srec_ready, zl_ready, local_ready, z_ready = (
            counted(n, "DVE", 2) for n in ("ssum_ready", "srec_ready", "zl_ready", "local_ready", "z_ready"))
        ez_ready = counted("ez_ready", "ACT", 2)
        g1_ready, gate_ready, dif_ready, dg_ready, mix_ready = (
            counted(n, "DVE", 2) for n in ("g1_ready", "gate_ready", "dif_ready", "dg_ready", "mix_ready"))
        mixT_psum, mixT_ready = counted("mixT_psum", "PE", 2), counted("mixT_ready", "ACT", 2)
        xb_ready = counted("xb_ready", "POOL", 2)
        out_psum, x1_ready = counted("out_psum", "PE", 2), counted("x1_ready", "DVE", 2)
        st2_ready, mv2_ready, ve2_ready, h2n_ready = (
            counted(n, "DVE", 3) for n in ("st2_ready", "mv2_ready", "ve2_ready", "h2n_ready"))
        rstd2_ready, rstd3_ready = counted("rstd2_ready", "POOL", 3), counted("rstd3_ready", "POOL", 3)
        ux_ready, h2a_ready, h2_ready = (counted(n, "POOL", 3) for n in ("ux_ready", "h2a_ready", "h2_ready"))
        st3_ready, mv3_ready, ve3_ready, h3_ready = (
            counted(n, "DVE", 3) for n in ("st3_ready", "mv3_ready", "ve3_ready", "h3_ready"))
        ya_ready, y_ready = counted("ya_ready", "POOL", 3), counted("y_ready", "POOL", 3)

        def done(t):
            return t[0] + (t[1] + 1 + BASE)

        def back(t, k):
            return (t[0], t[1] - k)

        def batch(t):
            return t[0] + 8 * (t[1] // NB) + 8

        def x_of(t):
            return x_all[:, bass.ds((t[0] + (t[1] + XPAD)) * D, D)]

        def per_batch(tile, t, width=D):
            return tile[:, bass.ds(batch(t) * (width // NB), width)]

        def heads(ap, k=HD):
            return ap.rearrange("p (h k) -> p h k", k=k)

        def bc(ap, n):
            return ap.unsqueeze(2).to_broadcast([ap.shape[0], ap.shape[1], n])

        def slots(tok, rule):
            a, e, s = rule
            return tok[:, :, :].rearrange("p h (s k) -> p h s k", k=HD)[:, :, a:e:s, :]

        def rep(ap, rule):
            a, e, s = rule
            n = len(range(a, e, s))
            return heads(ap).unsqueeze(2).to_broadcast([P, H, n, HD])

        block = ctx.enter_context(nc.Block())

        def wait_apart(eng, *waits):
            values = [v if isinstance(v, int) else eng.snap(eng.to_reg(v)) for _, v in waits]
            eng.wait_ge(su_act, 1)
            for (s, _), v in zip(waits, values):
                eng.wait_ge(s, v)

        def run(eng, slot):
            slot((0, -2), "A")
            slot((0, -1), "AK")
            with eng.Fori(0, NT - NB + 1, NB) as i:
                for n in range(NB):
                    slot((i, n), "AKSTCD")
            slot((NT, 0), "TCD")
            slot((NT, 1), "CD")
            slot((NT, 2), "D")

        def stored(t):
            return t[0] * 8 + 16 * (t[1] // 2 + 1 + Y_BASE)

        @block.sync
        def _(sp):
            for p in range(2):
                sp.sem_inc(y_stored[p], 16 * Y_BASE)
            sp.dma_start(ct[:, :, :], c_t).then_inc(loaded_c, 16)
            sp.dma_start(wm, wmod.rearrange("(k p) n -> p k n", p=P)).then_inc(loaded_c, 16)
            sp.dma_start(cst[:, :], consts).then_inc(loaded_w, 16)
            sp.dma_start(row[:, :], rows.partition_broadcast(P)).then_inc(loaded_w, 16)
            sp.dma_start(x_all[:, XPAD * D:(XPAD + NB) * D].rearrange("p (t d) -> p t d", d=D),
                         x[0:NB].rearrange("t p d -> p t d")).then_inc(loaded_x0, 16)
            sp.dma_start(x_all[:, (XPAD + NB) * D:(XPAD + NT) * D].rearrange("p (t d) -> p t d", d=D),
                         x[NB:NT].rearrange("t p d -> p t d")).then_inc(loaded_x, 16)

            def store(t):
                sp.wait_ge(y_ready, done(t))
                sp.dma_start(out[bass.ds(t[0] + t[1], 1)].rearrange("t p d -> (t p) d"),
                             y[:, t[1] % 2, :]).then_inc(y_stored[t[1] % 2], 16)

            for n in range(3, NB):
                store((0, n - 3))
            with sp.Fori(NB, NT - NB + 1, NB) as i:
                for n in range(NB):
                    store((i, n - 3))
            for n in range(3):
                store((NT, n - 3))
            for p in range(2):
                sp.wait_ge(y_stored[p], stored((NT, p - 2)))

        @block.gpsimd
        def _(pool):
            for s, v in started["POOL"]:
                pool.sem_inc(s, v)
            for t in (rqT, vp, loT, bvd, rem, pooled, wrq, wrk, wro, mtok, mod_t):
                pool.memset(t[:], 0.0).then_inc(su_pool, 1)
            pool.memset(oT[:, :], 0.0).then_inc(su_pool, 1)
            pool.memset(x_all[:, 0:XPAD * D], 0.0).then_inc(su_pool, 1)
            pool.memset(x_all[:, (XPAD + NT) * D:], 0.0).then_inc(su_pool, 1)
            for t in (obg, c1, s1, g3, b3):
                pool.memset(t[:, 0:D], 0.0).then_inc(su_pool, 1)
            pool.memset(wo[:, 0:KC * D], 0.0).then_inc(su_pool, 1)
            pool.memset(x1[:], 0.0).then_inc(su_pool, 1)
            pool.memset(half[:, :], -0.5).then_inc(su_pool, 1)
            pool.wait_ge(su_pool, SU_POOL)
            pool.wait_ge(su_dve, SU_ALL)
            pool.wait_ge(loaded_x0, 16)
            pool.wait_ge(loaded_x, 16)

            def res1(t):
                pool.wait_ge(part1_ready, done(t))
                pool.tensor_tensor(heads(res[:, 0:D]), heads(qkf[:, 0:D]), slots(qtok, Q_SLOTS[1])[:, :, 0, :], ALU.subtract)
                pool.tensor_tensor(heads(res[:, D:2 * D]), heads(qkf[:, D:2 * D]), slots(ktok, K_SLOTS[1])[:, :, 0, :],
                                   ALU.subtract).then_inc(res_ready, 1)

            def part3(t):
                pool.wait_ge(part2_ready, done(t))
                pool.tensor_tensor(slots(qtok, Q_SLOTS[3])[:, :, 0, :], heads(res[:, 0:D]),
                                   slots(qtok, Q_SLOTS[2])[:, :, 0, :], ALU.subtract)
                pool.tensor_tensor(slots(ktok, K_SLOTS[3])[:, :, 0, :], heads(res[:, D:2 * D]),
                                   slots(ktok, K_SLOTS[2])[:, :, 0, :], ALU.subtract).then_inc(part3_ready, 1)

            def mask(t, g):
                wait_apart(pool, (exp_done[2 * g + 1], done(t)))
                own = pr[:, 4 * g:4 * g + 4, 1, :]
                ins = pool.affine_select(out=own, in_=own, compare_op=ALU.is_ge, fill=0.0, base=-1,
                                         pattern=[[0, 4], [1, P]], channel_multiplier=-1)
                if t[1] % NB:
                    prev = pr[:, 4 * g:4 * g + 4, 0, :]
                    ins = pool.affine_select(out=prev, in_=prev, compare_op=ALU.is_ge, fill=0.0, base=-1,
                                             pattern=[[0, 4], [-P, P]], channel_multiplier=P + 1)
                ins.then_inc(masked[g], 1)

            def power(ve_, rstd_, s_ve, s_rstd, t):
                pool.wait_ge(s_ve, done(t))
                pool.tensor_tensor(rstd_[:, :], ve_[:, :], half[:, :], ALU.pow).then_inc(s_rstd, 1)

            def rstd1(t):
                pool.wait_ge(xn_ready, done(back(t, 1)))
                power(ve1, rstd, ve1_ready, rstd1_ready, t)

            def rstd2_of(t):
                power(ve2, rstd2, ve2_ready, rstd2_ready, t)

            def rstd3_of(t):
                power(ve3, rstd3, ve3_ready, rstd3_ready, t)

            def add_bias(t):
                wait_apart(pool, (x1_ready, done(back(t, 1))))
                pool.tensor_tensor(xb[:, :], x_of(t), per_batch(obg, t), ALU.add).then_inc(xb_ready, 1)

            def add_u(t):
                wait_apart(pool, (x1_ready, done(t)), (y_ready, done(back(t, 1))))
                pool.tensor_tensor(ux[:, :], x1[:, t[1] % 2, :], per_batch(b3, t), ALU.add).then_inc(ux_ready, 1)

            def scale2(t):
                wait_apart(pool, (h2n_ready, done(t)))
                pool.tensor_tensor(h2a[:, :], h2n[:, :], per_batch(c1, t), ALU.mult).then_inc(h2a_ready, 1)

            def shift2(t):
                wait_apart(pool, (h2a_ready, done(t)), (h3_ready, done(back(t, 1))))
                pool.tensor_tensor(h2[:, :], h2a[:, :], per_batch(s1, t), ALU.add).then_inc(h2_ready, 1)

            def scale3(t):
                wait_apart(pool, (h3_ready, done(t)))
                pool.tensor_tensor(ya[:, :], h3[:, :], per_batch(g3, t), ALU.mult).then_inc(ya_ready, 1)

            def finish(t):
                pool.wait_ge(ya_ready, done(t))
                pool.wait_ge(ux_ready, done(t))
                pool.wait_ge(y_stored[t[1] % 2], stored(back(t, 2)))
                pool.tensor_tensor(y[:, t[1] % 2, :], ya[:, :], ux[:, :], ALU.add).then_inc(y_ready, 1)

            def slot(t, stages):
                a, m, c, d = back(t, -2), back(t, 1), back(t, 2), back(t, 3)
                A, T, C, D = ("A" in stages, "T" in stages, "C" in stages, "D" in stages)
                if C:
                    add_bias(c)
                if D:
                    add_u(d)
                if A:
                    rstd1(a)
                if D:
                    rstd2_of(d)
                    scale2(d)
                    shift2(d)
                if T:
                    mask(m, 0)
                    mask(m, 1)
                    mask(m, 2)
                if D:
                    rstd3_of(d)
                if A:
                    res1(a)
                if T:
                    mask(m, 3)
                if D:
                    scale3(d)
                if A:
                    part3(a)
                if D:
                    finish(d)

            run(pool, slot)

        @block.scalar
        def _(act):
            act.dma_start(wqk[:, :, :], qkv_w[:, 0:2 * D].rearrange("(k p) n -> p k n", p=P)).then_inc(loaded_w, 16)
            act.dma_start(tmp[:, 0:KC * D].rearrange("p (k n) -> p k n", k=KC),
                          qkv_w[:, 2 * D:3 * D].rearrange("(k p) n -> p k n", p=P)).then_inc(loaded_w, 16)
            act.dma_start(tmp[:, KC * D:2 * KC * D].rearrange("p (k n) -> p k n", k=KC),
                          out_w.rearrange("(k p) n -> p k n", p=P)).then_inc(loaded_w, 16)
            act.wait_ge(su_pool, SU_POOL)
            act.dma_start(wrq[:, :, 0:LD], rq_w.rearrange("(k p) n -> p k n", p=P)).then_inc(loaded_w, 16)
            act.dma_start(wrk[:, :, 0:LD], rkv_w[:, 0:LD].rearrange("(k p) n -> p k n", p=P)).then_inc(loaded_w, 16)
            act.dma_start(wrv[:, :, :], rkv_w[:, LD:2 * LD].rearrange("(k p) n -> p k n", p=P)).then_inc(loaded_w, 16)
            act.dma_start(wro[0:LD, 0:D], rout_w).then_inc(loaded_w, 16)
            act.dma_start(wro[LD:LD + 1, 0:D], rout_b).then_inc(loaded_w, 16)
            act.dma_start(brq[:, :], rq_b).then_inc(loaded_w, 16)
            act.dma_start(brk[0:LD, :], rk_b).then_inc(loaded_w, 16)
            for s, v in started["ACT"]:
                act.sem_inc(s, v)
            act.wait_ge(loaded_c, 32)
            act.activation(cs[:, :, :], ct[:, :, :], ACT.Exp, scale=-1.0).then_inc(su_act, 1)

            def modulated(t):
                wait_apart(act, (hT_psum, done(t)), (v_psum, done(back(t, 2))), (lat_psum, done(back(t, 2))))
                for k in range(KC):
                    ins = act.activation(hT[:, t[1] % 2, k, :], p_a[:, k * P:(k + 1) * P], ACT.Identity,
                                         scale=mod_t[:, bass.ds(batch(t) + (k - 8), 1)],
                                         bias=mod_t[:, bass.ds(batch(t) + (k + KC - 8), 1)])
                ins.then_inc(hT_ready, 1)

            def part1(t):
                act.wait_ge(qk_copied, done(t))
                act.wait_ge(stack_psum[3], done(back(t, 1)))
                act.activation(slots(qtok, Q_SLOTS[1]), rep(qkf[:, 0:D], Q_SLOTS[1]), ACT.Copy)
                act.activation(slots(ktok, K_SLOTS[1]), rep(qkf[:, D:2 * D], K_SLOTS[1]), ACT.Copy).then_inc(part1_ready, 1)

            def part2(t):
                act.wait_ge(res_ready, done(t))
                act.activation(slots(qtok, Q_SLOTS[2]), rep(res[:, 0:D], Q_SLOTS[2]), ACT.Copy)
                act.activation(slots(ktok, K_SLOTS[2]), rep(res[:, D:2 * D], K_SLOTS[2]), ACT.Copy).then_inc(part2_ready, 1)

            def stack_act(t, u):
                act.wait_ge(stack_psum[u], done(t))
                act.wait_ge(st_psum[NP - 1], done(back(t, 3)))
                act.activation((qst, kst)[u // 2][0:KS, t[1] % RING, 0:8, :].rearrange("p h n -> p (h n)"),
                               p_x[0][0:KS, :].bitcast(BF16), ACT.Copy).then_inc(stack_copied[u], 1)

            def exps(t, i):
                act.wait_ge(st_psum[i], done(t))
                act.wait_ge(pv_psum[i // 2], done(back(t, 1)))
                src = p_y[i % 2][:, :].rearrange("p (h a n) -> p h a n", h=2, a=2)
                if t[1] % NB:
                    act.activation(pr[:, 2 * i:2 * i + 2, :, :], src, ACT.Exp).then_inc(exp_done[i], 1)
                else:
                    act.activation(pr[:, 2 * i:2 * i + 2, 1, :], src[:, :, 1, :], ACT.Exp).then_inc(exp_done[i], 1)

            def out_t(t):
                act.wait_ge(pv_psum[NG - 1], done(t))
                act.wait_ge(o_psum, done(back(t, 1)))
                act.activation(oT[:, :], p_pv[:, :], ACT.Copy).then_inc(oT_ready, 1)

            def lat_exp(t):
                act.wait_ge(ls_ready, done(t))
                act.wait_ge(lp_ready, done(back(t, 1)))
                act.activation(le[:, :, :], ls[:, :, :], ACT.Exp).then_inc(lexp_ready, 1)

            def lat_pT(t):
                act.wait_ge(lpT_psum, done(t))
                act.wait_ge(loT_psum, done(back(t, 1)))
                act.activation(lpT[:, :], p_a[:, 0:2 * P], ACT.Copy).then_inc(lpT_ready, 1)

            def lat_oT(t):
                act.wait_ge(loT_psum, done(t))
                act.wait_ge(rem_psum, done(back(t, 1)))
                act.activation(loT[0:LD, :], p_misc[0:LD, 0:P], ACT.Copy).then_inc(loT_ready, 1)

            def remote(t):
                act.wait_ge(rem_psum, done(t))
                act.wait_ge(mix_ready, done(back(t, RING)))
                act.activation(rem[:, t[1] % RING, :], p_misc[:, 0:D + H], ACT.Copy).then_inc(rem_ready, 1)

            def gate_exp(t):
                act.wait_ge(z_ready, done(t))
                act.wait_ge(g1_ready, done(back(t, 1)))
                act.activation(ez[:, :], z[:, :], ACT.Exp, scale=-1.0).then_inc(ez_ready, 1)

            def mixed_t(t):
                act.wait_ge(mixT_psum, done(t))
                act.wait_ge(out_psum, done(back(t, 1)))
                act.activation(mixT[:, :], p_misc[:, 0:D], ACT.Copy).then_inc(mixT_ready, 1)

            def slot(t, stages):
                a, k, m, c = back(t, -2), back(t, -1), back(t, 1), back(t, 2)
                A, K, S, T, C = ("A" in stages, "K" in stages, "S" in stages, "T" in stages, "C" in stages)
                if C:
                    out_t(c)
                if S:
                    lat_exp(t)
                if K:
                    stack_act(k, 0)
                if T:
                    exps(m, 0)
                    exps(m, 1)
                    exps(m, 2)
                if A:
                    modulated(a)
                if T:
                    exps(m, 3)
                    exps(m, 4)
                if C:
                    gate_exp(c)
                if K:
                    stack_act(k, 2)
                if S:
                    lat_pT(t)
                if T:
                    exps(m, 5)
                if S:
                    lat_oT(t)
                if A:
                    part1(a)
                if S:
                    remote(t)
                if T:
                    exps(m, 6)
                    exps(m, 7)
                if C:
                    mixed_t(c)
                if A:
                    part2(a)

            act.wait_ge(su_dve, SU_MODT)
            run(act, slot)

        @block.tensor
        def _(pe):
            for s, v in started["PE"]:
                pe.sem_inc(s, v)
            pe.wait_ge(su_dve, SU_SILU)
            pe.wait_ge(loaded_c, 32)
            for j in range(2 * KC):
                for k in range(KC):
                    ins = pe.matmul(p_a[:, j * B:(j + 1) * B], wm[:, k, j * P:(j + 1) * P], cs[:, k, :],
                                    start=(k == 0), stop=(k == KC - 1))
            ins.then_inc(su_pe, 1)
            for b in range(B):
                for j in range(2):
                    if b:
                        pe.wait_ge(su_dve, SU_PRE + SU_BATCH * (b - 1) + (SU_GA, SU_BATCH)[j])
                    for k in range(KC):
                        ins = pe.matmul(p_y[j][:, :], cbc[:, k, b, :], wm[:, k, 2 * D + j * 512:2 * D + (j + 1) * 512],
                                        start=(k == 0), stop=(k == KC - 1))
                    ins.then_inc(su_pe, 1)
            pe.wait_ge(su_dve, SU_ALL)

            def ln_t(t):
                pe.wait_ge(xn_ready, done(t))
                pe.wait_ge(rqT_ready, done(back(t, 1)))
                pe.wait_ge(lat_copied, done(back(t, 1)))
                pe.wait_ge(rvb_ready, done(back(t, 1)))
                for k in range(KC):
                    ins = pe.transpose(p_a[:, k * P:(k + 1) * P], xn[:, t[1] % 2, k * P:(k + 1) * P], ident)
                ins.then_inc(hT_psum, 1)

            def project_qk(t):
                pe.wait_ge(hT_ready, done(t))
                pe.wait_ge(v_copied, done(back(t, 1)))
                for k in range(KC):
                    ins = pe.matmul(p_qkv[:, :], hT[:, t[1] % 2, k, :], wqk[:, k, :], start=(k == 0), stop=(k == KC - 1))
                ins.then_inc(qk_psum, 1)

            def project_v(t):
                pe.wait_ge(hT_ready, done(t))
                pe.wait_ge(qk_copied, done(t))
                for k in range(KC):
                    ins = pe.matmul(p_qkv[:, 0:H * (HD + 1)], hT[:, t[1] % 2, k, :],
                                    wv[:, k, :, :].rearrange("p h k -> p (h k)"), start=(k == 0), stop=(k == KC - 1))
                ins.then_inc(v_psum, 1)

            def project_lat(t):
                pe.wait_ge(pooled_ready, done(t))
                pe.wait_ge(ls_ready, done(back(t, 1)))
                if t[1] < 1 and isinstance(t[0], int):
                    pe.wait_ge(hT_ready, done(t))
                for k in range(KC):
                    pe.matmul(p_a[:, 0:P], wrq[:, k, :], hT[:, t[1] % 2, k, :], start=(k == 0), stop=(k == KC - 1))
                for k in range(KC):
                    pe.matmul(p_a[:, 2 * P:2 * P + LT], wrk[:, k, :], pooled[:, k, 0, :], start=(k == 0), stop=(k == KC - 1))
                for k in range(KC):
                    ins = pe.matmul(p_a[:, 3 * P:3 * P + LD], pooled[:, k, :, :].rearrange("p a l -> p (a l)"), wrv[:, k, :], start=(k == 0), stop=(k == KC - 1))
                ins.then_inc(lat_psum, 1)

            def stack(t, u):
                pe.wait_ge(part3_ready, done(t))
                if u == 0:
                    pe.wait_ge(s_max[6], done(back(t, 2)))
                elif u == 1:
                    pe.wait_ge(s_max[7], done(back(t, 2)))
                elif u == 2:
                    pe.wait_ge(stack_copied[0], done(t))
                elif u == 3:
                    pe.wait_ge(stack_copied[1], done(t))
                src = (qtok, ktok)[u // 2]
                dst = p_x[u % 2][0:KS, :].bitcast(BF16)
                for j in range(8):
                    ins = pe.transpose(dst[:, j * P:(j + 1) * P], src[:, 8 * (u % 2) + j, :], ident_bf[:, :])
                ins.then_inc(stack_psum[u], 1)

            def scores(t, i):
                if i == 0:
                    for u in range(4):
                        pe.wait_ge(stack_copied[u], done(t))
                if i == 0:
                    pe.wait_ge(stack_copied[2], done(back(t, -1)))
                elif i == 1:
                    pe.wait_ge(stack_copied[3], done(back(t, -1)))
                else:
                    pe.wait_ge(s_max[i - 2], done(t))
                n = t[1]
                for h in (2 * i, 2 * i + 1):
                    at = (h % 2) * 2 * P
                    q = qst[0:KS, n % RING, h, :]
                    if n % NB:
                        pe.matmul(p_x[i % 2][:, at:at + P], q, kst[0:KS, (n - 1) % RING, h, :], start=True, stop=True)
                    ins = pe.matmul(p_x[i % 2][:, at + P:at + 2 * P], q, kst[0:KS, n % RING, h, :], start=True, stop=True)
                ins.then_inc(s_psum[i], 1)

            def max_t(t):
                pe.wait_ge(m_ready, done(t))
                pe.wait_ge(oT_ready, done(back(t, 1)))
                pe.transpose(p_pv[:, 0:P // 2].bitcast(BF16), mtok[:, :], ident_bf[:, :]).then_inc(mT_psum, 1)

            def scores_t(t, i):
                pe.wait_ge(shift_ready, done(t))
                pe.wait_ge(exp_done[(i - 2) % NP], done(t if i >= 2 else back(t, 1)))
                n = t[1]
                for h in (2 * i, 2 * i + 1):
                    at = (h % 2) * 2 * P
                    q = qst[0:KS + H, n % RING, h, :]
                    if n % NB:
                        pe.matmul(p_y[i % 2][:, at:at + P], kst[0:KS + H, (n - 1) % RING, h, :], q, start=True, stop=True)
                    ins = pe.matmul(p_y[i % 2][:, at + P:at + 2 * P], kst[0:KS + H, n % RING, h, :], q, start=True, stop=True)
                ins.then_inc(st_psum[i], 1)

            def sum_v(t, g):
                pe.wait_ge(masked[g], done(t))
                n = t[1]
                for a in range(0 if n % NB else 1, 2):
                    for j in range(4):
                        h = 4 * g + j
                        ins = pe.matmul(p_pv[32 * j:32 * j + VC, g * P:(g + 1) * P], vp[:, (n - 1 + a) % RING, h, :],
                                        pr[:, h, a, :], start=(a == 0 or n % NB == 0), stop=(a == 1),
                                        tile_position=(0, 32 * j))
                ins.then_inc(pv_psum[g], 1)

            def lat_scores(t):
                pe.wait_ge(rqT_ready, done(t))
                pe.wait_ge(lat_copied, done(t))
                pe.wait_ge(lpT_ready, done(back(t, 1)))
                pe.matmul(p_a[:, 0:LH * LT], rqT[:, t[1] % 2, :], bd[:, t[1] % 2, :, :].rearrange("p h l -> p (h l)"),
                          start=True, stop=True).then_inc(ls_psum, 1)

            def lat_p_t(t):
                pe.wait_ge(lp_ready, done(t))
                pe.wait_ge(hT_ready, done(back(t, -2)))
                for k in range(2):
                    ins = pe.transpose(p_a[:, k * P:(k + 1) * P], lp[:, k * P:(k + 1) * P], ident)
                ins.then_inc(lpT_psum, 1)

            def lat_out_t(t):
                pe.wait_ge(lpT_ready, done(t))
                pe.wait_ge(bvd_ready, done(t))
                pe.wait_ge(zl_ready, done(back(t, 2)))
                pe.wait_ge(local_ready, done(back(t, 2)))
                for k in range(2):
                    ins = pe.matmul(p_misc[:, 0:P], bvd[:, t[1] % 2, k, :], lpT[:, k * P:(k + 1) * P],
                                    start=(k == 0), stop=(k == 1))
                ins.then_inc(loT_psum, 1)

            def lat_remote(t):
                pe.wait_ge(loT_ready, done(t))
                pe.wait_ge(loT_ready, done(t))
                pe.matmul(p_misc[:, 0:D + H], loT[:, :], wro[:, :], start=True, stop=True).then_inc(rem_psum, 1)

            def out_tokens(t):
                pe.wait_ge(oT_ready, done(t))
                pe.wait_ge(x1_ready, done(back(t, 1)))
                pe.wait_ge(x1_ready, done(back(t, 1)))
                for g in range(4):
                    ins = pe.transpose(p_misc[:, g * P:(g + 1) * P], oT[:, g * P:(g + 1) * P], ident)
                ins.then_inc(o_psum, 1)

            def mixed_t(t):
                pe.wait_ge(mix_ready, done(t))
                pe.wait_ge(rem_ready, at_most_last(back(t, -2)))
                for k in range(KC):
                    ins = pe.transpose(p_misc[:, k * P:(k + 1) * P], mix[:, k * P:(k + 1) * P], ident)
                ins.then_inc(mixT_psum, 1)

            def project_out(t):
                pe.wait_ge(mixT_ready, done(t))
                pe.wait_ge(mixT_ready, done(t))
                for k in range(KC):
                    ins = pe.matmul(p_misc[:, 0:D], mixT[:, k * P:(k + 1) * P],
                                    wo[:, bass.ds(batch(t) * (KC * D // NB) + k * D, D)],
                                    start=(k == 0), stop=(k == KC - 1))
                ins.then_inc(out_psum, 1)

            def at_most_last(t):
                return done(t) if not isinstance(t[0], int) else min(done(t), done((NT, -1)))

            def slot(t, stages):
                a, k, m, c = back(t, -2), back(t, -1), back(t, 1), back(t, 2)
                A, K, S, T, C = ("A" in stages, "K" in stages, "S" in stages, "T" in stages, "C" in stages)
                if S:
                    lat_scores(t)
                if K:
                    project_v(k)
                if T:
                    max_t(m)
                if K:
                    stack(k, 0)
                    project_lat(k)
                if T:
                    scores_t(m, 0)
                if C:
                    out_tokens(c)
                if T:
                    scores_t(m, 1)
                if K:
                    stack(k, 1)
                if T:
                    scores_t(m, 2)
                if A:
                    ln_t(a)
                if K:
                    stack(k, 2)
                if T:
                    scores_t(m, 3)
                    scores_t(m, 4)
                if K:
                    stack(k, 3)
                if A:
                    project_qk(a)
                if S:
                    lat_p_t(t)
                if T:
                    scores_t(m, 5)
                if S:
                    scores(t, 0)
                    scores(t, 1)
                if T:
                    scores_t(m, 6)
                if S:
                    lat_out_t(t)
                if T:
                    sum_v(m, 0)
                if S:
                    scores(t, 2)
                    scores(t, 3)
                if T:
                    scores_t(m, 7)
                if S:
                    lat_remote(t)
                    scores(t, 4)
                if T:
                    sum_v(m, 1)
                if S:
                    scores(t, 5)
                if C:
                    mixed_t(c)
                if S:
                    scores(t, 6)
                if T:
                    sum_v(m, 2)
                if S:
                    scores(t, 7)
                if C:
                    project_out(c)
                if T:
                    sum_v(m, 3)

            run(pe, slot)

        @block.vector
        def _(dve):
            for s, v in started["DVE"]:
                dve.sem_inc(s, v)
            count = [0]

            def setup(ins):
                count[0] += 1
                ins.then_inc(su_dve, 1)
                dve.wait_ge(su_dve, count[0])

            dve.wait_ge(su_act, 1)
            setup(dve.tensor_scalar(cs[:, :, :], cs[:, :, :], 1.0, None, ALU.add))
            setup(dve.reciprocal(cs[:, :, :], cs[:, :, :]))
            setup(dve.tensor_tensor(cs[:, :, :], cs[:, :, :], ct[:, :, :], ALU.mult))
            setup(dve.tensor_copy(cbc[:, :, :, :], cs[:, :, :].unsqueeze(3).to_broadcast([P, KC, B, P])))
            assert count[0] == SU_SILU
            dve.wait_ge(su_pe, 1)
            mt = mod_t[:, :].rearrange("p (b j) -> p j b", j=8)
            dve.wait_ge(su_pool, SU_POOL)
            setup(dve.tensor_scalar(mt[:, 0:KC, 0:B], p_a[:, KC * B:2 * KC * B].rearrange("p (j b) -> p j b", b=B),
                                    1.0, None, ALU.add))
            setup(dve.tensor_copy(mt[:, KC:2 * KC, 0:B], p_a[:, 0:KC * B].rearrange("p (j b) -> p j b", b=B)))
            assert count[0] == SU_MODT
            dve.wait_ge(loaded_w, 16 * 12)
            setup(dve.tensor_copy(ident_bf[:, :], ident))
            setup(dve.tensor_scalar(wqk[:, :, 0:D], wqk[:, :, 0:D], HD ** -0.5, None, ALU.mult))
            setup(dve.tensor_scalar(row[:, 0:D], row[:, 0:D], HD ** -0.5, None, ALU.mult))
            setup(dve.tensor_scalar(wrq[:, :, :], wrq[:, :, :], (LD // LH) ** -0.5, None, ALU.mult))
            setup(dve.tensor_scalar(brq[:, :], brq[:, :], (LD // LH) ** -0.5, None, ALU.mult))
            setup(dve.tensor_scalar(wrk[:, :, :], wrk[:, :, :], 1.0 / CH, None, ALU.mult))
            setup(dve.tensor_scalar(wrv[:, :, :], wrv[:, :, :], 1.0 / CH, None, ALU.mult))
            glb = row[:, R_GL:R_GL + HD].unsqueeze(1).to_broadcast([P, H, HD])
            grb = row[:, R_GR:R_GR + HD].unsqueeze(1).to_broadcast([P, H, HD])
            jk = heads(junk[:, 0:2, :].rearrange("p j n -> p (j n)").bitcast(F32))
            for k in range(KC):
                w = heads(tmp[:, k * D:(k + 1) * D])
                setup(dve.tensor_copy(wv[:, k, :, 0:HD], w))
                setup(dve.tensor_tensor(jk, w, glb, ALU.mult))
                setup(dve.tensor_reduce(wv[:, k, :, HD], jk, AX_X, ALU.add))
            bvr = heads(row[:, R_V:R_V + D])
            setup(dve.tensor_copy(bv[:, :, 0:HD], bvr))
            setup(dve.tensor_tensor(jk, bvr, glb, ALU.mult))
            setup(dve.tensor_reduce(bv[:, :, HD], jk, AX_X, ALU.add))
            setup(dve.tensor_tensor(jk, heads(wro[:, 0:D]), grb, ALU.mult))
            setup(dve.tensor_reduce(wro[:, D:D + H], jk, AX_X, ALU.add))
            setup(dve.memset(vp[:, :, :, HD + 1:VC], 1.0))
            setup(dve.memset(loT[LD:LD + 1, :], 1.0))
            setup(dve.memset(p_pv[:, :], 0.0))
            for p in range(2):
                setup(dve.tensor_copy(rqT[LD:P, p, :], cst[LD:P, C_IND:C_IND + P]))
            setup(dve.tensor_copy(brk[LD:P, :], cst[LD:P, C_BRK:C_BRK + 1]))
            assert count[0] == SU_PRE, count[0]
            wo_in = tmp[:, KC * D:2 * KC * D]
            for b in range(B):
                lo, hi = (b + 1) * D, (b + 2) * D
                for j, (src, at) in enumerate(((p_y[0], 0), (p_y[1], D))):
                    dve.wait_ge(su_pe, 2 + 2 * b + j)
                    g_in, g_abs, g_sign, g_out = (gt[:, q * D:(q + 1) * D] for q in range(4))
                    setup(dve.tensor_copy(g_in, src[:, at:at + D]))
                    setup(dve.scalar_tensor_tensor(out=g_abs, in0=g_in, scalar=-1.0, in1=g_in, op0=ALU.mult, op1=ALU.max))
                    setup(dve.tensor_scalar(g_abs, g_abs, 0.25, None, ALU.max))
                    setup(dve.tensor_scalar(g_sign, g_in, 0.0, 2.0, ALU.is_ge, ALU.mult))
                    setup(dve.scalar_tensor_tensor(out=g_out, in0=g_sign, scalar=-1.0, in1=g_abs, op0=ALU.add, op1=ALU.mult))
                    if j == 0:
                        for k in range(KC):
                            setup(dve.tensor_tensor(wo[:, ((b + 1) * KC + k) * D:((b + 1) * KC + k + 1) * D],
                                                    wo_in[:, k * D:(k + 1) * D], g_out, ALU.mult))
                        setup(dve.tensor_tensor(obg[:, lo:hi], row[:, R_O:R_O + D], g_out, ALU.mult))
                        setup(dve.tensor_copy(s1[:, lo:hi], p_y[0][:, D:2 * D]))
                    else:
                        setup(dve.tensor_tensor(g3[:, lo:hi], row[:, R_G:R_G + D], g_out, ALU.mult))
                        setup(dve.tensor_tensor(b3[:, lo:hi], row[:, R_B:R_B + D], g_out, ALU.mult))
                        setup(dve.tensor_scalar(c1[:, lo:hi], p_y[1][:, 0:D], 1.0, None, ALU.add))
            setup(dve.memset(pr[:, :, :, :].rearrange("p h a n -> p (h a n)"), 0.0))
            setup(dve.memset(qst[:, :, :, :].rearrange("p r h n -> p (r h n)"), 0.0))
            setup(dve.memset(kst[:, :, :, :].rearrange("p r h n -> p (r h n)"), 0.0))
            for p in range(RING):
                setup(dve.tensor_copy(kst[KS:KS + 32, p, :, :],
                                      bc(cst[KS:KS + 32, C_SEL:C_SEL + H], P)))
            assert count[0] == SU_ALL, count[0]

            def bn1(t):
                dve.bn_stats(st[:, :], x_of(t)).then_inc(st1_ready, 1)

            def bn2(t):
                dve.wait_ge(x1_ready, done(t))
                dve.bn_stats(st2[:, :], x1[:, t[1] % 2, :]).then_inc(st2_ready, 1)

            def bn3(t):
                dve.wait_ge(h2_ready, done(t))
                dve.bn_stats(st3[:, :], h2[:, :]).then_inc(st3_ready, 1)

            def moments(s_stats, st_, mv_, s_mv, t):
                wait_apart(dve, (s_stats, done(t)))
                dve.bn_aggr(mv_[:, :], st_[:, :]).then_inc(s_mv, 1)

            def moments1(t):
                moments(st1_ready, st, mv, mv1_ready, t)

            def moments2(t):
                moments(st2_ready, st2, mv2, mv2_ready, t)

            def moments3(t):
                moments(st3_ready, st3, mv3, mv3_ready, t)

            def add_eps(s_mv, mv_, ve_, s_ve, t):
                dve.wait_ge(s_mv, done(t))
                dve.tensor_scalar(ve_[:, :], mv_[:, 1:2], EPS, None, ALU.add).then_inc(s_ve, 1)

            def add_eps1(t):
                add_eps(mv1_ready, mv, ve1, ve1_ready, t)

            def add_eps2(t):
                add_eps(mv2_ready, mv2, ve2, ve2_ready, t)

            def add_eps3(t):
                add_eps(mv3_ready, mv3, ve3, ve3_ready, t)

            def norm1(t):
                dve.wait_ge(rstd1_ready, done(t))
                dve.wait_ge(hT_psum, done(back(t, 2)))
                dve.tensor_scalar(xn[:, t[1] % 2, :], x_of(t), mv[:, 0:1], rstd[:, :], ALU.subtract, ALU.mult)\
                   .then_inc(xn_ready, 1)

            def pool_tokens(t):
                dve.wait_ge(hT_ready, done(t))
                dve.wait_ge(lat_psum, done(back(t, 1)))
                n = t[1] % NB
                new = slice(n * CPB, (n + 1) * CPB)
                dve.tensor_reduce(pooled[:, :, 0, new], hT[:, t[1] % 2, :, :].rearrange("p k (c s) -> p k c s", s=CH),
                                  AX_X, ALU.add).then_inc(pooled_once, 1)

            def pool_twice(t):
                new = slice(t[1] % NB * CPB, (t[1] % NB + 1) * CPB)
                dve.wait_ge(pooled_once, done(t))
                dve.tensor_copy(pooled[:, :, 1, new], pooled[:, :, 0, new]).then_inc(pooled_ready, 1)

            def copy_qk(t):
                dve.wait_ge(qk_psum, done(t))
                dve.wait_ge(part3_ready, done(back(t, 1)))
                dve.tensor_tensor(qkf[:, :], p_qkv[:, :], row[:, R_QK:R_QK + 2 * D], ALU.add).then_inc(qk_copied, 1)

            def copy_v(t):
                dve.wait_ge(v_psum, done(t))
                dve.wait_ge(pv_psum[NG - 1], done(back(t, 3)))
                dve.tensor_tensor(vp[:, t[1] % RING, :, 0:HD + 1], heads(p_qkv[:, 0:H * (HD + 1)], HD + 1), bv[:, :, :],
                                  ALU.add).then_inc(v_copied, 1)

            def copy_rq(t):
                dve.wait_ge(lat_psum, done(t))
                dve.wait_ge(ls_psum, done(back(t, 2)))
                dve.tensor_scalar(rqT[0:LD, t[1] % 2, :], p_a[0:LD, 0:P], brq[:, :], None, ALU.add).then_inc(rqT_ready, 1)

            def copy_rk(t):
                dve.wait_ge(lat_psum, done(t))
                dve.wait_ge(ls_psum, done(back(t, 2)))
                rk = p_a[:, 2 * P:2 * P + LT].unsqueeze(1).to_broadcast([P, LH, LT])
                at = C_BD + t[1] % NB * LH * LT
                dve.scalar_tensor_tensor(out=bd[:, t[1] % 2, :, :], in0=rk, scalar=brk[:, :],
                                         in1=cst[:, at:at + LH * LT].rearrange("p (h l) -> p h l", h=LH),
                                         op0=ALU.add, op1=ALU.mult).then_inc(lat_copied, 1)

            def copy_rv(t):
                dve.wait_ge(lat_psum, done(t))
                dve.tensor_tensor(rvb[:, :], p_a[:, 3 * P:3 * P + LD], row[:, R_RV:R_RV + LD], ALU.add).then_inc(rvb_ready, 1)

            def spread_rv(t):
                dve.wait_ge(rvb_ready, done(t))
                dve.wait_ge(loT_psum, done(back(t, 2)))
                dve.tensor_tensor(bvd[:, t[1] % 2, :, 0:LD], rvb[:, :].unsqueeze(1).to_broadcast([P, 2, LD]),
                                  cst[:, C_RV:C_RV + 2 * LD].rearrange("p (k l) -> p k l", k=2), ALU.mult).then_inc(bvd_ready, 1)

            def stack_dve(t, u):
                dve.wait_ge(stack_psum[u], done(t))
                dve.wait_ge(st_psum[NP - 1], done(back(t, 3)))
                dve.tensor_copy((qst, kst)[u // 2][0:KS, t[1] % RING, 8:16, :].rearrange("p h n -> p (h n)"),
                                p_x[1][0:KS, :].bitcast(BF16)).then_inc(stack_copied[u], 1)

            def maxima(t, i):
                wait_apart(dve, (s_psum[i], done(t)), (s_max[i - 2], done(t if i >= 2 else back(t, 1))),
                           (m_ready, done(back(t, 1))))
                for h in (2 * i, 2 * i + 1):
                    at = (h % 2) * 2 * P
                    scr = junk[:, h % 4, :]
                    if t[1] % NB:
                        ins = dve.tensor_tensor_reduce(scr, p_x[i % 2][:, at:at + 2 * P], smask, 1.0, -3.0e38,
                                                       ALU.add, ALU.max, mx[:, h:h + 1])
                    else:
                        ins = dve.tensor_tensor_reduce(scr[:, 0:P], p_x[i % 2][:, at + P:at + 2 * P], smask0, 1.0,
                                                       -3.0e38, ALU.add, ALU.max, mx[:, h:h + 1])
                ins.then_inc(s_max[i], 1)

            def negate_max(t):
                dve.wait_ge(s_max[NP - 1], done(t))
                dve.wait_ge(mT_psum, done(back(t, 1)))
                dve.tensor_scalar(mtok[:, KS:KS + H], mx[:, :], -1.0, None, ALU.mult).then_inc(m_ready, 1)

            def shift(t):
                dve.wait_ge(mT_psum, done(t))
                dve.tensor_copy(qst[KS:KS + H, t[1] % RING, :, :],
                                p_pv[KS:KS + H, 0:P // 2].bitcast(BF16).unsqueeze(1).to_broadcast([H, H, P]))\
                   .then_inc(shift_ready, 1)

            def lat_max(t):
                dve.wait_ge(ls_psum, done(t))
                dve.tensor_reduce(lmx[:, :], p_a[:, 0:LH * LT].rearrange("p (h l) -> p h l", h=LH), AX_X, ALU.max)\
                   .then_inc(lmx_ready, 1)

            def lat_shift(t):
                dve.wait_ge(lmx_ready, done(t))
                dve.wait_ge(lexp_ready, done(back(t, 1)))
                dve.tensor_tensor(ls[:, :, :], p_a[:, 0:LH * LT].rearrange("p (h l) -> p h l", h=LH),
                                  bc(lmx[:, :], LT), ALU.subtract).then_inc(ls_ready, 1)

            def lat_sum(t):
                dve.wait_ge(lexp_ready, done(t))
                dve.tensor_reduce(lsum[:, :], le[:, :, :], AX_X, ALU.add).then_inc(lsum_ready, 1)

            def lat_recip(t):
                dve.wait_ge(lsum_ready, done(t))
                dve.reciprocal(lrec[:, :], lsum[:, :]).then_inc(lrec_ready, 1)

            def lat_valid(t):
                dve.wait_ge(lrec_ready, done(t))
                valid = cst[:, C_VAL:C_VAL + 1] if t[1] % NB == 0 else 1.0
                dve.tensor_scalar(lrec2[:, :], lrec[:, :], valid, None, ALU.mult).then_inc(lval_ready, 1)

            def lat_norm(t):
                dve.wait_ge(lval_ready, done(t))
                dve.wait_ge(lpT_psum, done(back(t, 1)))
                dve.tensor_tensor(lp[:, :].rearrange("p (h l) -> p h l", h=LH), le[:, :, :], bc(lrec2[:, :], LT),
                                  ALU.mult).then_inc(lp_ready, 1)

            def prob_sum(t):
                dve.wait_ge(o_psum, done(t))
                dve.tensor_scalar(ssum[:, :], heads(p_misc[:, :], 32)[:, :, HD + 1], 1e-30, None, ALU.max)\
                   .then_inc(ssum_ready, 1)

            def prob_recip(t):
                dve.wait_ge(ssum_ready, done(t))
                dve.reciprocal(srec[:, :], ssum[:, :]).then_inc(srec_ready, 1)

            def gate_local(t):
                dve.wait_ge(srec_ready, done(t))
                dve.tensor_tensor(zl[:, :], heads(p_misc[:, :], 32)[:, :, HD], srec[:, :], ALU.mult).then_inc(zl_ready, 1)

            def local_out(t):
                dve.wait_ge(srec_ready, done(t))
                dve.tensor_tensor(local[:, :, :], heads(p_misc[:, :], 32)[:, :, 0:HD], bc(srec[:, :], HD), ALU.mult)\
                   .then_inc(local_ready, 1)

            def gate_sum(t):
                dve.wait_ge(zl_ready, done(t))
                dve.wait_ge(rem_ready, done(t))
                dve.wait_ge(ez_ready, done(back(t, 1)))
                dve.tensor_tensor(z[:, :], zl[:, :], rem[:, t[1] % RING, D:D + H], ALU.add).then_inc(z_ready, 1)

            def difference(t):
                dve.wait_ge(local_ready, done(t))
                dve.wait_ge(rem_ready, done(t))
                dve.tensor_tensor(heads(dif[:, :]), local[:, :, :], heads(rem[:, t[1] % RING, 0:D]), ALU.subtract)\
                   .then_inc(dif_ready, 1)

            def gate_one(t):
                dve.wait_ge(ez_ready, done(t))
                dve.tensor_scalar(g1[:, :], ez[:, :], 1.0, None, ALU.add).then_inc(g1_ready, 1)

            def gate_recip(t):
                dve.wait_ge(g1_ready, done(t))
                dve.reciprocal(gate[:, :], g1[:, :]).then_inc(gate_ready, 1)

            def gate_dif(t):
                dve.wait_ge(gate_ready, done(t))
                dve.wait_ge(dif_ready, done(t))
                dve.tensor_tensor(heads(dg[:, :]), heads(dif[:, :]), bc(gate[:, :], HD), ALU.mult).then_inc(dg_ready, 1)

            def mix_heads(t):
                dve.wait_ge(dg_ready, done(t))
                dve.wait_ge(mixT_psum, done(back(t, 1)))
                dve.tensor_tensor(mix[:, :], dg[:, :], rem[:, t[1] % RING, 0:D], ALU.add).then_inc(mix_ready, 1)

            def first_residual(t):
                dve.wait_ge(out_psum, done(t))
                dve.wait_ge(xb_ready, done(t))
                dve.wait_ge(ux_ready, done(back(t, 2)))
                dve.tensor_tensor(x1[:, t[1] % 2, :], p_misc[:, 0:D], xb[:, :], ALU.add).then_inc(x1_ready, 1)

            def norm2(t):
                dve.wait_ge(rstd2_ready, done(t))
                dve.wait_ge(h2a_ready, done(back(t, 1)))
                dve.tensor_scalar(h2n[:, :], x1[:, t[1] % 2, :], mv2[:, 0:1], rstd2[:, :], ALU.subtract, ALU.mult)\
                   .then_inc(h2n_ready, 1)

            def norm3(t):
                dve.wait_ge(rstd3_ready, done(t))
                dve.wait_ge(ya_ready, done(back(t, 1)))
                dve.tensor_scalar(h3[:, :], h2[:, :], mv3[:, 0:1], rstd3[:, :], ALU.subtract, ALU.mult)\
                   .then_inc(h3_ready, 1)

            def slot(t, stages):
                a, k, m, c, d = back(t, -2), back(t, -1), back(t, 1), back(t, 2), back(t, 3)
                A, K, S, T, C, D = ("A" in stages, "K" in stages, "S" in stages, "T" in stages, "C" in stages, "D" in stages)
                if K:
                    pool_tokens(k)
                if A:
                    bn1(a)
                if K:
                    pool_twice(k)
                if S:
                    lat_max(t)
                if D:
                    bn2(d)
                if S:
                    lat_shift(t)
                if A:
                    moments1(a)
                if T:
                    shift(m)
                if A:
                    add_eps1(a)
                if S:
                    lat_sum(t)
                if D:
                    moments2(d)
                if K:
                    copy_rk(k)
                    copy_rv(k)
                    copy_rq(k)
                if D:
                    add_eps2(d)
                if C:
                    prob_sum(c)
                if A:
                    norm1(a)
                if K:
                    copy_v(k)
                    stack_dve(k, 1)
                if S:
                    lat_recip(t)
                if D:
                    norm2(d)
                if C:
                    prob_recip(c)
                if K:
                    spread_rv(k)
                if S:
                    lat_valid(t)
                if C:
                    gate_local(c)
                    local_out(c)
                    gate_sum(c)
                if K:
                    stack_dve(k, 3)
                if S:
                    lat_norm(t)
                if C:
                    difference(c)
                    gate_one(c)
                if D:
                    bn3(d)
                if A:
                    copy_qk(a)
                if D:
                    moments3(d)
                if S:
                    maxima(t, 0)
                if D:
                    add_eps3(d)
                if C:
                    gate_recip(c)
                if S:
                    maxima(t, 1)
                if C:
                    gate_dif(c)
                if S:
                    maxima(t, 2)
                if C:
                    mix_heads(c)
                if S:
                    maxima(t, 3)
                    maxima(t, 4)
                    maxima(t, 5)
                    maxima(t, 6)
                if D:
                    norm3(d)
                if S:
                    maxima(t, 7)
                    negate_max(t)
                if C:
                    first_residual(c)

            dve.wait_ge(loaded_x0, 16)
            dve.wait_ge(loaded_x, 16)
            run(dve, slot)


def constants():
    import numpy as np

    c = np.zeros((P, C_END), np.float32)
    i, j = np.arange(P)[:, None], np.arange(P)[None, :]
    c[:, C_ID:C_ID + P] = i == j
    seen_before = (j >= i) & ((i > 0) | (j > 0))
    c[:, C_SM:C_SM + P] = np.where(seen_before, 0, BIG)
    c[:, C_SM + P:C_SM + 2 * P] = np.where(j < i, 0, BIG)
    c[:, C_SM0:C_SM0 + P] = np.where((j < i) | ((i == 0) & (j == 0)), 0, BIG)
    hd = LD // LH
    for n in range(NB):
        t = c[:, C_BD + n * LH * LT:C_BD + (n + 1) * LH * LT].reshape(P, LH, LT)
        for h in range(LH):
            t[h * hd:(h + 1) * hd, h, :] = 1
        for q in range(CPB):
            t[LD + q, :, n * CPB + q:] = BIG
    c[:, C_BD:C_BD + NB * LH * LT] = np.concatenate(
        [c[:, C_BD + n * LH * LT:C_BD + (n + 1) * LH * LT] for n in range(NB)], 1)
    for g in range(2):
        for u in range(2):
            h = 2 * g + u
            c[u * LT:(u + 1) * LT, C_RV + g * LD + h * hd:C_RV + g * LD + (h + 1) * hd] = 1
    for q in range(CPB):
        c[LD + q, C_IND + q * CH:C_IND + (q + 1) * CH] = 1
    for h in range(H):
        c[KS + h, C_SEL + h] = 1
    c[CH:, C_VAL] = 1
    c[LD:LD + CPB, C_BRK] = 1
    return c


def kernel(**inputs):
    import numpy as np
    import concourse.bacc as bacc
    from concourse.bass_utils import run_bass_kernel_spmd

    a = {k: np.ascontiguousarray(v) for k, v in inputs.items()}
    rows = np.concatenate([a["L0_attn_qkv_b"], a["L0_attn_rkv_b"][LD:], a["L0_ffn_ln_g"], a["L0_ffn_ln_b"],
                           a["L0_attn_out_b"], a["L0_attn_gl_w"][:, 0], a["L0_attn_gr_w"][:, 0]])
    arrays = {
        "x": a["L0_attn_x"].reshape(NT, P, D),
        "qkv_w": a["L0_attn_qkv_w"],
        "rq_w": a["L0_attn_rq_w"],
        "rq_b": a["L0_attn_rq_b"].reshape(LD, 1),
        "rkv_w": a["L0_attn_rkv_w"],
        "rk_b": np.ascontiguousarray(a["L0_attn_rkv_b"][:LD].reshape(LD, 1)),
        "rout_w": a["L0_attn_rout_w"],
        "rout_b": a["L0_attn_rout_b"].reshape(1, D),
        "out_w": a["L0_attn_out_w"],
        "c_t": np.ascontiguousarray(a["L0_c"].T.reshape(KC, P, B).transpose(1, 0, 2)),
        "wmod": a["L0_wmod"],
        "rows": rows,
        "consts": constants(),
    }
    nc = bacc.Bacc("TRN2", target_bir_lowering=False, num_devices=1)
    args = [nc.dram_tensor(f"in_{k}", v.shape, mybir.dt.from_np(v.dtype), kind="ExternalInput").ap()
            for k, v in arrays.items()]
    out = nc.dram_tensor("out_y", (NT, P, D), F32, kind="ExternalOutput").ap()
    build(nc, *args, out)
    r = run_bass_kernel_spmd(nc, [{f"in_{k}": v for k, v in arrays.items()}], core_ids=[0])
    return r.results[0]["out_y"].reshape(B, S, D)
```

```python
from contextlib import ExitStack

import concourse.bass as bass
from concourse import mybir

F32 = mybir.dt.float32
BF16 = mybir.dt.bfloat16
ALU = mybir.AluOpType
ACT = mybir.ActivationFunctionType
AX_X = mybir.AxisListType.X

B, S, D = 4, 1024, 256
P = 128
KC = D // P
H, HD = 16, 16
NB = S // P
NT = B * NB
LH, LT, LD = 4, 64, 64
CH = S // LT
CPB = P // CH
VC = HD + 2
NTERM = 6
KS = NTERM * HD
NP = H // 2
NG = H // 4
RING = 4
EPS = 1e-5
BIG = -1.0e9
Q_SLOTS = {1: (2, 5, 1), 2: (1, 6, 4), 3: (0, 1, 1)}
K_SLOTS = {1: (0, 3, 1), 2: (3, 6, 2), 3: (4, 5, 1)}

BASE = 6
Y_BASE = 3

SU_SILU, SU_MODT, SU_PRE = 3, 14, 27
SU_ROWS = SU_PRE + 13
SU_ALL = SU_ROWS + B // 2 + 1
SP_LOADED, SP_ZERO, SP_SCALED = 4, 17, 21
SP_ALL = SP_SCALED + B // 2
SA_EXP, SA_QK, SA_ALL = 1, 3, 3 + RING

C_ID, C_SM, C_SM0, C_RV = 0, P, P + 2 * P, P + 3 * P
C_IND = C_RV + 2 * LD
C_SEL = C_IND + P
C_VAL = C_SEL + H
C_BRK = C_VAL + 1
C_BD = C_BRK + 1
C_END = C_BD + NB * LH * LT

R_QK, R_V, R_RV = 0, 2 * D, 3 * D
R_G, R_B, R_O = R_RV + LD, R_RV + LD + D, R_RV + LD + 2 * D
R_GL, R_GR = R_O + D, R_O + D + HD
R_END = R_GR + HD


def build(nc, x, qkv_w, rq_w, rq_b, rkv_w, rk_b, rout_w, rout_b, out_w, c_t, wmod, rows, consts, out):
    ctx = ExitStack()
    with ctx:
        def sb(name, shape, dt=F32):
            return ctx.enter_context(nc.sbuf_tensor(name, shape, dt))

        def bank(name):
            return ctx.enter_context(nc.psum_tensor(name, [P, 512], F32))

        started = {"PE": [], "DVE": [], "ACT": [], "POOL": []}

        def sem(name):
            return ctx.enter_context(nc.semaphore(name))

        def counted(name, engine, dummies=0):
            s = sem(name)
            started[engine].append((s, BASE - dummies))
            return s

        XPAD = 3
        x_all = sb("x_all", [P, (XPAD + NT + 2) * D])
        cst = sb("cst", [P, C_END])
        row = sb("row", [P, R_END])
        ident = cst[:, C_ID:C_ID + P]
        ident_bf = sb("ident_bf", [P, P], BF16)
        smask = cst[:, C_SM:C_SM + 2 * P]
        smask0 = cst[:, C_SM0:C_SM0 + P]
        wqk = sb("wqk", [P, KC, 2 * D])
        wv = sb("wv", [P, KC, H, HD + 1])
        bv = sb("bv", [P, H, HD + 1])
        wrq = sb("wrq", [P, KC, P])
        wrk = sb("wrk", [P, KC, P])
        wrv = sb("wrv", [P, KC, LD])
        brq = sb("brq", [LD, 1])
        brk = sb("brk", [P, 1])
        wro = sb("wro", [P, D + H])
        wo = sb("wo", [P, (B + 1) * KC * D])
        obg = sb("obg", [P, (B + 1) * D])
        c1 = sb("c1", [P, (B + 1) * D])
        s1 = sb("s1", [P, (B + 1) * D])
        g3 = sb("g3", [P, (B + 1) * D])
        b3 = sb("b3", [P, (B + 1) * D])
        mod_t = sb("mod_t", [P, (B + 1) * 8])
        ct = sb("ct", [P, KC, B])
        cs = sb("cs", [P, KC, B])
        st = sb("st", [P, 6])
        mv = sb("mv", [P, 2])
        rstd = sb("rstd", [P, 1])
        ve1, ve2, ve3 = sb("ve1", [P, 1]), sb("ve2", [P, 1]), sb("ve3", [P, 1])
        half = sb("half", [P, 1])
        xn = sb("xn", [P, 2, D])
        hT = sb("hT", [P, 2, KC, P])
        pooled = sb("pooled", [P, KC, 2, LT])
        qkf = sb("qkf", [P, 2 * D])
        res = sb("res", [P, 2 * D])
        qtok = sb("qtok", [P, H, KS], BF16)
        ktok = sb("ktok", [P, H, KS], BF16)
        qst = sb("qst", [P, RING, H, P], BF16)
        kst = sb("kst", [P, RING, H, P], BF16)
        vp = sb("vp", [P, RING, H, VC])
        rqT = sb("rqT", [P, 2, P])
        bd = sb("bd", [P, 2, LH, LT])
        rvb = sb("rvb", [P, LD])
        bvd = sb("bvd", [P, 2, 2, P])
        mx = sb("mx", [P, H])
        mtok = sb("mtok", [P, P], BF16)
        mrow = sb("mrow", [P, P], BF16)
        junk = sb("junk", [P, 4, 2 * P], BF16)
        pr = sb("pr", [P, H, 2, P])
        oT = sb("oT", [P, 4 * P])
        lmx = sb("lmx", [P, LH])
        lneg = sb("lneg", [P, LH])
        le = sb("le", [P, LH, LT])
        lsum = sb("lsum", [P, LH])
        lrec = sb("lrec", [P, LH])
        lrec2 = sb("lrec2", [P, LH])
        lp = sb("lp", [P, LH * LT])
        lpT = sb("lpT", [P, 2 * P])
        loT = sb("loT", [P, P])
        rem = sb("rem", [P, RING, D + H])
        ssum = sb("ssum", [P, H])
        srec = sb("srec", [P, H])
        local = sb("local", [P, H, HD])
        zl = sb("zl", [P, H])
        z = sb("z", [P, H])
        ez = sb("ez", [P, H])
        g1 = sb("g1", [P, H])
        gate = sb("gate", [P, H])
        dif = sb("dif", [P, D])
        dg = sb("dg", [P, D])
        mix = sb("mix", [P, D])
        mixT = sb("mixT", [P, D])
        xb = sb("xb", [P, D])
        x1 = sb("x1", [P, 2, D])
        st2 = sb("st2", [P, 6])
        mv2 = sb("mv2", [P, 2])
        rstd2 = sb("rstd2", [P, 1])
        h2n = sb("h2n", [P, D])
        h2a = sb("h2a", [P, D])
        h2 = sb("h2", [P, D])
        st3 = sb("st3", [P, 6])
        mv3 = sb("mv3", [P, 2])
        rstd3 = sb("rstd3", [P, 1])
        h3 = sb("h3", [P, D])
        ux = sb("ux", [P, D])
        ya = sb("ya", [P, D])
        y = sb("y", [P, 2, D])
        wm = pr[:, 0:12, :, :].rearrange("p h a n -> p (h a n)").rearrange("p (k n) -> p k n", k=KC)
        gt = pr[:, 12:16, :, :].rearrange("p h a n -> p (h a n)")
        wv_in = y[:, :, :].rearrange("p a d -> p (a d)")
        wo_in = rem[:, 0:2, :].rearrange("p r d -> p (r d)")[:, 0:KC * D]

        p_a, p_qkv, p_misc = bank("p_a"), bank("p_qkv"), bank("p_misc")
        p_x = [bank("p_x0"), bank("p_x1")]
        p_y = [bank("p_y0"), bank("p_y1")]
        p_pv = bank("p_pv")

        mrow6 = qst[0:B, 1:3, :, :].rearrange("p r h n -> p (r h n)").bitcast(F32).rearrange("p (j d) -> p j d", d=D)
        ga = pr[:, 0:4, :, :].rearrange("p h a n -> p (h a n)")
        mod_rows = nc.dram_tensor("mod_rows", (6, B, D), F32, kind="Internal").ap()

        loaded_c, loaded_m, loaded_m2 = sem("loaded_c"), sem("loaded_m"), sem("loaded_m2")
        loaded_k, loaded_bd, loaded_w = sem("loaded_k"), sem("loaded_bd"), sem("loaded_w")
        rows_stored, loaded_g, loaded_t = sem("rows_stored"), sem("loaded_g"), sem("loaded_t")
        loaded_q, loaded_x0, loaded_x = sem("loaded_q"), sem("loaded_x0"), sem("loaded_x")
        loaded_x1 = sem("loaded_x1")
        y_stored = [sem("y_stored0"), sem("y_stored1")]
        su_dve, su_act, su_pe, su_pool = sem("setup_dve"), sem("setup_act"), sem("setup_pe"), sem("setup_pool")

        st1_ready, mv1_ready, ve1_ready = (counted(n, "DVE") for n in ("st1_ready", "mv1_ready", "ve1_ready"))
        rstd1_ready = counted("rstd1_ready", "POOL")
        xn_ready = counted("xn_ready", "DVE")
        hT_psum, hT_ready = counted("hT_psum", "PE"), counted("hT_ready", "ACT")
        pooled_once, pooled_ready = counted("pooled_once", "DVE"), counted("pooled_ready", "DVE")
        qk_psum, qk_copied = counted("qk_psum", "PE"), counted("qk_copied", "DVE")
        v_psum, v_copied = counted("v_psum", "PE"), counted("v_copied", "DVE")
        rqT_ready = counted("rqT_ready", "DVE")
        lat_psum, lat_copied, rvb_ready, bvd_ready = (counted("lat_psum", "PE"), counted("lat_copied", "DVE"),
                                                      counted("rvb_ready", "DVE"), counted("bvd_ready", "DVE"))
        part1_ready, res_ready = counted("part1_ready", "ACT"), counted("res_ready", "POOL")
        part2_ready, part3_ready = counted("part2_ready", "ACT"), counted("part3_ready", "POOL")
        stack_psum = [counted(f"stack_psum{u}", "PE") for u in range(4)]
        stack_copied = [counted(f"stack_copied{u}", "ACT") for u in range(4)]
        s_psum = [counted(f"s_psum{i}", "PE") for i in range(NP)]
        s_max = [counted(f"s_max{i}", "DVE") for i in range(NP)]
        m_ready = counted("m_ready", "DVE")
        mT_psum, mrow_ready, shift_ready = (counted("mT_psum", "PE", 1), counted("mrow_ready", "DVE", 1),
                                            counted("shift_ready", "DVE", 1))
        st_psum = [counted(f"st_psum{i}", "PE", 1) for i in range(NP)]
        exp_done = [counted(f"exp_done{i}", "ACT", 1) for i in range(NP)]
        masked = [counted(f"masked{g}", "POOL", 1) for g in range(NG)]
        pv_psum = [counted(f"pv_psum{g}", "PE", 1) for g in range(NG)]
        ls_psum, lmax_ready, lmx_ready, lexp_ready = (counted("ls_psum", "PE"), counted("lmax_ready", "DVE"),
                                                      counted("lmx_ready", "DVE"), counted("lexp_ready", "ACT"))
        lval_ready, lp_ready = counted("lval_ready", "DVE"), counted("lp_ready", "DVE")
        lrec_ready = sem("lrec_ready")
        lpT_psum, lpT_ready = counted("lpT_psum", "PE"), counted("lpT_ready", "ACT")
        loT_psum, loT_ready = counted("loT_psum", "PE", 1), counted("loT_ready", "ACT", 1)
        rem_psum, rem_ready = counted("rem_psum", "PE", 1), counted("rem_ready", "ACT", 1)
        oT_ready = counted("oT_ready", "ACT", 2)
        o_psum = counted("o_psum", "PE", 2)
        ssum_ready, srec_ready, zl_ready, local_ready, z_ready = (
            counted(n, "DVE", 2) for n in ("ssum_ready", "srec_ready", "zl_ready", "local_ready", "z_ready"))
        ez_ready = counted("ez_ready", "ACT", 2)
        g1_ready, gate_ready, dg_ready, mix_ready = (
            counted(n, "DVE", 2) for n in ("g1_ready", "gate_ready", "dg_ready", "mix_ready"))
        dif_ready = counted("dif_ready", "POOL", 2)
        mixT_psum, mixT_ready = counted("mixT_psum", "PE", 2), counted("mixT_ready", "ACT", 2)
        xb_ready = counted("xb_ready", "POOL", 2)
        out_psum, x1_ready = counted("out_psum", "PE", 2), counted("x1_ready", "DVE", 2)
        st2_ready, mv2_ready, ve2_ready, h2n_ready = (
            counted(n, "DVE", 3) for n in ("st2_ready", "mv2_ready", "ve2_ready", "h2n_ready"))
        rstd2_ready, rstd3_ready = counted("rstd2_ready", "POOL", 3), counted("rstd3_ready", "POOL", 3)
        ux_ready, h2a_ready, h2_ready = (counted(n, "POOL", 3) for n in ("ux_ready", "h2a_ready", "h2_ready"))
        st3_ready, mv3_ready, ve3_ready, h3_ready = (
            counted(n, "DVE", 3) for n in ("st3_ready", "mv3_ready", "ve3_ready", "h3_ready"))
        ya_ready, y_ready = counted("ya_ready", "POOL", 3), counted("y_ready", "POOL", 3)

        def done(t):
            return t[0] + (t[1] + 1 + BASE)

        def back(t, k):
            return (t[0], t[1] - k)

        def batch(t):
            return t[0] + 8 * (t[1] // NB) + 8

        def x_of(t):
            return x_all[:, bass.ds((t[0] + (t[1] + XPAD)) * D, D)]

        def per_batch(tile, t, width=D):
            return tile[:, bass.ds(batch(t) * (width // NB), width)]

        def heads(ap, k=HD):
            return ap.rearrange("p (h k) -> p h k", k=k)

        def bc(ap, n):
            return ap.unsqueeze(2).to_broadcast([ap.shape[0], ap.shape[1], n])

        def slots(tok, rule):
            a, e, s = rule
            return tok[:, :, :].rearrange("p h (s k) -> p h s k", k=HD)[:, :, a:e:s, :]

        def rep(ap, rule):
            a, e, s = rule
            n = len(range(a, e, s))
            return heads(ap).unsqueeze(2).to_broadcast([P, H, n, HD])

        def scale_wo(eng, b, setup_sem):
            return eng.tensor_tensor(wo[:, (b + 1) * KC * D:(b + 2) * KC * D].rearrange("p (k n) -> p k n", k=KC),
                                     wo_in.rearrange("p (k n) -> p k n", k=KC),
                                     ga[:, b * D:(b + 1) * D].unsqueeze(1).to_broadcast([P, KC, D]), ALU.mult)\
                      .then_inc(setup_sem, 1)

        block = ctx.enter_context(nc.Block())

        def wait_apart(eng, *waits):
            values = [v if isinstance(v, int) else eng.snap(eng.to_reg(v)) for _, v in waits]
            eng.wait_ge(su_act, 1)
            for (s, _), v in zip(waits, values):
                eng.wait_ge(s, v)

        def run(eng, slot):
            with eng.Fori(0, NT - NB + 1, NB) as i:
                for n in range(NB):
                    slot((i, n), "AKSTCD")
            slot((NT, 0), "TCD")
            slot((NT, 1), "CD")
            slot((NT, 2), "D")

        def stored(t):
            return t[0] * 8 + 16 * (t[1] // 2 + 1 + Y_BASE)

        @block.sync
        def _(sp):
            for p in range(2):
                sp.sem_inc(y_stored[p], 16 * Y_BASE)
            sp.dma_start(ct[:, :, :], c_t).then_inc(loaded_c, 16)
            wmod_k = wmod.rearrange("(k p) n -> p k n", p=P)
            sp.dma_start(wm[:, :, 0:2 * D], wmod_k[:, :, 0:2 * D]).then_inc(loaded_m, 16)
            sp.dma_start(cst[:, 0:C_BD], consts[:, 0:C_BD]).then_inc(loaded_k, 16)
            sp.dma_start(row[:, :], rows.partition_broadcast(P)).then_inc(loaded_k, 16)
            sp.dma_start(x_all[:, XPAD * D:(XPAD + 2) * D].rearrange("p (t d) -> p t d", d=D),
                         x[0:2].rearrange("t p d -> p t d")).then_inc(loaded_x0, 16)
            sp.dma_start(wm[:, :, 2 * D:], wmod_k[:, :, 2 * D:]).then_inc(loaded_m2, 16)
            sp.wait_ge(loaded_w, 16 * 9)
            sp.dma_start(cst[:, C_BD:], consts[:, C_BD:]).then_inc(loaded_bd, 16)
            sp.dma_start(x_all[:, (XPAD + 2) * D:(XPAD + NB) * D].rearrange("p (t d) -> p t d", d=D),
                         x[2:NB].rearrange("t p d -> p t d")).then_inc(loaded_x1, 16)
            sp.wait_ge(su_dve, SU_ROWS)
            sp.dma_start(mod_rows.rearrange("j b d -> b j d"), mrow6[:, 0:6, :]).then_inc(rows_stored, 16)
            sp.wait_ge(rows_stored, 16)
            sp.dma_start(ga, mod_rows[0].rearrange("b d -> (b d)").partition_broadcast(P)).then_inc(loaded_g, 16)
            for j, tile in enumerate((obg, s1, c1, g3, b3)):
                sp.dma_start(tile[:, D:], mod_rows[1 + j].rearrange("b d -> (b d)").partition_broadcast(P))\
                  .then_inc(loaded_t, 16)
            sp.dma_start(x_all[:, (XPAD + NB) * D:(XPAD + NT) * D].rearrange("p (t d) -> p t d", d=D),
                         x[NB:NT].rearrange("t p d -> p t d")).then_inc(loaded_x, 16)

            def store(t):
                sp.wait_ge(y_ready, done(t))
                sp.dma_start(out[bass.ds(t[0] + t[1], 1)].rearrange("t p d -> (t p) d"),
                             y[:, t[1] % 2, :]).then_inc(y_stored[t[1] % 2], 16)

            for n in range(3, NB):
                store((0, n - 3))
            with sp.Fori(NB, NT - NB + 1, NB) as i:
                for n in range(NB):
                    store((i, n - 3))
            for n in range(3):
                store((NT, n - 3))
            for p in range(2):
                sp.wait_ge(y_stored[p], stored((NT, p - 2)))

        @block.gpsimd
        def _(pool):
            for s, v in started["POOL"]:
                pool.sem_inc(s, v)
            for t in (wrq, wrk, wro, mod_t):
                pool.memset(t[:], 0.0).then_inc(su_pool, 1)
            pool.memset(half[:, :], -0.5).then_inc(su_pool, 1)
            for t in (rqT, vp, loT, bvd, pooled, mtok):
                pool.memset(t[:], 0.0).then_inc(su_pool, 1)
            pool.memset(rem[:, 2:4, :].rearrange("p r d -> p (r d)"), 0.0).then_inc(su_pool, 1)
            for t in (obg, c1, s1, g3, b3):
                pool.memset(t[:, 0:D], 0.0).then_inc(su_pool, 1)

            def scale_weights():
                pool.wait_ge(loaded_w, 16 * 9)
                pool.tensor_scalar(wrq[:, :, :], wrq[:, :, :], (LD // LH) ** -0.5, None, ALU.mult).then_inc(su_pool, 1)
                pool.tensor_scalar(brq[:, :], brq[:, :], (LD // LH) ** -0.5, None, ALU.mult).then_inc(su_pool, 1)
                pool.tensor_scalar(wrk[:, :, :], wrk[:, :, :], 1.0 / CH, None, ALU.mult).then_inc(su_pool, 1)
                pool.tensor_scalar(wrv[:, :, :], wrv[:, :, :], 1.0 / CH, None, ALU.mult).then_inc(su_pool, 1)

            def res1(t):
                pool.wait_ge(part1_ready, done(t))
                pool.tensor_tensor(heads(res[:, 0:D]), heads(qkf[:, 0:D]), slots(qtok, Q_SLOTS[1])[:, :, 0, :], ALU.subtract)
                pool.tensor_tensor(heads(res[:, D:2 * D]), heads(qkf[:, D:2 * D]), slots(ktok, K_SLOTS[1])[:, :, 0, :],
                                   ALU.subtract).then_inc(res_ready, 1)

            def part3(t):
                pool.wait_ge(part2_ready, done(t))
                pool.tensor_tensor(slots(qtok, Q_SLOTS[3])[:, :, 0, :], heads(res[:, 0:D]),
                                   slots(qtok, Q_SLOTS[2])[:, :, 0, :], ALU.subtract)
                pool.tensor_tensor(slots(ktok, K_SLOTS[3])[:, :, 0, :], heads(res[:, D:2 * D]),
                                   slots(ktok, K_SLOTS[2])[:, :, 0, :], ALU.subtract).then_inc(part3_ready, 1)

            def mask(t, g):
                wait_apart(pool, (exp_done[2 * g + 1], done(t)))
                own = pr[:, 4 * g:4 * g + 4, 1, :]
                ins = pool.affine_select(out=own, in_=own, compare_op=ALU.is_ge, fill=0.0, base=-1,
                                         pattern=[[0, 4], [1, P]], channel_multiplier=-1)
                if t[1] % NB:
                    prev = pr[:, 4 * g:4 * g + 4, 0, :]
                    ins = pool.affine_select(out=prev, in_=prev, compare_op=ALU.is_ge, fill=0.0, base=-1,
                                             pattern=[[0, 4], [-P, P]], channel_multiplier=P + 1)
                ins.then_inc(masked[g], 1)

            def power(ve_, rstd_, s_ve, s_rstd, t):
                pool.wait_ge(s_ve, done(t))
                pool.tensor_tensor(rstd_[:, :], ve_[:, :], half[:, :], ALU.pow).then_inc(s_rstd, 1)

            def rstd1(t):
                pool.wait_ge(xn_ready, done(back(t, 1)))
                power(ve1, rstd, ve1_ready, rstd1_ready, t)

            def rstd2_of(t):
                power(ve2, rstd2, ve2_ready, rstd2_ready, t)

            def rstd3_of(t):
                power(ve3, rstd3, ve3_ready, rstd3_ready, t)

            def difference(t):
                pool.wait_ge(local_ready, done(t))
                pool.wait_ge(rem_ready, done(t))
                pool.wait_ge(dg_ready, done(back(t, 1)))
                pool.tensor_tensor(heads(dif[:, :]), local[:, :, :], heads(rem[:, t[1] % RING, 0:D]), ALU.subtract)\
                    .then_inc(dif_ready, 1)

            def add_bias(t):
                wait_apart(pool, (x1_ready, done(back(t, 1))))
                if t[1] == 0:
                    pool.wait_ge(loaded_t, 16 * 5)
                    pool.wait_ge(loaded_x, 16)
                pool.tensor_tensor(xb[:, :], x_of(t), per_batch(obg, t), ALU.add).then_inc(xb_ready, 1)

            def add_u(t):
                wait_apart(pool, (x1_ready, done(t)), (y_ready, done(back(t, 1))))
                pool.tensor_tensor(ux[:, :], x1[:, t[1] % 2, :], per_batch(b3, t), ALU.add).then_inc(ux_ready, 1)

            def scale2(t):
                wait_apart(pool, (h2n_ready, done(t)))
                pool.tensor_tensor(h2a[:, :], h2n[:, :], per_batch(c1, t), ALU.mult).then_inc(h2a_ready, 1)

            def shift2(t):
                wait_apart(pool, (h2a_ready, done(t)), (h3_ready, done(back(t, 1))))
                pool.tensor_tensor(h2[:, :], h2a[:, :], per_batch(s1, t), ALU.add).then_inc(h2_ready, 1)

            def scale3(t):
                wait_apart(pool, (h3_ready, done(t)))
                pool.tensor_tensor(ya[:, :], h3[:, :], per_batch(g3, t), ALU.mult).then_inc(ya_ready, 1)

            def finish(t):
                pool.wait_ge(ya_ready, done(t))
                pool.wait_ge(ux_ready, done(t))
                pool.wait_ge(y_stored[t[1] % 2], stored(back(t, 2)))
                pool.tensor_tensor(y[:, t[1] % 2, :], ya[:, :], ux[:, :], ALU.add).then_inc(y_ready, 1)

            def slot(t, stages):
                a, k, m, c, d = back(t, -2), back(t, -1), back(t, 1), back(t, 2), back(t, 3)
                A, K, T, C, D = ("A" in stages, "K" in stages, "T" in stages, "C" in stages, "D" in stages)
                if D:
                    add_u(d)
                if C:
                    add_bias(c)
                if A:
                    rstd1(a)
                if D:
                    rstd2_of(d)
                if T:
                    mask(m, 0)
                if K:
                    part3(k)
                if D:
                    scale2(d)
                if C:
                    difference(c)
                if D:
                    shift2(d)
                if T:
                    mask(m, 1)
                    mask(m, 2)
                if D:
                    rstd3_of(d)
                if T:
                    mask(m, 3)
                if D:
                    scale3(d)
                    finish(d)
                if A:
                    res1(a)

            pool.wait_ge(su_pool, SP_ZERO)
            pool.wait_ge(loaded_k, 32)
            b0, b1 = (0, 0), (0, 1)
            rstd1(b0)
            scale_weights()
            rstd1(b1)
            res1(b0)
            part3(b0)
            res1(b1)
            pool.wait_ge(loaded_g, 16)
            for b in range(B // 2):
                scale_wo(pool, b, su_pool)
            pool.wait_ge(su_pool, SP_ALL)
            pool.wait_ge(su_dve, SU_ALL)
            pool.wait_ge(loaded_x1, 16)
            run(pool, slot)

        @block.scalar
        def _(act):
            act.dma_start(wqk[:, :, :], qkv_w[:, 0:2 * D].rearrange("(k p) n -> p k n", p=P)).then_inc(loaded_q, 16)
            act.dma_start(wv_in.rearrange("p (k n) -> p k n", k=KC),
                          qkv_w[:, 2 * D:3 * D].rearrange("(k p) n -> p k n", p=P)).then_inc(loaded_w, 16)
            act.wait_ge(loaded_c, 16)
            act.activation(cs[:, :, :], ct[:, :, :], ACT.Exp, scale=-1.0).then_inc(su_act, 1)
            act.wait_ge(su_pool, SP_LOADED)
            act.dma_start(wrq[:, :, 0:LD], rq_w.rearrange("(k p) n -> p k n", p=P)).then_inc(loaded_w, 16)
            act.dma_start(wrk[:, :, 0:LD], rkv_w[:, 0:LD].rearrange("(k p) n -> p k n", p=P)).then_inc(loaded_w, 16)
            act.dma_start(wrv[:, :, :], rkv_w[:, LD:2 * LD].rearrange("(k p) n -> p k n", p=P)).then_inc(loaded_w, 16)
            act.dma_start(wro[0:LD, 0:D], rout_w).then_inc(loaded_w, 16)
            act.dma_start(wro[LD:LD + 1, 0:D], rout_b).then_inc(loaded_w, 16)
            act.dma_start(brq[:, :], rq_b).then_inc(loaded_w, 16)
            act.dma_start(brk[0:LD, :], rk_b).then_inc(loaded_w, 16)
            act.dma_start(wo_in.rearrange("p (k n) -> p k n", k=KC),
                          out_w.rearrange("(k p) n -> p k n", p=P)).then_inc(loaded_w, 16)
            for s, v in started["ACT"]:
                act.sem_inc(s, v)
            act.wait_ge(loaded_q, 16)
            act.activation(wqk[:, :, 0:D], wqk[:, :, 0:D], ACT.Copy, scale=HD ** -0.5).then_inc(su_act, 1)
            act.wait_ge(loaded_k, 32)
            act.activation(row[:, 0:D], row[:, 0:D], ACT.Copy, scale=HD ** -0.5).then_inc(su_act, 1)

            def pick(r):
                act.activation(kst[KS:KS + H, r, :, :], bc(cst[KS:KS + H, C_SEL:C_SEL + H], P), ACT.Copy).then_inc(su_act, 1)

            def modulated(t):
                wait_apart(act, (hT_psum, done(t)), (v_psum, done(back(t, 2))), (lat_psum, done(back(t, 2))))
                for k in range(KC):
                    ins = act.activation(hT[:, t[1] % 2, k, :], p_a[:, k * P:(k + 1) * P], ACT.Identity,
                                         scale=mod_t[:, bass.ds(batch(t) + (k - 8), 1)],
                                         bias=mod_t[:, bass.ds(batch(t) + (k + KC - 8), 1)])
                ins.then_inc(hT_ready, 1)

            def part1(t):
                act.wait_ge(qk_copied, done(t))
                act.wait_ge(stack_psum[3], done(back(t, 1)))
                act.activation(slots(qtok, Q_SLOTS[1]), rep(qkf[:, 0:D], Q_SLOTS[1]), ACT.Copy)
                act.activation(slots(ktok, K_SLOTS[1]), rep(qkf[:, D:2 * D], K_SLOTS[1]), ACT.Copy).then_inc(part1_ready, 1)

            def part2(t):
                act.wait_ge(res_ready, done(t))
                act.activation(slots(qtok, Q_SLOTS[2]), rep(res[:, 0:D], Q_SLOTS[2]), ACT.Copy)
                act.activation(slots(ktok, K_SLOTS[2]), rep(res[:, D:2 * D], K_SLOTS[2]), ACT.Copy).then_inc(part2_ready, 1)

            def stack_copy(t, u):
                act.wait_ge(stack_psum[u], done(t))
                act.wait_ge(st_psum[NP - 1], done(back(t, 3)))
                dst = (qst, kst)[u % 2][0:KS, t[1] % RING, 8 * (u // 2):8 * (u // 2) + 8, :]
                act.activation(dst.rearrange("p h n -> p (h n)"), p_x[u % 2][0:KS, :].bitcast(BF16), ACT.Copy)\
                   .then_inc(stack_copied[u], 1)

            def exps(t, i):
                act.wait_ge(st_psum[i], done(t))
                act.wait_ge(pv_psum[i // 2], done(back(t, 1)))
                src = p_y[i % 2][:, :].rearrange("p (h a n) -> p h a n", h=2, a=2)
                if t[1] % NB:
                    act.activation(pr[:, 2 * i:2 * i + 2, :, :], src, ACT.Exp).then_inc(exp_done[i], 1)
                else:
                    act.activation(pr[:, 2 * i:2 * i + 2, 1, :], src[:, :, 1, :], ACT.Exp).then_inc(exp_done[i], 1)

            def out_t(t):
                act.wait_ge(pv_psum[NG - 1], done(t))
                act.wait_ge(o_psum, done(back(t, 1)))
                act.activation(oT[:, :], p_pv[:, :], ACT.Copy).then_inc(oT_ready, 1)

            def lat_exp(t):
                act.wait_ge(lmx_ready, done(t))
                act.wait_ge(lp_ready, done(back(t, 1)))
                for h in range(LH):
                    ins = act.activation(le[:, h, :], p_a[:, h * LT:(h + 1) * LT], ACT.Exp, bias=lneg[:, h:h + 1],
                                         accum_out=lsum[:, h:h + 1])
                ins.then_inc(lexp_ready, 1)

            def lat_pT(t):
                act.wait_ge(lpT_psum, done(t))
                act.wait_ge(loT_psum, done(back(t, 1)))
                act.activation(lpT[:, :], p_a[:, 0:2 * P], ACT.Copy).then_inc(lpT_ready, 1)

            def lat_oT(t):
                act.wait_ge(loT_psum, done(t))
                act.wait_ge(rem_psum, done(back(t, 1)))
                act.activation(loT[0:LD, :], p_misc[0:LD, 0:P], ACT.Copy).then_inc(loT_ready, 1)

            def remote(t):
                act.wait_ge(rem_psum, done(t))
                act.wait_ge(mix_ready, done(back(t, RING)))
                act.wait_ge(dif_ready, done(back(t, RING)))
                act.activation(rem[:, t[1] % RING, :], p_qkv[:, 0:D + H], ACT.Copy).then_inc(rem_ready, 1)

            def gate_exp(t):
                act.wait_ge(z_ready, done(t))
                act.wait_ge(g1_ready, done(back(t, 1)))
                act.activation(ez[:, :], z[:, :], ACT.Exp, scale=-1.0).then_inc(ez_ready, 1)

            def mixed_t(t):
                act.wait_ge(mixT_psum, done(t))
                act.wait_ge(out_psum, done(back(t, 1)))
                act.activation(mixT[:, :], p_misc[:, 0:D], ACT.Copy).then_inc(mixT_ready, 1)

            def slot(t, stages):
                a, k, m, c = back(t, -2), back(t, -1), back(t, 1), back(t, 2)
                A, K, S, T, C = ("A" in stages, "K" in stages, "S" in stages, "T" in stages, "C" in stages)
                if C:
                    out_t(c)
                if T:
                    lat_oT(m)
                if K:
                    part2(k)
                if T:
                    exps(m, 0)
                    exps(m, 1)
                if S:
                    lat_exp(t)
                if T:
                    exps(m, 2)
                    exps(m, 3)
                if A:
                    modulated(a)
                if T:
                    exps(m, 4)
                if C:
                    gate_exp(c)
                if T:
                    exps(m, 5)
                    remote(m)
                    exps(m, 6)
                if K:
                    stack_copy(k, 0)
                    stack_copy(k, 1)
                if T:
                    exps(m, 7)
                if C:
                    mixed_t(c)
                if K:
                    stack_copy(k, 2)
                if A:
                    part1(a)
                if S:
                    lat_pT(t)
                if K:
                    stack_copy(k, 3)

            act.wait_ge(su_dve, SU_MODT)
            act.wait_ge(su_pool, SP_ZERO)
            b0, b1 = (0, 0), (0, 1)
            modulated(b0)
            pick(0)
            pick(1)
            part1(b0)
            modulated(b1)
            pick(2)
            part2(b0)
            pick(3)
            for u in range(4):
                stack_copy(b0, u)
            part1(b1)
            act.wait_ge(su_dve, SU_ALL)
            act.wait_ge(su_pool, SP_ALL)
            run(act, slot)

        @block.tensor
        def _(pe):
            for s, v in started["PE"]:
                pe.sem_inc(s, v)
            pe.wait_ge(su_dve, SU_SILU)
            pe.wait_ge(loaded_m, 16)
            for j in range(2 * KC):
                for k in range(KC):
                    ins = pe.matmul(p_a[:, j * B:(j + 1) * B], wm[:, k, j * P:(j + 1) * P], cs[:, k, :],
                                    start=(k == 0), stop=(k == KC - 1))
            ins.then_inc(su_pe, 1)

            def modulation_rows():
                for j in range(2):
                    for k in range(KC):
                        ins = pe.matmul(p_y[j][0:B, :], cs[:, k, :], wm[:, k, 2 * D + j * 512:2 * D + (j + 1) * 512],
                                        start=(k == 0), stop=(k == KC - 1))
                ins.then_inc(su_pe, 1)

            def ln_t(t):
                pe.wait_ge(xn_ready, done(t))
                pe.wait_ge(lexp_ready, done(back(t, 2)))
                if t[1] < 2 and isinstance(t[0], int):
                    pe.wait_ge(rqT_ready, done(back(t, 2)))
                    pe.wait_ge(lat_copied, done(back(t, 2)))
                    pe.wait_ge(rvb_ready, done(back(t, 2)))
                for k in range(KC):
                    ins = pe.transpose(p_a[:, k * P:(k + 1) * P], xn[:, t[1] % 2, k * P:(k + 1) * P], ident)
                ins.then_inc(hT_psum, 1)

            def project_qk(t):
                pe.wait_ge(hT_ready, done(t))
                pe.wait_ge(rem_ready, done(back(t, 3)))
                if t[1] < 2 and isinstance(t[0], int):
                    pe.wait_ge(v_copied, done(back(t, 1)))
                for k in range(KC):
                    ins = pe.matmul(p_qkv[:, :], hT[:, t[1] % 2, k, :], wqk[:, k, :], start=(k == 0), stop=(k == KC - 1))
                ins.then_inc(qk_psum, 1)

            def project_v(t):
                pe.wait_ge(hT_ready, done(t))
                pe.wait_ge(mrow_ready, done(back(t, 2)))
                if t[1] < 1 and isinstance(t[0], int):
                    pe.wait_ge(qk_copied, done(t))
                for k in range(KC):
                    ins = pe.matmul(p_qkv[:, 0:H * (HD + 1)], hT[:, t[1] % 2, k, :],
                                    wv[:, k, :, :].rearrange("p h k -> p (h k)"), start=(k == 0), stop=(k == KC - 1))
                ins.then_inc(v_psum, 1)

            def project_lat(t):
                pe.wait_ge(pooled_ready, done(t))
                pe.wait_ge(hT_ready, done(back(t, -1)))
                for k in range(KC):
                    pe.matmul(p_a[:, 0:P], wrq[:, k, :], hT[:, t[1] % 2, k, :], start=(k == 0), stop=(k == KC - 1))
                for k in range(KC):
                    pe.matmul(p_a[:, 2 * P:2 * P + LT], wrk[:, k, :], pooled[:, k, 0, :], start=(k == 0), stop=(k == KC - 1))
                for k in range(KC):
                    ins = pe.matmul(p_a[:, 3 * P:3 * P + LD], pooled[:, k, :, :].rearrange("p a l -> p (a l)"),
                                    wrv[:, k, :], start=(k == 0), stop=(k == KC - 1))
                ins.then_inc(lat_psum, 1)

            def stack(t, u):
                pe.wait_ge(part3_ready, done(t))
                if u == 0:
                    pe.wait_ge(s_max[6], done(back(t, 1)))
                elif u == 1:
                    pe.wait_ge(s_max[7], done(back(t, 1)))
                elif u == 2:
                    pe.wait_ge(stack_copied[0], done(t))
                elif u == 3:
                    pe.wait_ge(stack_copied[1], done(t))
                src = (qtok, ktok)[u % 2]
                dst = p_x[u % 2][0:KS, :].bitcast(BF16)
                for j in range(8):
                    ins = pe.transpose(dst[:, j * P:(j + 1) * P], src[:, 8 * (u // 2) + j, :], ident_bf[:, :])
                ins.then_inc(stack_psum[u], 1)

            def scores(t, i):
                if i % 4 == 0:
                    pe.wait_ge(stack_copied[i // 2], done(t))
                    pe.wait_ge(stack_copied[i // 2 + 1], done(t))
                if i == 0:
                    pe.wait_ge(stack_copied[2], done(t))
                elif i == 1:
                    pe.wait_ge(stack_copied[3], done(t))
                else:
                    pe.wait_ge(s_max[i - 2], done(t))
                n = t[1]
                for h in (2 * i, 2 * i + 1):
                    at = (h % 2) * 2 * P
                    q = qst[0:KS, n % RING, h, :]
                    if n % NB:
                        pe.matmul(p_x[i % 2][:, at:at + P], q, kst[0:KS, (n - 1) % RING, h, :], start=True, stop=True)
                    ins = pe.matmul(p_x[i % 2][:, at + P:at + 2 * P], q, kst[0:KS, n % RING, h, :], start=True, stop=True)
                ins.then_inc(s_psum[i], 1)

            def max_t(t):
                pe.wait_ge(m_ready, done(t))
                pe.wait_ge(qk_copied, at_most_last(back(t, -2), 2))
                if isinstance(t[0], int):
                    pe.wait_ge(rem_ready, done(back(t, 1)))
                pe.transpose(p_qkv[:, 0:P // 2].bitcast(BF16), mtok[:, :], ident_bf[:, :]).then_inc(mT_psum, 1)

            def scores_t(t, i):
                pe.wait_ge(shift_ready, done(t))
                pe.wait_ge(exp_done[(i - 2) % NP], done(t if i >= 2 else back(t, 1)))
                n = t[1]
                for h in (2 * i, 2 * i + 1):
                    at = (h % 2) * 2 * P
                    q = qst[0:KS + H, n % RING, h, :]
                    if n % NB:
                        pe.matmul(p_y[i % 2][:, at:at + P], kst[0:KS + H, (n - 1) % RING, h, :], q, start=True, stop=True)
                    ins = pe.matmul(p_y[i % 2][:, at + P:at + 2 * P], kst[0:KS + H, n % RING, h, :], q,
                                    start=True, stop=True)
                ins.then_inc(st_psum[i], 1)

            def sum_v(t, g):
                pe.wait_ge(masked[g], done(t))
                if g == 0:
                    pe.wait_ge(oT_ready, done(back(t, 1)))
                n = t[1]
                for a in range(0 if n % NB else 1, 2):
                    for j in range(4):
                        h = 4 * g + j
                        ins = pe.matmul(p_pv[32 * j:32 * j + VC, g * P:(g + 1) * P], vp[:, (n - 1 + a) % RING, h, :],
                                        pr[:, h, a, :], start=(a == 0 or n % NB == 0), stop=(a == 1),
                                        tile_position=(0, 32 * j))
                ins.then_inc(pv_psum[g], 1)

            def lat_scores(t):
                pe.wait_ge(rqT_ready, done(t))
                pe.wait_ge(lat_copied, done(t))
                pe.wait_ge(lpT_ready, done(back(t, 1)))
                pe.matmul(p_a[:, 0:LH * LT], rqT[:, t[1] % 2, :], bd[:, t[1] % 2, :, :].rearrange("p h l -> p (h l)"),
                          start=True, stop=True).then_inc(ls_psum, 1)

            def lat_p_t(t):
                pe.wait_ge(lp_ready, done(t))
                pe.wait_ge(rqT_ready, done(back(t, -1)))
                pe.wait_ge(lat_copied, done(back(t, -1)))
                pe.wait_ge(rvb_ready, done(back(t, -1)))
                for k in range(2):
                    ins = pe.transpose(p_a[:, k * P:(k + 1) * P], lp[:, k * P:(k + 1) * P], ident)
                ins.then_inc(lpT_psum, 1)

            def lat_out_t(t):
                pe.wait_ge(lpT_ready, done(t))
                pe.wait_ge(bvd_ready, done(t))
                pe.wait_ge(x1_ready, done(back(t, 2)))
                for k in range(2):
                    ins = pe.matmul(p_misc[:, 0:P], bvd[:, t[1] % 2, k, :], lpT[:, k * P:(k + 1) * P],
                                    start=(k == 0), stop=(k == 1))
                ins.then_inc(loT_psum, 1)

            def lat_remote(t):
                pe.wait_ge(loT_ready, done(t))
                pe.wait_ge(v_copied, at_most_last(back(t, -2), 1))
                if isinstance(t[0], int):
                    pe.wait_ge(mrow_ready, done(t))
                pe.matmul(p_qkv[:, 0:D + H], loT[:, :], wro[:, :], start=True, stop=True).then_inc(rem_psum, 1)

            def out_tokens(t):
                pe.wait_ge(oT_ready, done(t))
                pe.wait_ge(loT_ready, at_most_last(back(t, -1)))
                pe.wait_ge(x1_ready, done(back(t, 1)))
                for g in range(4):
                    ins = pe.transpose(p_misc[:, g * P:(g + 1) * P], oT[:, g * P:(g + 1) * P], ident)
                ins.then_inc(o_psum, 1)

            def mixed_t(t):
                pe.wait_ge(mix_ready, done(t))
                pe.wait_ge(zl_ready, done(t))
                pe.wait_ge(local_ready, done(t))
                for k in range(KC):
                    ins = pe.transpose(p_misc[:, k * P:(k + 1) * P], mix[:, k * P:(k + 1) * P], ident)
                ins.then_inc(mixT_psum, 1)

            def project_out(t):
                pe.wait_ge(mixT_ready, done(t))
                pe.wait_ge(mixT_ready, done(t))
                for k in range(KC):
                    ins = pe.matmul(p_misc[:, 0:D], mixT[:, k * P:(k + 1) * P],
                                    wo[:, bass.ds(batch(t) * (KC * D // NB) + k * D, D)],
                                    start=(k == 0), stop=(k == KC - 1))
                ins.then_inc(out_psum, 1)

            def at_most_last(t, ahead=0):
                return done(t) if not isinstance(t[0], int) else min(done(t), done((NT, ahead - 1)))

            def slot(t, stages):
                a, k, m, c = back(t, -2), back(t, -1), back(t, 1), back(t, 2)
                A, K, S, T, C = ("A" in stages, "K" in stages, "S" in stages, "T" in stages, "C" in stages)
                if T:
                    max_t(m)
                if S:
                    scores(t, 0)
                    lat_scores(t)
                if T:
                    lat_out_t(m)
                if S:
                    scores(t, 1)
                if K:
                    project_v(k)
                if T:
                    scores_t(m, 0)
                if S:
                    scores(t, 2)
                if T:
                    scores_t(m, 1)
                if C:
                    out_tokens(c)
                if S:
                    scores(t, 3)
                if T:
                    lat_remote(m)
                    scores_t(m, 2)
                if S:
                    scores(t, 4)
                if T:
                    scores_t(m, 3)
                if S:
                    scores(t, 5)
                if A:
                    ln_t(a)
                if T:
                    sum_v(m, 0)
                if S:
                    scores(t, 6)
                if T:
                    scores_t(m, 4)
                    scores_t(m, 5)
                if S:
                    scores(t, 7)
                if K:
                    project_lat(k)
                if T:
                    scores_t(m, 6)
                if K:
                    stack(k, 0)
                if T:
                    scores_t(m, 7)
                if K:
                    stack(k, 1)
                if A:
                    project_qk(a)
                if C:
                    mixed_t(c)
                if K:
                    stack(k, 2)
                if S:
                    lat_p_t(t)
                if K:
                    stack(k, 3)
                if C:
                    project_out(c)
                if T:
                    sum_v(m, 1)
                    sum_v(m, 2)
                    sum_v(m, 3)

            pe.wait_ge(su_dve, SU_MODT)
            b0, b1 = (0, 0), (0, 1)
            ln_t(b0)
            pe.wait_ge(su_act, SA_QK)
            project_qk(b0)
            pe.wait_ge(loaded_m2, 16)
            modulation_rows()
            pe.wait_ge(su_dve, SU_PRE)
            project_v(b0)
            ln_t(b1)
            project_qk(b1)
            for u in range(4):
                stack(b0, u)
            pe.wait_ge(su_pool, SP_SCALED)
            project_lat(b0)
            pe.wait_ge(su_dve, SU_ALL)
            pe.wait_ge(su_act, SA_ALL)
            run(pe, slot)

        @block.vector
        def _(dve):
            for s, v in started["DVE"]:
                dve.sem_inc(s, v)
            count = [0]

            def setup(*instructions):
                for ins in instructions:
                    ins.then_inc(su_dve, 1)
                count[0] += len(instructions)
                dve.wait_ge(su_dve, count[0])

            dve.wait_ge(su_act, SA_EXP)
            setup(dve.tensor_scalar(cs[:, :, :], cs[:, :, :], 1.0, None, ALU.add))
            setup(dve.reciprocal(cs[:, :, :], cs[:, :, :]))
            setup(dve.tensor_tensor(cs[:, :, :], cs[:, :, :], ct[:, :, :], ALU.mult))
            assert count[0] == SU_SILU
            setup(dve.memset(lpT[:, :], 0.0),
                  dve.memset(x1[:, :, :].rearrange("p a d -> p (a d)"), 0.0),
                  dve.memset(oT[:, :], 0.0),
                  dve.memset(wo[:, 0:KC * D], 0.0),
                  dve.memset(x_all[:, 0:XPAD * D], 0.0),
                  dve.memset(x_all[:, (XPAD + NT) * D:], 0.0),
                  dve.memset(qst[0:KS, 3, :, :].rearrange("p h n -> p (h n)"), 0.0),
                  dve.memset(kst[0:KS, 2:4, :, :].rearrange("p r h n -> p (r h n)"), 0.0))
            dve.wait_ge(loaded_k, 32)
            setup(dve.tensor_copy(ident_bf[:, :], ident))
            dve.wait_ge(su_pe, 1)
            dve.wait_ge(su_pool, SP_LOADED)
            mt = mod_t[:, :].rearrange("p (b j) -> p j b", j=8)
            setup(dve.tensor_scalar(mt[:, 0:KC, 0:B], p_a[:, KC * B:2 * KC * B].rearrange("p (j b) -> p j b", b=B),
                                    1.0, None, ALU.add),
                  dve.tensor_copy(mt[:, KC:2 * KC, 0:B], p_a[:, 0:KC * B].rearrange("p (j b) -> p j b", b=B)))
            assert count[0] == SU_MODT

            def weights():
                dve.wait_ge(su_pool, SP_ZERO)
                glb = row[:, R_GL:R_GL + HD].unsqueeze(1)
                grb = row[:, R_GR:R_GR + HD].unsqueeze(1)
                wv_gl = gt[:, 0:KC * D].rearrange("p (h k) -> p h k", k=HD)
                bv_gl, wro_gr = heads(gt[:, KC * D:KC * D + D]), heads(gt[:, KC * D + D:KC * D + 2 * D])
                w = wv_in.rearrange("p (h k) -> p h k", k=HD)
                wvh = wv[:, :, :, :].rearrange("p k h n -> p (k h) n")
                bvr = heads(row[:, R_V:R_V + D])
                dve.wait_ge(loaded_w, 16 * 9)
                setup(dve.tensor_copy(wvh[:, :, 0:HD], w),
                      dve.tensor_tensor(wv_gl, w, glb.to_broadcast([P, KC * H, HD]), ALU.mult),
                      dve.tensor_copy(bv[:, :, 0:HD], bvr),
                      dve.tensor_tensor(bv_gl, bvr, glb.to_broadcast([P, H, HD]), ALU.mult),
                      dve.tensor_tensor(wro_gr, heads(wro[:, 0:D]), grb.to_broadcast([P, H, HD]), ALU.mult))
                setup(dve.tensor_reduce(wvh[:, :, HD], wv_gl, AX_X, ALU.add),
                      dve.tensor_reduce(bv[:, :, HD], bv_gl, AX_X, ALU.add),
                      dve.tensor_reduce(wro[:, D:D + H], wro_gr, AX_X, ALU.add),
                      dve.memset(vp[:, :, :, HD + 1:VC], 1.0),
                      dve.memset(loT[LD:LD + 1, :], 1.0),
                      dve.tensor_copy(rqT[LD:P, 0, :], cst[LD:P, C_IND:C_IND + P]),
                      dve.tensor_copy(rqT[LD:P, 1, :], cst[LD:P, C_IND:C_IND + P]),
                      dve.tensor_copy(brk[LD:P, :], cst[LD:P, C_BRK:C_BRK + 1]))
                assert count[0] == SU_PRE, count[0]

            def modulation_rows():
                dve.wait_ge(su_pe, 2)
                g_in = [p_y[0][0:B, 0:D], p_y[1][0:B, D:2 * D]]
                g = [mrow6[:, 0, :], mrow6[:, 6, :]]
                g_abs = [mrow6[:, 1, :], mrow6[:, 7, :]]
                g_sign = [mrow6[:, 4, :], mrow6[:, 5, :]]
                setup(*[dve.tensor_scalar(g_sign[j], g_in[j], 0.0, 2.0, ALU.is_ge, ALU.mult) for j in range(2)],
                      *[dve.tensor_scalar(g_abs[j], g_in[j], -1.0, 0.25, ALU.mult, ALU.max) for j in range(2)],
                      dve.tensor_copy(mrow6[:, 2, :], p_y[0][0:B, D:2 * D]),
                      dve.tensor_scalar(mrow6[:, 3, :], p_y[1][0:B, 0:D], 1.0, None, ALU.add))
                setup(*[dve.tensor_tensor(g_abs[j], g_in[j], g_abs[j], ALU.max) for j in range(2)])
                setup(*[dve.scalar_tensor_tensor(out=g[j], in0=g_sign[j], scalar=-1.0, in1=g_abs[j], op0=ALU.add, op1=ALU.mult)
                        for j in range(2)])
                setup(dve.tensor_tensor(mrow6[:, 1, :], row[0:B, R_O:R_O + D], g[0], ALU.mult),
                      dve.tensor_tensor(mrow6[:, 4, :], row[0:B, R_G:R_G + D], g[1], ALU.mult),
                      dve.tensor_tensor(mrow6[:, 5, :], row[0:B, R_B:R_B + D], g[1], ALU.mult))
                assert count[0] == SU_ROWS

            def bn1(t):
                if t[1] == NB:
                    dve.wait_ge(loaded_x, 16)
                dve.bn_stats(st[:, :], x_of(t)).then_inc(st1_ready, 1)

            def bn2(t):
                dve.wait_ge(x1_ready, done(t))
                dve.bn_stats(st2[:, :], x1[:, t[1] % 2, :]).then_inc(st2_ready, 1)

            def bn3(t):
                dve.wait_ge(h2_ready, done(t))
                dve.bn_stats(st3[:, :], h2[:, :]).then_inc(st3_ready, 1)

            def moments(s_stats, st_, mv_, s_mv, t):
                wait_apart(dve, (s_stats, done(t)))
                dve.bn_aggr(mv_[:, :], st_[:, :]).then_inc(s_mv, 1)

            def moments1(t):
                moments(st1_ready, st, mv, mv1_ready, t)

            def moments2(t):
                moments(st2_ready, st2, mv2, mv2_ready, t)

            def moments3(t):
                moments(st3_ready, st3, mv3, mv3_ready, t)

            def add_eps(s_mv, mv_, ve_, s_ve, t):
                dve.wait_ge(s_mv, done(t))
                dve.tensor_scalar(ve_[:, :], mv_[:, 1:2], EPS, None, ALU.add).then_inc(s_ve, 1)

            def add_eps1(t):
                add_eps(mv1_ready, mv, ve1, ve1_ready, t)

            def add_eps2(t):
                add_eps(mv2_ready, mv2, ve2, ve2_ready, t)

            def add_eps3(t):
                add_eps(mv3_ready, mv3, ve3, ve3_ready, t)

            def norm1(t):
                dve.wait_ge(rstd1_ready, done(t))
                dve.wait_ge(hT_psum, done(back(t, 2)))
                dve.tensor_scalar(xn[:, t[1] % 2, :], x_of(t), mv[:, 0:1], rstd[:, :], ALU.subtract, ALU.mult)\
                   .then_inc(xn_ready, 1)

            def pool_tokens(t):
                dve.wait_ge(hT_ready, done(t))
                dve.wait_ge(lat_psum, done(back(t, 1)))
                n = t[1] % NB
                new = slice(n * CPB, (n + 1) * CPB)
                dve.tensor_reduce(pooled[:, :, 0, new], hT[:, t[1] % 2, :, :].rearrange("p k (c s) -> p k c s", s=CH),
                                  AX_X, ALU.add).then_inc(pooled_once, 1)

            def pool_twice(t):
                new = slice(t[1] % NB * CPB, (t[1] % NB + 1) * CPB)
                dve.wait_ge(pooled_once, done(t))
                dve.tensor_copy(pooled[:, :, 1, new], pooled[:, :, 0, new]).then_inc(pooled_ready, 1)

            def copy_qk(t):
                dve.wait_ge(qk_psum, done(t))
                dve.wait_ge(part3_ready, done(back(t, 1)))
                dve.tensor_tensor(qkf[:, :], p_qkv[:, :], row[:, R_QK:R_QK + 2 * D], ALU.add).then_inc(qk_copied, 1)

            def copy_v(t):
                dve.wait_ge(v_psum, done(t))
                dve.wait_ge(pv_psum[NG - 1], done(back(t, 3)))
                dve.tensor_tensor(vp[:, t[1] % RING, :, 0:HD + 1], heads(p_qkv[:, 0:H * (HD + 1)], HD + 1), bv[:, :, :],
                                  ALU.add).then_inc(v_copied, 1)

            def copy_rq(t):
                dve.wait_ge(lat_psum, done(t))
                dve.wait_ge(ls_psum, done(back(t, 2)))
                dve.tensor_scalar(rqT[0:LD, t[1] % 2, :], p_a[0:LD, 0:P], brq[:, :], None, ALU.add).then_inc(rqT_ready, 1)

            def copy_rk(t):
                dve.wait_ge(lat_psum, done(t))
                dve.wait_ge(ls_psum, done(back(t, 2)))
                rk = p_a[:, 2 * P:2 * P + LT].unsqueeze(1).to_broadcast([P, LH, LT])
                at = C_BD + t[1] % NB * LH * LT
                dve.scalar_tensor_tensor(out=bd[:, t[1] % 2, :, :], in0=rk, scalar=brk[:, :],
                                         in1=cst[:, at:at + LH * LT].rearrange("p (h l) -> p h l", h=LH),
                                         op0=ALU.add, op1=ALU.mult).then_inc(lat_copied, 1)

            def copy_rv(t):
                dve.wait_ge(lat_psum, done(t))
                dve.tensor_tensor(rvb[:, :], p_a[:, 3 * P:3 * P + LD], row[:, R_RV:R_RV + LD], ALU.add).then_inc(rvb_ready, 1)

            def spread_rv(t):
                dve.wait_ge(rvb_ready, done(t))
                dve.wait_ge(loT_psum, done(back(t, 2)))
                dve.tensor_tensor(bvd[:, t[1] % 2, :, 0:LD], rvb[:, :].unsqueeze(1).to_broadcast([P, 2, LD]),
                                  cst[:, C_RV:C_RV + 2 * LD].rearrange("p (k l) -> p k l", k=2), ALU.mult).then_inc(bvd_ready, 1)

            def maxima(t, i):
                wait_apart(dve, (s_psum[i], done(t)), (s_max[i - 2], done(t if i >= 2 else back(t, 1))),
                           (m_ready, done(back(t, 1))))
                for h in (2 * i, 2 * i + 1):
                    at = (h % 2) * 2 * P
                    scr = junk[:, h % 4, :]
                    if t[1] % NB:
                        ins = dve.tensor_tensor_reduce(scr, p_x[i % 2][:, at:at + 2 * P], smask, 1.0, -3.0e38,
                                                       ALU.add, ALU.max, mx[:, h:h + 1])
                    else:
                        ins = dve.tensor_tensor_reduce(scr[:, 0:P], p_x[i % 2][:, at + P:at + 2 * P], smask0, 1.0,
                                                       -3.0e38, ALU.add, ALU.max, mx[:, h:h + 1])
                ins.then_inc(s_max[i], 1)

            def negate_max(t):
                dve.wait_ge(s_max[NP - 1], done(t))
                dve.wait_ge(mT_psum, done(back(t, 1)))
                dve.tensor_scalar(mtok[:, KS:KS + H], mx[:, :], -1.0, None, ALU.mult).then_inc(m_ready, 1)

            def copy_shift(t):
                dve.wait_ge(mT_psum, done(t))
                dve.tensor_copy(mrow[KS:KS + H, :], p_qkv[KS:KS + H, 0:P // 2].bitcast(BF16)).then_inc(mrow_ready, 1)

            def shift(t):
                dve.wait_ge(mrow_ready, done(t))
                dve.tensor_copy(qst[KS:KS + H, t[1] % RING, :, :],
                                mrow[KS:KS + H, :].unsqueeze(1).to_broadcast([H, H, P])).then_inc(shift_ready, 1)

            def lat_max(t):
                dve.wait_ge(ls_psum, done(t))
                dve.tensor_reduce(lmx[:, :], p_a[:, 0:LH * LT].rearrange("p (h l) -> p h l", h=LH), AX_X, ALU.max)\
                   .then_inc(lmax_ready, 1)

            def lat_negate(t):
                dve.wait_ge(lmax_ready, done(t))
                dve.wait_ge(lexp_ready, done(back(t, 1)))
                dve.tensor_scalar(lneg[:, :], lmx[:, :], -1.0, None, ALU.mult).then_inc(lmx_ready, 1)

            def lat_recip(t):
                dve.wait_ge(lexp_ready, done(t))
                if t[1] % NB:
                    dve.reciprocal(lrec[:, :], lsum[:, :]).then_inc(lval_ready, 1)
                else:
                    dve.reciprocal(lrec2[:, :], lsum[:, :]).then_inc(lrec_ready, NB)
                    dve.wait_ge(lrec_ready, t[0] + NB)
                    dve.tensor_scalar(lrec[:, :], lrec2[:, :], cst[:, C_VAL:C_VAL + 1], None, ALU.mult).then_inc(lval_ready, 1)

            def lat_norm(t):
                dve.wait_ge(lval_ready, done(t))
                dve.wait_ge(lpT_psum, done(back(t, 1)))
                dve.tensor_tensor(lp[:, :].rearrange("p (h l) -> p h l", h=LH), le[:, :, :], bc(lrec[:, :], LT),
                                  ALU.mult).then_inc(lp_ready, 1)

            def prob_sum(t):
                dve.wait_ge(o_psum, done(t))
                dve.tensor_scalar(ssum[:, :], heads(p_misc[:, :], 32)[:, :, HD + 1], 1e-30, None, ALU.max)\
                   .then_inc(ssum_ready, 1)

            def prob_recip(t):
                dve.wait_ge(ssum_ready, done(t))
                dve.reciprocal(srec[:, :], ssum[:, :]).then_inc(srec_ready, 1)

            def gate_local(t):
                dve.wait_ge(srec_ready, done(t))
                dve.tensor_tensor(zl[:, :], heads(p_misc[:, :], 32)[:, :, HD], srec[:, :], ALU.mult).then_inc(zl_ready, 1)

            def local_out(t):
                dve.wait_ge(srec_ready, done(t))
                dve.wait_ge(dif_ready, done(back(t, 1)))
                dve.tensor_tensor(local[:, :, :], heads(p_misc[:, :], 32)[:, :, 0:HD], bc(srec[:, :], HD), ALU.mult)\
                   .then_inc(local_ready, 1)

            def gate_sum(t):
                dve.wait_ge(zl_ready, done(t))
                dve.wait_ge(rem_ready, done(t))
                dve.wait_ge(ez_ready, done(back(t, 1)))
                dve.tensor_tensor(z[:, :], zl[:, :], rem[:, t[1] % RING, D:D + H], ALU.add).then_inc(z_ready, 1)

            def gate_one(t):
                dve.wait_ge(ez_ready, done(t))
                dve.tensor_scalar(g1[:, :], ez[:, :], 1.0, None, ALU.add).then_inc(g1_ready, 1)

            def gate_recip(t):
                dve.wait_ge(g1_ready, done(t))
                dve.reciprocal(gate[:, :], g1[:, :]).then_inc(gate_ready, 1)

            def gate_dif(t):
                dve.wait_ge(gate_ready, done(t))
                dve.wait_ge(dif_ready, done(t))
                dve.tensor_tensor(heads(dg[:, :]), heads(dif[:, :]), bc(gate[:, :], HD), ALU.mult).then_inc(dg_ready, 1)

            def mix_heads(t):
                dve.wait_ge(dg_ready, done(t))
                dve.wait_ge(mixT_psum, done(back(t, 1)))
                dve.tensor_tensor(mix[:, :], dg[:, :], rem[:, t[1] % RING, 0:D], ALU.add).then_inc(mix_ready, 1)

            def first_residual(t):
                dve.wait_ge(out_psum, done(t))
                dve.wait_ge(xb_ready, done(t))
                dve.wait_ge(ux_ready, done(back(t, 2)))
                dve.tensor_tensor(x1[:, t[1] % 2, :], p_misc[:, 0:D], xb[:, :], ALU.add).then_inc(x1_ready, 1)

            def norm2(t):
                dve.wait_ge(rstd2_ready, done(t))
                dve.wait_ge(h2a_ready, done(back(t, 1)))
                dve.tensor_scalar(h2n[:, :], x1[:, t[1] % 2, :], mv2[:, 0:1], rstd2[:, :], ALU.subtract, ALU.mult)\
                   .then_inc(h2n_ready, 1)

            def norm3(t):
                dve.wait_ge(rstd3_ready, done(t))
                dve.wait_ge(ya_ready, done(back(t, 1)))
                dve.tensor_scalar(h3[:, :], h2[:, :], mv3[:, 0:1], rstd3[:, :], ALU.subtract, ALU.mult)\
                   .then_inc(h3_ready, 1)

            def slot(t, stages):
                a, k, m, c, d = back(t, -2), back(t, -1), back(t, 1), back(t, 2), back(t, 3)
                A, K, S, T, C, D = ("A" in stages, "K" in stages, "S" in stages, "T" in stages, "C" in stages, "D" in stages)
                if A:
                    bn1(a)
                if D:
                    bn2(d)
                if A:
                    moments1(a)
                if K:
                    pool_tokens(k)
                if D:
                    moments2(d)
                if A:
                    add_eps1(a)
                if T:
                    copy_shift(m)
                if S:
                    maxima(t, 0)
                if T:
                    shift(m)
                if D:
                    add_eps2(d)
                if S:
                    lat_max(t)
                    maxima(t, 1)
                if K:
                    copy_v(k)
                if S:
                    lat_negate(t)
                    maxima(t, 2)
                    maxima(t, 3)
                if A:
                    norm1(a)
                if C:
                    prob_sum(c)
                if S:
                    maxima(t, 4)
                if C:
                    prob_recip(c)
                if S:
                    maxima(t, 5)
                if C:
                    gate_local(c)
                if K:
                    pool_twice(k)
                if D:
                    norm2(d)
                if C:
                    local_out(c)
                    gate_sum(c)
                if S:
                    maxima(t, 6)
                    maxima(t, 7)
                if C:
                    gate_one(c)
                if K:
                    copy_rv(k)
                if C:
                    gate_recip(c)
                if K:
                    copy_rk(k)
                if C:
                    gate_dif(c)
                if D:
                    bn3(d)
                if S:
                    lat_recip(t)
                if C:
                    mix_heads(c)
                if K:
                    copy_rq(k)
                if D:
                    moments3(d)
                if S:
                    lat_norm(t)
                    negate_max(t)
                if D:
                    add_eps3(d)
                if A:
                    copy_qk(a)
                if D:
                    norm3(d)
                if K:
                    spread_rv(k)
                if C:
                    first_residual(c)

            dve.wait_ge(loaded_x0, 16)
            b0, b1 = (0, 0), (0, 1)
            bn1(b0)
            moments1(b0)
            add_eps1(b0)
            norm1(b0)
            weights()
            copy_qk(b0)
            bn1(b1)
            moments1(b1)
            add_eps1(b1)
            copy_v(b0)
            norm1(b1)
            pool_tokens(b0)
            pool_twice(b0)
            modulation_rows()
            copy_qk(b1)
            dve.wait_ge(loaded_bd, 16)
            copy_rk(b0)
            copy_rq(b0)
            copy_rv(b0)
            spread_rv(b0)
            dve.wait_ge(loaded_g, 16)
            for b in range(B // 2, B):
                scale_wo(dve, b, su_dve)
                count[0] += 1
            setup(dve.memset(p_pv[:, :], 0.0))
            assert count[0] == SU_ALL, count[0]
            dve.wait_ge(loaded_x1, 16)
            run(dve, slot)


def constants():
    import numpy as np

    c = np.zeros((P, C_END), np.float32)
    i, j = np.arange(P)[:, None], np.arange(P)[None, :]
    c[:, C_ID:C_ID + P] = i == j
    seen_before = (j >= i) & ((i > 0) | (j > 0))
    c[:, C_SM:C_SM + P] = np.where(seen_before, 0, BIG)
    c[:, C_SM + P:C_SM + 2 * P] = np.where(j < i, 0, BIG)
    c[:, C_SM0:C_SM0 + P] = np.where((j < i) | ((i == 0) & (j == 0)), 0, BIG)
    hd = LD // LH
    for n in range(NB):
        t = c[:, C_BD + n * LH * LT:C_BD + (n + 1) * LH * LT].reshape(P, LH, LT)
        for h in range(LH):
            t[h * hd:(h + 1) * hd, h, :] = 1
        for q in range(CPB):
            t[LD + q, :, n * CPB + q:] = BIG
    c[:, C_BD:C_BD + NB * LH * LT] = np.concatenate(
        [c[:, C_BD + n * LH * LT:C_BD + (n + 1) * LH * LT] for n in range(NB)], 1)
    for g in range(2):
        for u in range(2):
            h = 2 * g + u
            c[u * LT:(u + 1) * LT, C_RV + g * LD + h * hd:C_RV + g * LD + (h + 1) * hd] = 1
    for q in range(CPB):
        c[LD + q, C_IND + q * CH:C_IND + (q + 1) * CH] = 1
    for h in range(H):
        c[KS + h, C_SEL + h] = 1
    c[CH:, C_VAL] = 1
    c[LD:LD + CPB, C_BRK] = 1
    return c


def kernel(**inputs):
    import numpy as np
    import concourse.bacc as bacc
    from concourse.bass_utils import run_bass_kernel_spmd

    a = {k: np.ascontiguousarray(v) for k, v in inputs.items()}
    rows = np.concatenate([a["L0_attn_qkv_b"], a["L0_attn_rkv_b"][LD:], a["L0_ffn_ln_g"], a["L0_ffn_ln_b"],
                           a["L0_attn_out_b"], a["L0_attn_gl_w"][:, 0], a["L0_attn_gr_w"][:, 0]])
    arrays = {
        "x": a["L0_attn_x"].reshape(NT, P, D),
        "qkv_w": a["L0_attn_qkv_w"],
        "rq_w": a["L0_attn_rq_w"],
        "rq_b": a["L0_attn_rq_b"].reshape(LD, 1),
        "rkv_w": a["L0_attn_rkv_w"],
        "rk_b": np.ascontiguousarray(a["L0_attn_rkv_b"][:LD].reshape(LD, 1)),
        "rout_w": a["L0_attn_rout_w"],
        "rout_b": a["L0_attn_rout_b"].reshape(1, D),
        "out_w": a["L0_attn_out_w"],
        "c_t": np.ascontiguousarray(a["L0_c"].T.reshape(KC, P, B).transpose(1, 0, 2)),
        "wmod": a["L0_wmod"],
        "rows": rows,
        "consts": constants(),
    }
    nc = bacc.Bacc("TRN2", target_bir_lowering=False, num_devices=1)
    args = [nc.dram_tensor(f"in_{k}", v.shape, mybir.dt.from_np(v.dtype), kind="ExternalInput").ap()
            for k, v in arrays.items()]
    out = nc.dram_tensor("out_y", (NT, P, D), F32, kind="ExternalOutput").ap()
    build(nc, *args, out)
    r = run_bass_kernel_spmd(nc, [{f"in_{k}": v for k, v in arrays.items()}], core_ids=[0])
    return r.results[0]["out_y"].reshape(B, S, D)
```
